# Optimizing a Trainium2 kernel written in Bass

```python
import numpy as np
import jax
import jax.numpy as jnp

def _softmax(x, axis=-1):
    return jax.nn.softmax(x, axis=axis)

def _gelu(x):
    return jax.nn.gelu(x, approximate=True)

def _silu(x):
    return jax.nn.silu(x)

def _sigmoid(x):
    return jax.nn.sigmoid(x)

def _layernorm(x, axis=-1, eps=1e-05):
    m = jnp.mean(x, axis=axis, keepdims=True)
    v = jnp.var(x, axis=axis, keepdims=True)
    return (x - m) / jnp.sqrt(v + eps)

def _scatter_add(tgt, idx, src, axis=0):
    return tgt.at[idx].add(src)

def _segment_sum(src, seg, n):
    return jax.ops.segment_sum(src, seg, n)
kernel_name = 'mk_gnn_resnorm_d4_gnn_r64_04d013'

def setup_inputs(seed: int=0):
    np.random.seed(seed)
    _w = jnp.asarray

    def _rec_inputs():
        import jax
        import jax.numpy as jnp
        _gk = jax.random.key(seed)
        x = -0.000202 + 1 * jax.random.normal(jax.random.fold_in(_gk, 1), (50000, 128), jnp.float32)
        src = jax.random.randint(jax.random.fold_in(_gk, 2), (12500,), 0, 50000, jnp.int32)
        dst = jax.random.randint(jax.random.fold_in(_gk, 3), (12500,), 0, 50000, jnp.int32)
        _o = jnp.argsort(dst, stable=True)
        src = src[_o]
        dst = dst[_o]
        edge_attr_4 = 0.0012443 + 1.0001 * jax.random.normal(jax.random.fold_in(_gk, 12), (12500, 4), jnp.float32)
        edge_attr_8 = 0.000398945 + 1.00003 * jax.random.normal(jax.random.fold_in(_gk, 13), (12500, 8), jnp.float32)
        edge_type_16 = jax.random.randint(jax.random.fold_in(_gk, 15), (12500,), 0, 16, jnp.int32)
        node_vec1 = jax.random.uniform(jax.random.fold_in(_gk, 16), (50000, 1), jnp.float32, 0.0, 1)
        return (x, src, dst, edge_attr_4, edge_attr_8, edge_type_16, node_vec1)
    x, src, dst, edge_attr_4, edge_attr_8, edge_type_16, node_vec1 = _rec_inputs()

    def _L0_gnn_setup():
        import jax, jax.numpy as jnp
        import numpy as np
        N = 50000
        E = 12500
        D = 128
        H = 8
        HD = D // H
        key = jax.random.key(seed)
        ks = jax.random.split(key, 12)
        s = 1.0 / np.sqrt(D)
        x = jax.random.normal(ks[0], (N, D), dtype=jnp.float32)
        edge_index = jax.random.randint(ks[1], (2, E), 0, N, dtype=jnp.int64)
        edge_bias = jax.random.normal(ks[2], (E, H), dtype=jnp.float32)
        Wq = jax.random.uniform(ks[3], (D, D), jnp.float32, -s, s)
        bq = jax.random.uniform(ks[4], (D,), jnp.float32, -s, s)
        Wk = jax.random.uniform(ks[5], (D, D), jnp.float32, -s, s)
        bk = jax.random.uniform(ks[6], (D,), jnp.float32, -s, s)
        Wv = jax.random.uniform(ks[7], (D, D), jnp.float32, -s, s)
        bv = jax.random.uniform(ks[8], (D,), jnp.float32, -s, s)
        Wo = jax.random.uniform(ks[9], (D, D), jnp.float32, -s, s)
        bo = jax.random.uniform(ks[10], (D,), jnp.float32, -s, s)
        return {'x': x, 'edge_index': edge_index, 'edge_bias': edge_bias, 'Wq': Wq, 'bq': bq, 'Wk': Wk, 'bk': bk, 'Wv': Wv, 'bv': bv, 'Wo': Wo, 'bo': bo}
    _L0_gnn_all = _L0_gnn_setup()
    _L0_gnn_in = {k: v for k, v in _L0_gnn_all.items() if k in ('Wq', 'bq', 'Wk', 'bk', 'Wv', 'bv', 'Wo', 'bo')}
    del _L0_gnn_all

    def _L1_gnn_setup():
        import jax, jax.numpy as jnp
        import numpy as np
        N, H = (50000, 128)
        E = 12500
        ETD = 32
        NUM_ET = 16
        LN_EPS = 1e-05
        key = jax.random.key(seed)
        ks = jax.random.split(key, 9)
        x = jax.random.normal(ks[0], (N, H), dtype=jnp.float32)
        edge_index = jax.random.randint(ks[1], (2, E), 0, N, dtype=jnp.int64)
        edge_type = jax.random.randint(ks[2], (E,), 0, NUM_ET, dtype=jnp.int64)
        edge_emb_W = jax.random.normal(ks[3], (NUM_ET, ETD), dtype=jnp.float32)
        lim_msg = 1.0 / np.sqrt(H + ETD)
        msg_W = jax.random.uniform(ks[4], (H, H + ETD), jnp.float32, -lim_msg, lim_msg)
        msg_b = jax.random.uniform(ks[5], (H,), jnp.float32, -lim_msg, lim_msg)
        lim_upd = 1.0 / np.sqrt(H)
        upd_W = jax.random.uniform(ks[6], (H, H), jnp.float32, -lim_upd, lim_upd)
        upd_b = jax.random.uniform(ks[7], (H,), jnp.float32, -lim_upd, lim_upd)
        ln_g = jnp.ones((H,), jnp.float32)
        ln_b = jnp.zeros((H,), jnp.float32)
        return {'x': x, 'edge_index': edge_index, 'edge_type': edge_type, 'edge_emb_W': edge_emb_W, 'msg_W': msg_W, 'msg_b': msg_b, 'upd_W': upd_W, 'upd_b': upd_b, 'ln_g': ln_g, 'ln_b': ln_b}
    _L1_gnn_all = _L1_gnn_setup()
    _L1_gnn_in = {k: v for k, v in _L1_gnn_all.items() if k in ('edge_emb_W', 'msg_W', 'msg_b', 'upd_W', 'upd_b', 'ln_g', 'ln_b')}
    del _L1_gnn_all

    def _L2_gnn_setup():
        import jax, jax.numpy as jnp
        import numpy as np
        N_NODES = 625
        N_EDGES = 10000
        MUL = 32
        NUM_NEIGHBORS = 16.0
        SILU_NORM = 1.6791767923989418
        SQRT3 = 3.0 ** 0.5
        key = jax.random.key(seed)
        ks = jax.random.split(key, 12)
        return {'node_input': jax.random.normal(ks[0], (N_NODES, 4 * MUL), dtype=jnp.float32), 'node_attr': jnp.ones((N_NODES, 1), dtype=jnp.float32), 'edge_src': jax.random.randint(ks[1], (N_EDGES,), 0, N_NODES, dtype=jnp.int32), 'edge_dst': jax.random.randint(ks[2], (N_EDGES,), 0, N_NODES, dtype=jnp.int32), 'edge_attr': jax.random.normal(ks[3], (N_EDGES, 4), dtype=jnp.float32), 'edge_scalars': jax.random.normal(ks[4], (N_EDGES, 8), dtype=jnp.float32), 'w_lin1_s': jax.random.normal(ks[5], (MUL, MUL), dtype=jnp.float32), 'w_lin1_v': jax.random.normal(ks[6], (MUL, MUL), dtype=jnp.float32), 'fc_w1': jax.random.normal(ks[7], (8, 64), dtype=jnp.float32), 'fc_w2': jax.random.normal(ks[8], (64, 4 * MUL), dtype=jnp.float32), 'w_lin2_s': jax.random.normal(ks[9], (2 * MUL, MUL), dtype=jnp.float32), 'w_lin2_v': jax.random.normal(ks[10], (2 * MUL, MUL), dtype=jnp.float32)}
    _L2_gnn_all = _L2_gnn_setup()
    _L2_gnn_in = {k: v for k, v in _L2_gnn_all.items() if k in ('w_lin1_s', 'w_lin1_v', 'fc_w1', 'fc_w2', 'w_lin2_s', 'w_lin2_v')}
    del _L2_gnn_all

    def _L3_gnn_setup():
        import jax, jax.numpy as jnp
        import numpy as np
        N_NODES, N_EDGES, N_INC = (50000, 10000, 12500)
        IN_C, HID_C, OUT_C = (128, 128, 128)
        EPS = 1e-05

        def _hconv(x, W, b, node_idx, edge_idx, hw):
            x = x @ W.T
            D = jax.ops.segment_sum(hw[edge_idx], node_idx, num_segments=N_NODES)
            Dinv = jnp.where(D > 0, 1.0 / D, 0.0)
            Bdeg = jax.ops.segment_sum(jnp.ones_like(edge_idx, dtype=x.dtype), edge_idx, num_segments=N_EDGES)
            Binv = jnp.where(Bdeg > 0, 1.0 / Bdeg, 0.0)
            e = jax.ops.segment_sum(Binv[edge_idx][:, None] * x[node_idx], edge_idx, num_segments=N_EDGES)
            out = jax.ops.segment_sum(Dinv[node_idx][:, None] * e[edge_idx], node_idx, num_segments=N_NODES)
            return out + b
        key = jax.random.key(seed)
        ks = jax.random.split(key, 6)
        x = jax.random.normal(ks[0], (N_NODES, IN_C), jnp.float32)
        node_idx = jax.random.randint(ks[1], (N_INC,), 0, N_NODES)
        edge_idx = jax.random.randint(ks[2], (N_INC,), 0, N_EDGES)
        hyperedge_index = jnp.stack([node_idx, edge_idx])
        hyperedge_weight = jnp.ones((N_EDGES,), jnp.float32)
        s1 = 1.0 / np.sqrt(IN_C)
        s2 = 1.0 / np.sqrt(HID_C)
        W1 = jax.random.uniform(ks[3], (HID_C, IN_C), jnp.float32, -s1, s1)
        b1 = jnp.zeros((HID_C,), jnp.float32)
        gamma = jnp.ones((HID_C,), jnp.float32)
        beta = jnp.zeros((HID_C,), jnp.float32)
        W2 = jax.random.uniform(ks[4], (OUT_C, HID_C), jnp.float32, -s2, s2)
        b2 = jnp.zeros((OUT_C,), jnp.float32)
        return dict(x=x, hyperedge_index=hyperedge_index, hyperedge_weight=hyperedge_weight, W1=W1, b1=b1, gamma=gamma, beta=beta, W2=W2, b2=b2)
    _L3_gnn_all = _L3_gnn_setup()
    _L3_gnn_in = {k: v for k, v in _L3_gnn_all.items() if k in ('hyperedge_weight', 'W1', 'b1', 'gamma', 'beta', 'W2', 'b2')}
    del _L3_gnn_all
    return {'x': x, 'src': src, 'dst': dst, 'edge_attr_4': edge_attr_4, 'edge_attr_8': edge_attr_8, 'edge_type_16': edge_type_16, 'node_vec1': node_vec1, 'L0_gnn_Wq': _L0_gnn_in['Wq'], 'L0_gnn_bq': _L0_gnn_in['bq'], 'L0_gnn_Wk': _L0_gnn_in['Wk'], 'L0_gnn_bk': _L0_gnn_in['bk'], 'L0_gnn_Wv': _L0_gnn_in['Wv'], 'L0_gnn_bv': _L0_gnn_in['bv'], 'L0_gnn_Wo': _L0_gnn_in['Wo'], 'L0_gnn_bo': _L0_gnn_in['bo'], 'L1_gnn_edge_emb_W': _L1_gnn_in['edge_emb_W'], 'L1_gnn_msg_W': _L1_gnn_in['msg_W'], 'L1_gnn_msg_b': _L1_gnn_in['msg_b'], 'L1_gnn_upd_W': _L1_gnn_in['upd_W'], 'L1_gnn_upd_b': _L1_gnn_in['upd_b'], 'L1_gnn_ln_g': _L1_gnn_in['ln_g'], 'L1_gnn_ln_b': _L1_gnn_in['ln_b'], 'L2_gnn_w_lin1_s': _L2_gnn_in['w_lin1_s'], 'L2_gnn_w_lin1_v': _L2_gnn_in['w_lin1_v'], 'L2_gnn_fc_w1': _L2_gnn_in['fc_w1'], 'L2_gnn_fc_w2': _L2_gnn_in['fc_w2'], 'L2_gnn_w_lin2_s': _L2_gnn_in['w_lin2_s'], 'L2_gnn_w_lin2_v': _L2_gnn_in['w_lin2_v'], 'L3_gnn_hyperedge_weight': _L3_gnn_in['hyperedge_weight'], 'L3_gnn_W1': _L3_gnn_in['W1'], 'L3_gnn_b1': _L3_gnn_in['b1'], 'L3_gnn_gamma': _L3_gnn_in['gamma'], 'L3_gnn_beta': _L3_gnn_in['beta'], 'L3_gnn_W2': _L3_gnn_in['W2'], 'L3_gnn_b2': _L3_gnn_in['b2']}

def reference(x, src, dst, edge_attr_4, edge_attr_8, edge_type_16, node_vec1, L0_gnn_Wq, L0_gnn_bq, L0_gnn_Wk, L0_gnn_bk, L0_gnn_Wv, L0_gnn_bv, L0_gnn_Wo, L0_gnn_bo, L1_gnn_edge_emb_W, L1_gnn_msg_W, L1_gnn_msg_b, L1_gnn_upd_W, L1_gnn_upd_b, L1_gnn_ln_g, L1_gnn_ln_b, L2_gnn_w_lin1_s, L2_gnn_w_lin1_v, L2_gnn_fc_w1, L2_gnn_fc_w2, L2_gnn_w_lin2_s, L2_gnn_w_lin2_v, L3_gnn_hyperedge_weight, L3_gnn_W1, L3_gnn_b1, L3_gnn_gamma, L3_gnn_beta, L3_gnn_W2, L3_gnn_b2):
    import jax
    import jax.numpy as jnp

    def _L0_gnn_ref(x, edge_index, edge_bias, Wq, bq, Wk, bk, Wv, bv, Wo, bo):
        import jax, jax.numpy as jnp
        import numpy as np
        N = 50000
        E = 12500
        D = 128
        H = 8
        HD = D // H
        scale = HD ** (-0.5)
        row, col = (edge_index[0], edge_index[1])
        q = (x @ Wq + bq).reshape(N, H, HD)
        k = (x @ Wk + bk).reshape(N, H, HD)
        v = (x @ Wv + bv).reshape(N, H, HD)
        q_i = q[col]
        k_j = k[row]
        v_j = v[row]
        attn = jnp.einsum('ehd,ehd->eh', q_i, k_j) * scale + edge_bias
        seg_max = jax.ops.segment_max(attn, col, num_segments=N)
        seg_max = jnp.where(jnp.isfinite(seg_max), seg_max, 0.0)
        ex = jnp.exp(attn - seg_max[col])
        denom = jax.ops.segment_sum(ex, col, num_segments=N)
        attn = ex / (denom[col] + 1e-16)
        weighted_v = attn[:, :, None] * v_j
        out = jax.ops.segment_sum(weighted_v, col, num_segments=N)
        out = out.reshape(N, D)
        return out @ Wo + bo

    def _L1_gnn_ref(x, edge_index, edge_type, edge_emb_W, msg_W, msg_b, upd_W, upd_b, ln_g, ln_b):
        import jax, jax.numpy as jnp
        import numpy as np
        N, H = (50000, 128)
        E = 12500
        ETD = 32
        NUM_ET = 16
        LN_EPS = 1e-05
        src = edge_index[0]
        dst = edge_index[1]
        et = edge_emb_W[edge_type]
        m_in = jnp.concatenate([x[src], et], axis=-1)
        m = jax.nn.relu(m_in @ msg_W.T + msg_b)
        agg = jax.ops.segment_sum(m, dst, num_segments=x.shape[0])
        deg = jax.ops.segment_sum(jnp.ones_like(dst, dtype=x.dtype), dst, num_segments=x.shape[0])
        agg = agg / jnp.clip(deg, 1.0)[:, None]
        out = agg @ upd_W.T + upd_b
        h = x + out
        mu = jnp.mean(h, axis=-1, keepdims=True)
        var = jnp.mean((h - mu) ** 2, axis=-1, keepdims=True)
        return (h - mu) * jax.lax.rsqrt(var + LN_EPS) * ln_g + ln_b

    def _L2_gnn_ref(node_input, node_attr, edge_src, edge_dst, edge_attr, edge_scalars, w_lin1_s, w_lin1_v, fc_w1, fc_w2, w_lin2_s, w_lin2_v):
        import jax, jax.numpy as jnp
        import numpy as np
        N_NODES = 625
        N_EDGES = 10000
        MUL = 32
        NUM_NEIGHBORS = 16.0
        SILU_NORM = 1.6791767923989418
        SQRT3 = 3.0 ** 0.5
        N = node_input.shape[0]
        s = node_input[:, :MUL]
        v = node_input[:, MUL:].reshape(N, MUL, 3)
        s = s @ (w_lin1_s / jnp.sqrt(jnp.float32(MUL)))
        v = jnp.einsum('nui,uw->nwi', v, w_lin1_v / jnp.sqrt(jnp.float32(MUL)))
        h = jax.nn.silu(edge_scalars @ (fc_w1 / jnp.sqrt(jnp.float32(fc_w1.shape[0])))) * SILU_NORM
        w = h @ (fc_w2 / jnp.sqrt(jnp.float32(fc_w2.shape[0])))
        w0 = w[:, 0 * MUL:1 * MUL]
        w1 = w[:, 1 * MUL:2 * MUL]
        w2 = w[:, 2 * MUL:3 * MUL]
        w3 = w[:, 3 * MUL:4 * MUL]
        se = s[edge_src]
        ve = v[edge_src]
        es = edge_attr[:, :1]
        ev = edge_attr[:, 1:4]
        mid_s0 = w0 * se * es
        mid_s1 = w3 * jnp.einsum('eui,ei->eu', ve, ev) / SQRT3
        mid_v0 = (w1 * se)[:, :, None] * ev[:, None, :]
        mid_v1 = (w2 * es)[:, :, None] * ve
        mid_scal = jnp.concatenate([mid_s0, mid_s1], axis=1)
        mid_vec = jnp.concatenate([mid_v0, mid_v1], axis=1)
        inv = 1.0 / jnp.sqrt(jnp.float32(NUM_NEIGHBORS))
        ns = jax.ops.segment_sum(mid_scal, edge_dst, num_segments=N) * inv
        nv = jax.ops.segment_sum(mid_vec, edge_dst, num_segments=N) * inv
        fan = jnp.sqrt(jnp.float32(2 * MUL))
        out_s = ns @ (w_lin2_s / fan)
        out_v = jnp.einsum('nui,uw->nwi', nv, w_lin2_v / fan)
        return jnp.concatenate([out_s, out_v.reshape(N, -1)], axis=1)

    def _L3_gnn_ref(x, hyperedge_index, hyperedge_weight, W1, b1, gamma, beta, W2, b2):
        import jax, jax.numpy as jnp
        import numpy as np
        N_NODES, N_EDGES, N_INC = (50000, 10000, 12500)
        IN_C, HID_C, OUT_C = (128, 128, 128)
        EPS = 1e-05

        def _hconv(x, W, b, node_idx, edge_idx, hw):
            x = x @ W.T
            D = jax.ops.segment_sum(hw[edge_idx], node_idx, num_segments=N_NODES)
            Dinv = jnp.where(D > 0, 1.0 / D, 0.0)
            Bdeg = jax.ops.segment_sum(jnp.ones_like(edge_idx, dtype=x.dtype), edge_idx, num_segments=N_EDGES)
            Binv = jnp.where(Bdeg > 0, 1.0 / Bdeg, 0.0)
            e = jax.ops.segment_sum(Binv[edge_idx][:, None] * x[node_idx], edge_idx, num_segments=N_EDGES)
            out = jax.ops.segment_sum(Dinv[node_idx][:, None] * e[edge_idx], node_idx, num_segments=N_NODES)
            return out + b
        node_idx, edge_idx = (hyperedge_index[0], hyperedge_index[1])
        h = _hconv(x, W1, b1, node_idx, edge_idx, hyperedge_weight)
        mu = h.mean(axis=0)
        var = h.var(axis=0)
        h = gamma * (h - mu) * jax.lax.rsqrt(var + EPS) + beta
        return _hconv(h, W2, b2, node_idx, edge_idx, hyperedge_weight)
    edge_index = jnp.stack([src, dst])
    x = _layernorm(x + _L0_gnn_ref(x, edge_index, edge_attr_8, L0_gnn_Wq, L0_gnn_bq, L0_gnn_Wk, L0_gnn_bk, L0_gnn_Wv, L0_gnn_bv, L0_gnn_Wo, L0_gnn_bo), axis=-1)
    x = _layernorm(x + _L1_gnn_ref(x, edge_index, edge_type_16, L1_gnn_edge_emb_W, L1_gnn_msg_W, L1_gnn_msg_b, L1_gnn_upd_W, L1_gnn_upd_b, L1_gnn_ln_g, L1_gnn_ln_b), axis=-1)
    x = _layernorm(x + _L2_gnn_ref(x, node_vec1, src, dst, edge_attr_4, edge_attr_8, L2_gnn_w_lin1_s, L2_gnn_w_lin1_v, L2_gnn_fc_w1, L2_gnn_fc_w2, L2_gnn_w_lin2_s, L2_gnn_w_lin2_v), axis=-1)
    x = _layernorm(x + _L3_gnn_ref(x, edge_index, L3_gnn_hyperedge_weight, L3_gnn_W1, L3_gnn_b1, L3_gnn_gamma, L3_gnn_beta, L3_gnn_W2, L3_gnn_b2), axis=-1)
    return x

_drawn_inputs = setup_inputs


def setup_inputs(seed=0):
    import zlib

    import numpy as np

    out = dict(_drawn_inputs(seed))
    spreads = {'L1_gnn_ln_g': (1.0, 0.2),
     'L1_gnn_ln_b': (0.0, 0.1),
     'L3_gnn_hyperedge_weight': (1.0, 0.562),
     'L3_gnn_b1': (0.0, 2.0),
     'L3_gnn_gamma': (1.0, 0.2),
     'L3_gnn_beta': (0.0, 0.8),
     'L3_gnn_b2': (0.0, 0.1)}
    factors = {'L0_gnn_Wq': 8.0,
     'L0_gnn_bq': 63.533,
     'L0_gnn_Wk': 8.0,
     'L0_gnn_bk': 64.0,
     'L0_gnn_bv': 3.81,
     'L1_gnn_msg_b': 8.0}
    for name, (base, spread) in spreads.items():
        noise = np.random.default_rng([zlib.crc32(name.encode()), seed]).standard_normal(out[name].shape)
        drawn = base * np.exp(spread * noise) if base else spread * noise
        out[name] = jnp.asarray(drawn.astype(out[name].dtype))
    for name, factor in factors.items():
        out[name] = (out[name] * factor).astype(out[name].dtype)
    return out
```

```python
from contextlib import ExitStack

import numpy as np
import concourse.bass as bass
from concourse import mybir

F32 = mybir.dt.float32
BF16 = mybir.dt.bfloat16
I32 = mybir.dt.int32
ALU = mybir.AluOpType
ACT = mybir.ActivationFunctionType
AX = mybir.AxisListType.X

N, D, E = 50000, 128, 12500
NH = 10000
TP = 125
NT = E // TP
CT = 4
CE = CT * TP
NC = E // CE
EPS = 1e-5
LO = (N + 127) // 128
FAR = 1 << 20
NEG = 1.0e30
SILU = 1.6791767923989418


class Chain:

    def __init__(self, eng, sem, i=0, per=0):
        self.eng, self.sem, self.base, self.per, self.n = eng, sem, i * per, per, 0

    def __call__(self, ins):
        self.n += 1
        ins.then_inc(self.sem, 1)
        self.eng.wait_ge(self.sem, self.base + self.n)

    def done(self):
        assert self.n == self.per, (self.n, self.per)


def steps(eng, n):
    def run(body):
        body(0)
        if n > 1:
            with eng.Fori(1, n) as i:
                body(i)
    return run


class Place:

    def __init__(self, nc, ctx, tag):
        self.nc, self.ctx, self.tag, self.sems = nc, ctx, tag, []
        ctx.callback(self.clear)

    def sb(self, name, shape, dt=F32):
        return self.ctx.enter_context(self.nc.sbuf_tensor(f"{self.tag}_{name}", shape, dt))

    def ps(self, name, shape, dt=F32):
        return self.ctx.enter_context(self.nc.psum_tensor(f"{self.tag}_{name}", shape, dt))

    def sem(self, name):
        self.sems.append(self.nc.alloc_semaphore(f"{self.tag}_{name}"))
        return self.sems[-1]

    def clear(self):
        self.nc.clear_and_free_semaphores(self.sems)
        self.nc.all_engine_barrier()


def constants(nc, ctx):
    def sb(name, shape, dt=F32):
        return ctx.enter_context(nc.sbuf_tensor(f"k_{name}", shape, dt))

    K = {n: sb(n, s) for n, s in (("ident", [128, 128]), ("heads", [128, 128]), ("expand", [8, 128]), ("isH", [TP, NT]), ("rdeg", [TP, NT]), ("rdegH", [TP, NT]))}
    K["identb"] = sb("identb", [128, 128], BF16)
    K["iota_i"] = sb("iota_i", [128, LO], I32)
    K["junk"] = sb("junk", [128, 512])
    K["cols"] = sb("cols", [D, 9])
    for n in ("dst_end", "send", "idxS", "s_idxE", "s_idxS", "src_end"):
        K[n] = sb(n, [TP, NT], I32)
    return K


def rows_of(table, first, n):
    return table[bass.ds(first, n * TP), :].rearrange("(t p) f -> p t f", p=TP)


def index_phase(nc, g, K, T):
    with ExitStack() as ctx:
        a = Place(nc, ctx, "ix")
        src, dst, dstn = (a.sb(n, [TP, NT], I32) for n in ("src", "dst", "dstn"))
        srcf, dstf, dstnf, hif, lof, ef, tmp, endf = (
            a.sb(n, [TP, NT]) for n in ("srcf", "dstf", "dstnf", "hif", "lof", "ef", "tmp", "endf"))
        hii, loi, ei, clipi, scatI = (a.sb(n, [TP, NT], I32) for n in ("hii", "loi", "ei", "clipi", "scatI"))
        iot = a.sb("iot", [TP, LO])
        tri, triL = a.sb("tri", [128, 128]), a.sb("triL", [TP, TP])
        ohi, olo = a.sb("ohi", [TP, 2, 128], BF16), a.sb("olo", [TP, 2, LO], BF16)
        zero = a.sb("zero", [TP, LO], BF16)
        hiT = a.sb("hiT", [128, 2, TP])
        cnt, inc, cur, end = a.sb("cnt", [128, LO]), a.sb("inc", [128, LO]), a.sb("cur", [128, 2, LO]), a.sb("end", [128, LO])
        ones = a.sb("ones", [128, LO])
        offs = a.sb("offs", [128, 1])
        junk = a.sb("junk", [TP, 3, LO])
        srcb, srcbf = a.sb("srcb", [TP, 2, TP], I32), a.sb("srcbf", [TP, 2, TP])
        hit = a.sb("hit", [TP, 2, 3])
        slotf, sendf = a.sb("slotf", [TP, NT]), a.sb("sendf", [TP, NT])
        slotI = a.sb("slotI", [TP, NT], I32)
        ri, re = a.sb("ri", [TP, CT], I32), a.sb("re", [TP, CT])
        rj = a.sb("rj", [TP, CT], I32)
        pg, pq = a.sb("pg", [TP, CT, 2]), a.sb("pq", [TP, CT, 2])
        posE, hwE, posS = a.sb("posE", [TP, NT]), a.sb("hwE", [TP, NT]), a.sb("posS", [TP, NT])
        idxSf = a.sb("idxSf", [TP, NT])
        pay = a.sb("pay", [TP, NT, 4])
        rp = a.sb("rp", [TP, CT, 4])
        s4 = a.sb("s4", [TP, NT, 4])
        rowS, rowN, rowI = a.sb("rowS", [NT, TP]), a.sb("rowN", [NT, TP]), a.sb("rowI", [NT, TP])
        rowE = a.sb("rowE", [NT, TP])
        rowH = a.sb("rowH", [NT, TP])
        cap = a.sb("cap", [1, 1])

        pH, pL, pE = a.ps("pH", [128, 512]), a.ps("pL", [128, 2, 512]), a.ps("pE", [128, 512])
        pT = a.ps("pT", [128, 2, 1024], BF16)
        pR = a.ps("pR", [128, 512])

        s_in, s_tab, s_cst, s_dv, s_pl = (a.sem(n) for n in ("in", "tab", "cst", "dvchain", "plchain"))
        s_ends_idx, s_scat, s_gat, s_gat2, s_gcp = (a.sem(n) for n in ("ends_idx", "scat", "gat", "gat2", "gat_copied"))
        s_ring = a.sem("ring")
        s_ohA, s_hist, s_hist_all = a.sem("ohA"), a.sem("hist"), a.sem("hist_all")
        s_tot, s_off = a.sem("tot"), a.sem("off")
        s_cur, s_ohB, s_tr, s_hiT, s_look, s_used = (a.sem(n) for n in ("cur", "ohB", "transposed", "hiT", "looked", "lookup_used"))
        s_srcb = [a.sem(f"srcb{k}") for k in range(2)]
        s_slot, s_pay, s_s4, s_rowT, s_row, s_rowst, s_rown, s_rowi, s_colT, s_done = (
            a.sem(n) for n in ("slot", "pay", "s4", "rowT", "row", "row_stored", "row_next", "row_idx", "colT", "done"))
        s_dv2 = a.sem("srcb_f32")
        s_go = a.sem("go")
        block = ctx.enter_context(nc.Block())

        @block.sync
        def _(sp):
            for t, d in ((src, g["src_col"]), (dst, g["dst_col"]), (dstn, g["dstn_col"])):
                sp.dma_start(t[:], d).then_inc(s_in, 16)
            sp.dma_start(tri[:], g["tri"]).then_inc(s_in, 16)
            sp.dma_start(triL[:], g["tri"][0:TP, 0:TP].rearrange("a b -> a b")).then_inc(s_in, 16)
            for name in ("ident", "identb", "heads", "expand", "cols"):
                sp.dma_start(K[name][:], g[name]).then_inc(s_in, 16)
            sp.dma_start(T["ptab"].rearrange("(a b) c -> a (b c)", a=16), g["ptab0"].rearrange("(a b) c -> a (b c)", a=16)).then_inc(s_tab, 16)
            for k in range(2):
                sp.dma_start(srcb[:, k, :], g["src_row"][:, k * TP:(k + 1) * TP].broadcast_to([TP, TP])).then_inc(s_srcb[k], 16)
            with sp.Fori(1, NT // 2) as i:
                for k in range(2):
                    sp.wait_ge(s_slot, 2 * i + k - 1)
                    sp.dma_start(srcb[:, k, :], g["src_row"][:, bass.ds((2 * i + k) * TP, TP)].broadcast_to([TP, TP])).then_inc(s_srcb[k], 16)
            sp.wait_ge(s_pay, 16 * NT)
            sp.dma_start(s4[:], T["S4"].rearrange("(t p) c -> p t c", p=TP)).then_inc(s_s4, 16)
            sp.wait_ge(s_row, 1)
            sp.dma_start(T["srow"][:, 1:E + 1].rearrange("a (t p) -> (a t) p", p=TP), rowS[:]).then_inc(s_rowst, 16)
            sp.dma_start(T["hrow"].rearrange("a (t p) -> (a t) p", p=TP), rowH[:]).then_inc(s_rowst, 16)
            sp.dma_start(T["srow"][:, 0:1], cap[:]).then_inc(s_rowst, 16)
            sp.dma_start(T["srow"][:, E + 1:E + 2], cap[:]).then_inc(s_rowst, 16)
            sp.wait_ge(s_rowst, 64)
            sp.dma_start(rowN[:], T["srow"][:, 2:E + 2].rearrange("a (t p) -> (a t) p", p=TP)).then_inc(s_rown, 16)
            sp.wait_ge(s_rown, 16)

        @block.gpsimd
        def _(pool):
            plink = Chain(pool, s_pl)
            nc.gpsimd.iota(ei[:], pattern=[[TP, NT]], base=0, channel_multiplier=1)
            plink(nc.gpsimd.iota(K["iota_i"][:], pattern=[[1, LO]], base=0, channel_multiplier=0))
            nc.gpsimd.tensor_copy(iot[:], K["iota_i"][0:TP, :])
            nc.gpsimd.tensor_copy(ef[:], ei[:])
            nc.gpsimd.memset(ones[:], 1.0)
            nc.gpsimd.memset(cap[:], -1.0)
            nc.gpsimd.memset(zero[:], 0.0).then_inc(s_cst, 1)
            pool.wait_ge(s_cst, 1)
            pool.wait_ge(s_tab, 16)
            pool.wait_ge(s_ends_idx, 1)
            @steps(pool, NC)
            def _(c):
                pool.wait_ge(s_scat, 64 * c)
                pool.sem_inc(s_go, 1)
                nc.gpsimd.tensor_copy(re[:], ef[:, bass.ds(CT * c, CT)])
                nc.gpsimd.tensor_copy(ri[:], scatI[:, bass.ds(CT * c, CT)]).then_inc(s_ring, 1)
                pool.wait_ge(s_ring, c + 1)
                pool.sem_inc(s_go, 1)
                for k in range(CT):
                    nc.gpsimd.indirect_dma_start(
                        out=T["ptab1"], out_offset=bass.IndirectOffsetOnAxis(ap=ri[:, k:k + 1], axis=0),
                        in_=re[:, k:k + 1], in_offset=None, bounds_check=2 * N - 1, oob_is_err=False).then_inc(s_scat, 16)
            pool.wait_ge(s_scat, 16 * NT)
            @steps(pool, NC)
            def _(c):
                pool.wait_ge(s_gcp, c)
                pool.sem_inc(s_go, 1)
                nc.gpsimd.tensor_copy(rj[:], clipi[:, bass.ds(CT * c, CT)])
                nc.gpsimd.tensor_copy(ri[:], src[:, bass.ds(CT * c, CT)]).then_inc(s_ring, 1)
                pool.wait_ge(s_ring, NC + c + 1)
                pool.sem_inc(s_go, 1)
                for k in range(CT):
                    nc.gpsimd.indirect_dma_start(out=pg[:, k, :], out_offset=None, in_=T["ptab"],
                                                 in_offset=bass.IndirectOffsetOnAxis(ap=rj[:, k:k + 1], axis=0)).then_inc(s_gat, 16)
                    nc.gpsimd.indirect_dma_start(out=pq[:, k, :], out_offset=None, in_=T["ptab"],
                                                 in_offset=bass.IndirectOffsetOnAxis(ap=ri[:, k:k + 1], axis=0)).then_inc(s_gat2, 16)
                pool.wait_ge(s_gat, 64 * (c + 1))
                pool.sem_inc(s_go, 1)
                nc.gpsimd.tensor_copy(posE[:, bass.ds(CT * c, CT)], pg[:, :, 0])
                nc.gpsimd.tensor_copy(hwE[:, bass.ds(CT * c, CT)], pg[:, :, 1])
                pool.wait_ge(s_gat2, 64 * (c + 1))
                pool.sem_inc(s_go, 1)
                nc.gpsimd.tensor_copy(posS[:, bass.ds(CT * c, CT)], pq[:, :, 0]).then_inc(s_gcp, 1)
            pool.wait_ge(s_done, 1)
            @steps(pool, NC)
            def _(c):
                pool.wait_ge(s_pay, 64 * c)
                pool.sem_inc(s_go, 1)
                nc.gpsimd.tensor_copy(rp[:], pay[:, bass.ds(CT * c, CT), :])
                nc.gpsimd.tensor_copy(ri[:], slotI[:, bass.ds(CT * c, CT)]).then_inc(s_ring, 1)
                pool.wait_ge(s_ring, 2 * NC + c + 1)
                pool.sem_inc(s_go, 1)
                for k in range(CT):
                    nc.gpsimd.indirect_dma_start(out=T["S4"], out_offset=bass.IndirectOffsetOnAxis(ap=ri[:, k:k + 1], axis=0),
                                                 in_=rp[:, k, :], in_offset=None).then_inc(s_pay, 16)
            pool.wait_ge(s_pay, 16 * NT)

        @block.vector
        def _(dve):
            link = Chain(dve, s_dv)
            dve.wait_ge(s_in, 16 * 10)
            nc.vector.tensor_copy(srcf[:], src[:])
            nc.vector.tensor_copy(dstf[:], dst[:])
            nc.vector.tensor_copy(dstnf[:], dstn[:])
            nc.vector.tensor_scalar(hii[:], src[:], 127, None, ALU.bitwise_and)
            link(nc.vector.tensor_scalar(loi[:], src[:], 7, None, ALU.logical_shift_right))
            nc.vector.tensor_copy(hif[:], hii[:])
            nc.vector.tensor_copy(lof[:], loi[:])
            nc.vector.tensor_scalar(clipi[:], dstf[:], float(NH - 1), None, ALU.min)
            nc.vector.tensor_scalar(K["isH"][:], dstf[:], float(NH), None, ALU.is_lt)
            link(nc.vector.tensor_tensor(endf[:], dstf[:], dstnf[:], ALU.is_equal))
            nc.vector.tensor_scalar(endf[:], endf[:], float(FAR), None, ALU.mult)
            link(nc.vector.tensor_scalar(tmp[:], dstf[:], 2.0, None, ALU.mult))
            nc.vector.tensor_tensor(K["dst_end"][:], endf[:], dstf[:], ALU.add)
            nc.vector.tensor_tensor(scatI[:], endf[:], tmp[:], ALU.add).then_inc(s_ends_idx, 1)
            dve.wait_ge(s_cst, 1)
            @steps(dve, NT // 2)
            def _(i):
                for k in range(2):
                    dve.wait_ge(s_hist, 2 * i + k)
                    nc.vector.tensor_scalar(ohi[:, k, :], iot[:, 0:128], hif[:, bass.ds(2 * i + k, 1)], None, ALU.is_equal)
                    nc.vector.tensor_scalar(olo[:, k, :], iot[:], lof[:, bass.ds(2 * i + k, 1)], None, ALU.is_equal).then_inc(s_ohA, 1)
            dve.wait_ge(s_hist_all, 1)
            link(nc.vector.tensor_copy(cnt[:], pH[:, 0:LO]))
            nc.vector.tensor_tensor_scan(inc[:], ones[:], cnt[:], 0.0, ALU.mult, ALU.add).then_inc(s_tot, 1)
            dve.wait_ge(s_off, 1)
            link(nc.vector.tensor_copy(offs[:], pR[:, 0:1]))
            nc.vector.tensor_scalar(end[:], inc[:], offs[:], -1.0, ALU.add, ALU.add)
            link(nc.vector.tensor_scalar(junk2 := K["junk"][:, 0:LO], inc[:], offs[:], None, ALU.add))
            nc.vector.tensor_tensor(cur[:, 0, :], junk2, cnt[:], ALU.subtract).then_inc(s_cur, 1)
            @steps(dve, NT // 2)
            def _(i):
                for k in range(2):
                    nc.vector.tensor_scalar(ohi[:, k, :], iot[:, 0:128], hif[:, bass.ds(2 * i + k, 1)], None, ALU.is_equal)
                    nc.vector.tensor_scalar(olo[:, k, :], iot[:], lof[:, bass.ds(2 * i + k, 1)], None, ALU.is_equal).then_inc(s_ohB, 1)
                    dve.wait_ge(s_srcb[k], 16 * (i + 1))
                    nc.vector.tensor_copy(srcbf[:, k, :], srcb[:, k, :]).then_inc(s_dv2, 1)
                    dve.wait_ge(s_look, 2 * i + k + 1)
                    nc.vector.tensor_tensor(cur[:, 1 - k, :], cur[:, k, :], pH[:, 0:LO], ALU.add).then_inc(s_cur, 1)
                    dve.wait_ge(s_dv2, 2 * i + k + 1)
                    nc.vector.scalar_tensor_tensor(out=junk[:, 0, 0:TP], in0=srcbf[:, k, :], scalar=srcf[:, bass.ds(2 * i + k, 1)],
                                                   in1=triL[:], op0=ALU.is_equal, op1=ALU.mult, accum_out=hit[:, k, 0:1])
                    nc.vector.scalar_tensor_tensor(out=junk[:, 1, :], in0=pL[0:TP, k, 0:LO], scalar=1.0, in1=olo[:, k, :],
                                                   op0=ALU.mult, op1=ALU.mult, accum_out=hit[:, k, 1:2])
                    nc.vector.scalar_tensor_tensor(out=junk[:, 2, :], in0=pE[0:TP, 0:LO], scalar=1.0, in1=olo[:, k, :],
                                                   op0=ALU.mult, op1=ALU.mult, accum_out=hit[:, k, 2:3]).then_inc(s_used, 1)
                    dve.wait_ge(s_used, 2 * i + k + 1)
                    nc.vector.tensor_tensor(slotf[:, bass.ds(2 * i + k, 1)], hit[:, k, 0:1], hit[:, k, 1:2], ALU.add)
                    nc.vector.tensor_copy(sendf[:, bass.ds(2 * i + k, 1)], hit[:, k, 2:3]).then_inc(s_slot, 1)
            dve.wait_ge(s_slot, NT)
            nc.vector.tensor_copy(slotI[:], slotf[:])
            nc.vector.tensor_copy(K["send"][:], sendf[:])
            dve.wait_ge(s_gcp, NC)
            link(nc.vector.tensor_scalar(tmp[:], posS[:], float(E), None, ALU.is_equal))
            link(nc.vector.tensor_tensor(tmp[:], tmp[:], ef[:], ALU.mult))
            link(nc.vector.tensor_tensor(idxSf[:], posS[:], tmp[:], ALU.add))
            nc.vector.tensor_copy(K["idxS"][:], idxSf[:])
            nc.vector.tensor_copy(pay[:, :, 0], srcf[:])
            nc.vector.tensor_copy(pay[:, :, 1], posE[:])
            nc.vector.tensor_copy(pay[:, :, 2], hwE[:])
            nc.vector.tensor_copy(pay[:, :, 3], idxSf[:]).then_inc(s_done, 1)
            dve.wait_ge(s_s4, 16)
            nc.vector.tensor_copy(K["s_idxE"][:], s4[:, :, 1])
            nc.vector.tensor_copy(K["s_idxS"][:], s4[:, :, 3])
            dve.wait_ge(s_rowT, 1)
            nc.vector.tensor_copy(rowS[:], pR[0:NT, 0:TP])
            nc.vector.tensor_copy(rowH[:], pR[0:NT, TP:2 * TP]).then_inc(s_row, 1)
            dve.wait_ge(s_rown, 16)
            link(nc.vector.tensor_tensor(rowE[:], rowS[:], rowN[:], ALU.is_equal))
            nc.vector.scalar_tensor_tensor(out=rowI[:], in0=rowE[:], scalar=float(FAR), in1=rowS[:],
                                           op0=ALU.mult, op1=ALU.add).then_inc(s_rowi, 1)
            dve.wait_ge(s_colT, 1)
            link(nc.vector.tensor_copy(K["src_end"][:], pR[0:TP, 256:256 + NT]))

        @block.tensor
        def _(pe):
            pe.wait_ge(s_cst, 1)
            nc.tensor.matmul(pH[:, 0:LO], zero[:, 0:128], zero[:], start=True, stop=False)
            @steps(pe, NT // 2)
            def _(i):
                for k in range(2):
                    pe.wait_ge(s_ohA, 2 * i + k + 1)
                    nc.tensor.matmul(pH[:, 0:LO], ohi[:, k, :], olo[:, k, :], start=False, stop=False).then_inc(s_hist, 1)
            nc.tensor.matmul(pH[:, 0:LO], zero[:, 0:128], zero[:], start=False, stop=True).then_inc(s_hist_all, 1)
            pe.wait_ge(s_tot, 1)
            nc.tensor.matmul(pR[:, 0:1], tri[:], inc[:, LO - 1:LO], start=True, stop=True).then_inc(s_off, 1)
            @steps(pe, NT // 2)
            def _(i):
                for k in range(2):
                    pe.wait_ge(s_ohB, 2 * i + k + 1)
                    nc.tensor.transpose(pT[:, k, 0:TP], ohi[:, k, :], K["identb"][0:TP, 0:TP]).then_inc(s_tr, 1)
                    pe.wait_ge(s_hiT, 2 * i + k + 1)
                    pe.wait_ge(s_cur, 2 * i + k + 1)
                    pe.wait_ge(s_used, 2 * i + k)
                    nc.tensor.matmul(pH[:, 0:LO], ohi[:, k, :], olo[:, k, :], start=True, stop=True)
                    nc.tensor.matmul(pL[0:TP, k, 0:LO], hiT[:, k, :], cur[:, k, :], start=True, stop=True)
                    nc.tensor.matmul(pE[0:TP, 0:LO], hiT[:, k, :], end[:], start=True, stop=True).then_inc(s_look, 1)
            pe.wait_ge(s_s4, 16)
            nc.tensor.transpose(pR[0:NT, 0:TP], s4[:, :, 0], K["ident"][0:TP, 0:TP])
            nc.tensor.transpose(pR[0:NT, TP:2 * TP], s4[:, :, 2], K["ident"][0:TP, 0:TP]).then_inc(s_rowT, 1)
            pe.wait_ge(s_rowi, 1)
            nc.tensor.transpose(pR[0:TP, 256:256 + NT], rowI[:], K["ident"][0:NT, 0:NT]).then_inc(s_colT, 1)

        @block.scalar
        def _(act):
            @steps(act, NT // 2)
            def _(i):
                for k in range(2):
                    act.wait_ge(s_tr, 2 * i + k + 1)
                    act.wait_ge(s_look, 2 * i + k)
                    nc.scalar.activation(hiT[:, k, :], pT[:, k, 0:TP], ACT.Copy).then_inc(s_hiT, 1)


def gathers(pool, s_go, s_ring, s_full, ring, index, c, n, table, buf):
    nc = pool.bass
    nc.gpsimd.tensor_copy(ring[:], index[:, bass.ds(CT * c, CT)]).then_inc(s_ring, 1)
    pool.wait_ge(s_ring, n)
    pool.sem_inc(s_go, 1)
    for k in range(CT):
        nc.gpsimd.indirect_dma_start(out=buf[:, k, :], out_offset=None, in_=table,
                                     in_offset=bass.IndirectOffsetOnAxis(ap=ring[:, k:k + 1], axis=0)).then_inc(s_full, 16)


def row_stats(nc, z, rows, st, mv, s_stats):
    for r in range(rows):
        last = nc.vector.bn_stats(st[:, r, :], z[:, r, :])
    last.then_inc(s_stats, 1)


def row_aggr(nc, rows, st, mv):
    for r in range(rows):
        last = nc.vector.bn_aggr(mv[:, r, :], st[:, r, :])
    return last


def normalize(nc, out, z, rows, mv, rs):
    for r in range(rows):
        last = nc.vector.tensor_scalar(out[:, r, :], z[:, r, :], mv[:, r, 0:1], rs[:, r:r + 1], ALU.subtract, ALU.mult)
    return last


def bc(vec, rows):
    p = vec.shape[0]
    return vec[:, :].rearrange("p (o f) -> p o f", o=1).broadcast_to([p, rows, D])


def attention_phase(nc, g, K, T):
    with ExitStack() as ctx:
        a = Place(nc, ctx, "at")
        W = {n: a.sb(n, [D, D]) for n in ("Wq", "Wk", "Wv", "Wo")}
        cols = K["cols"]
        bo = a.sb("bo", [TP, D])
        eps = a.sb("eps", [128, 1])
        rs_, rd_ = a.sb("ring_s", [TP, CT], I32), a.sb("ring_d", [TP, CT], I32)
        srcI, dstI = a.sb("srcI", [TP, NT], I32), a.sb("dstI", [TP, NT], I32)
        ga, gb = a.sb("ga", [TP, CT, D]), a.sb("gb", [TP, CT, D])
        xs, xd, q, prod, f, p, pv, dif, o, oF = (a.sb(n, [D, CE]) for n in ("xs", "xd", "q", "prod", "f", "p", "pv", "dif", "o", "oF"))
        dr, rc = a.sb("dr", [D, CE]), a.sb("rc", [D, CE])
        t1, t2 = a.sb("t1", [D, CE]), a.sb("t2", [D, CE])
        dstb = a.sb("dstb", [D, CE + 1], I32)
        same, pen = a.sb("same", [D, CE]), a.sb("pen", [D, CE])
        eb = a.sb("eb", [8, CE])
        M, Nu, De = (a.sb(n, [D, CE + 1]) for n in ("M", "Nu", "De"))
        z, y = a.sb("z", [TP, 2 * CT, D]), a.sb("y", [TP, 2 * CT, D])
        st, mv, sd, rs = a.sb("st", [TP, 2 * CT, 6]), a.sb("mv", [TP, 2 * CT, 2]), a.sb("sd", [TP, 2 * CT]), a.sb("rs", [TP, 2 * CT])
        pA, pB, pQ, pK, pV, pAt, pO, pR = (a.ps(n, [128, 512]) for n in ("pA", "pB", "pQ", "pK", "pV", "pAt", "pO", "pR"))
        (s_w, s_go, s_ring, s_ga, s_gb, s_tA, s_tB, s_xs, s_xd, s_psQ, s_psK, s_psV, s_q, s_prod, s_att, s_args, s_exp, s_pv,
         s_o, s_psO, s_oF, s_psR, s_z, s_gbc, s_mask, s_sd, s_mv, s_y, s_eb, s_dstb, s_st, s_zs, s_dgo, s_ch, s_d, s_eps, s_init) = (
            a.sem(n) for n in ("weights", "go", "ring", "ga", "gb", "tA", "tB", "xs", "xd", "psQ", "psK", "psV", "q", "prod", "att",
                               "args", "exp", "pv", "o", "psO", "oF", "psR", "z", "gb_copied", "mask", "sd", "mv", "y", "eb",
                               "dstb", "stored", "zs", "dve_go", "chain", "stats", "eps", "init"))
        block = ctx.enter_context(nc.Block())

        @block.sync
        def _(sp):
            for n in W:
                sp.dma_start(W[n][:], g[n]).then_inc(s_w, 16)
            sp.dma_start(bo[:], g["rowv"][0:1, :].broadcast_to([TP, D])).then_inc(s_w, 16)
            sp.dma_start(srcI[:], g["src_col"]).then_inc(s_w, 16)
            sp.dma_start(dstI[:], g["dst_col"]).then_inc(s_w, 16)
            sp.dma_start(dstb[:], g["dst_pad"][:, 0:CE + 1].broadcast_to([D, CE + 1])).then_inc(s_dstb, 16)
            sp.dma_start(eb[:], g["ea8T"][:, 0:CE]).then_inc(s_eb, 16)

            def store(c):
                sp.wait_ge(s_y, c + 1)
                sp.dma_start(rows_of(T["T1"], CE * c, CT), y[:, 0:CT, :]).then_inc(s_st, 16)
                sp.dma_start(rows_of(T["T1"], CE * c + E, CT), y[:, CT:2 * CT, :]).then_inc(s_st, 16)

            @steps(sp, NC - 1)
            def _(c):
                sp.wait_ge(s_mask, c + 1)
                sp.dma_start(dstb[:], g["dst_pad"][:, bass.ds(CE * c + CE, CE + 1)].broadcast_to([D, CE + 1])).then_inc(s_dstb, 16)
                sp.wait_ge(s_att, c + 1)
                sp.dma_start(eb[:], g["ea8T"][:, bass.ds(CE * c + CE, CE)]).then_inc(s_eb, 16)
                store(c)
            store(NC - 1)
            sp.wait_ge(s_st, 32 * NC)

        @block.gpsimd
        def _(pool):
            pool.wait_ge(s_w, 16 * 7)
            nc.gpsimd.memset(eps[:], EPS).then_inc(s_eps, 1)
            @steps(pool, NC)
            def _(c):
                pool.wait_ge(s_zs, c)
                pool.wait_ge(s_tA, c)
                pool.sem_inc(s_go, 1)
                gathers(pool, s_go, s_ring, s_ga, rs_, srcI, c, 2 * c + 1, g["x"], ga)
                pool.wait_ge(s_gbc, c)
                pool.wait_ge(s_tB, c)
                pool.sem_inc(s_go, 1)
                gathers(pool, s_go, s_ring, s_gb, rd_, dstI, c, 2 * c + 2, g["x"], gb)

        @block.tensor
        def _(pe):
            pe.wait_ge(s_w, 16 * 7)
            @steps(pe, NC)
            def _(c):
                pe.wait_ge(s_ga, 64 * (c + 1))
                for k in range(CT):
                    last = nc.tensor.transpose(pA[:, k * TP:(k + 1) * TP], ga[:, k, :], K["ident"][0:TP, 0:TP])
                last.then_inc(s_tA, 1)
                pe.wait_ge(s_gb, 64 * (c + 1))
                for k in range(CT):
                    last = nc.tensor.transpose(pB[:, k * TP:(k + 1) * TP], gb[:, k, :], K["ident"][0:TP, 0:TP])
                last.then_inc(s_tB, 1)
                pe.wait_ge(s_xd, c + 1)
                nc.tensor.matmul(pQ[:, 0:CE], W["Wq"][:], xd[:], start=True, stop=True).then_inc(s_psQ, 1)
                pe.wait_ge(s_xs, c + 1)
                nc.tensor.matmul(pK[:, 0:CE], W["Wk"][:], xs[:], start=True, stop=True).then_inc(s_psK, 1)
                nc.tensor.matmul(pV[:, 0:CE], W["Wv"][:], xs[:], start=True, stop=True).then_inc(s_psV, 1)
                pe.wait_ge(s_prod, c + 1)
                pe.wait_ge(s_eb, 16 * (c + 1))
                nc.tensor.matmul(pAt[:, 0:CE], K["heads"][:], prod[:], start=True, stop=False)
                nc.tensor.matmul(pAt[:, 0:CE], K["expand"][:], eb[:], start=False, stop=True).then_inc(s_att, 1)
                pe.wait_ge(s_o, c + 1)
                nc.tensor.matmul(pO[:, 0:CE], W["Wo"][:], o[:], start=True, stop=True).then_inc(s_psO, 1)
                pe.wait_ge(s_oF, c + 1)
                for k in range(CT):
                    last = nc.tensor.transpose(pR[0:TP, k * D:(k + 1) * D], oF[:, k * TP:(k + 1) * TP], K["ident"][:])
                last.then_inc(s_psR, 1)

        @block.scalar
        def _(act):
            act.wait_ge(s_eps, 1)
            act.wait_ge(s_w, 16 * 7)
            @steps(act, NC)
            def _(c):
                act.wait_ge(s_tA, c + 1)
                act.wait_ge(s_psV, c)
                nc.scalar.activation(xs[:], pA[:, 0:CE], ACT.Copy).then_inc(s_xs, 1)
                act.wait_ge(s_tB, c + 1)
                act.wait_ge(s_psQ, c)
                nc.scalar.activation(xd[:], pB[:, 0:CE], ACT.Copy).then_inc(s_xd, 1)
                act.wait_ge(s_y, c)
                nc.scalar.activation(z[:, 0:CT, :], gb[:], ACT.Copy).then_inc(s_gbc, 1)
                act.wait_ge(s_psQ, c + 1)
                act.wait_ge(s_prod, c)
                nc.scalar.activation(q[:], pQ[:, 0:CE], ACT.Identity, bias=cols[:, 0:1]).then_inc(s_q, 1)
                act.wait_ge(s_args, c + 1)
                nc.scalar.activation(f[:], t2[:], ACT.Exp)
                nc.scalar.activation(p[:], dif[:], ACT.Exp).then_inc(s_exp, 1)
                act.wait_ge(s_psO, c + 1)
                act.wait_ge(s_psR, c)
                nc.scalar.activation(oF[:], pO[:, 0:CE], ACT.Identity, bias=cols[:, 3:4]).then_inc(s_oF, 1)
                act.wait_ge(s_mv, c + 1)
                nc.scalar.activation(sd[:], mv[:, :, 1], ACT.Sqrt, bias=eps[0:TP, :]).then_inc(s_sd, 1)

        @block.vector
        def _(dve):
            nc.vector.memset(M[:], -NEG)
            nc.vector.memset(Nu[:], 0.0)
            first = nc.vector.memset(De[:], 0.0)
            first.then_inc(s_init, 1)
            dve.wait_ge(s_init, 1)
            dve.wait_ge(s_w, 16 * 7)
            @steps(dve, NC)
            def _(c):
                link = Chain(dve, s_ch, c, 9)
                dve.wait_ge(s_dstb, 16 * (c + 1))
                nc.vector.tensor_tensor(same[:], dstb[:, 1:CE + 1], dstb[:, 0:CE], ALU.is_equal).then_inc(s_mask, 1)
                dve.wait_ge(s_mask, c + 1)
                nc.vector.tensor_scalar(pen[:], same[:], NEG, -NEG, ALU.mult, ALU.add)
                dve.wait_ge(s_ga, 64 * (c + 1))
                nc.vector.tensor_tensor(z[:, CT:2 * CT, :], ga[:], bc(bo, CT), ALU.add).then_inc(s_zs, 1)
                dve.wait_ge(s_psK, c + 1)
                dve.wait_ge(s_q, c + 1)
                nc.vector.scalar_tensor_tensor(out=prod[:], in0=pK[:, 0:CE], scalar=cols[:, 1:2], in1=q[:],
                                               op0=ALU.add, op1=ALU.mult).then_inc(s_prod, 1)
                nc.vector.tensor_copy(M[:, 0:1], M[:, CE:CE + 1])
                nc.vector.tensor_copy(Nu[:, 0:1], Nu[:, CE:CE + 1])
                link(nc.vector.tensor_copy(De[:, 0:1], De[:, CE:CE + 1]))
                dve.wait_ge(s_att, c + 1)
                link(nc.vector.tensor_tensor_scan(M[:, 1:CE + 1], pen[:], pAt[:, 0:CE], M[:, 0:1], ALU.add, ALU.max))
                nc.vector.tensor_tensor(dif[:], pAt[:, 0:CE], M[:, 1:CE + 1], ALU.subtract)
                link(nc.vector.tensor_tensor(t1[:], M[:, 0:CE], M[:, 1:CE + 1], ALU.subtract))
                nc.vector.scalar_tensor_tensor(out=t2[:], in0=t1[:], scalar=0.0, in1=pen[:], op0=ALU.min, op1=ALU.add).then_inc(s_args, 1)
                dve.wait_ge(s_exp, c + 1)
                dve.wait_ge(s_psV, c + 1)
                link(nc.vector.scalar_tensor_tensor(out=pv[:], in0=pV[:, 0:CE], scalar=cols[:, 2:3], in1=p[:], op0=ALU.add, op1=ALU.mult))
                nc.vector.tensor_tensor_scan(De[:, 1:CE + 1], f[:], p[:], De[:, 0:1], ALU.mult, ALU.add)
                link(nc.vector.tensor_tensor_scan(Nu[:, 1:CE + 1], f[:], pv[:], Nu[:, 0:1], ALU.mult, ALU.add))
                link(nc.vector.tensor_scalar(dr[:], De[:, 1:CE + 1], 1e-16, None, ALU.add))
                link(nc.vector.reciprocal(rc[:], dr[:]))
                nc.vector.tensor_tensor(o[:], Nu[:, 1:CE + 1], rc[:], ALU.mult).then_inc(s_o, 1)
                dve.wait_ge(s_gbc, c + 1)
                dve.wait_ge(s_psR, c + 1)
                link(nc.vector.tensor_tensor(z[:, 0:CT, :], z[:, 0:CT, :], pR[0:TP, :].rearrange("p (k f) -> p k f", k=CT), ALU.add))
                row_stats(nc, z, 2 * CT, st, mv, s_d)
                dve.wait_ge(s_d, c + 1)
                dve.sem_inc(s_dgo, 1)
                row_aggr(nc, 2 * CT, st, mv).then_inc(s_mv, 1)
                dve.wait_ge(s_sd, c + 1)
                link(nc.vector.reciprocal(rs[:], sd[:]))
                dve.wait_ge(s_st, 32 * c)
                normalize(nc, y, z, 2 * CT, mv, rs).then_inc(s_y, 1)
                dve.wait_ge(s_y, c + 1)
                link.done()


def message_phase(nc, g, K, T):
    with ExitStack() as ctx:
        a = Place(nc, ctx, "ms")
        Wx, Wu = a.sb("Wx", [D, D]), a.sb("Wu", [D, D])
        We, emb = a.sb("We", [32, D]), a.sb("emb", [32, 16])
        typeW = a.sb("typeW", [16, D])
        ub, lg, lb = a.sb("ub", [TP, D]), a.sb("lg", [TP, D]), a.sb("lb", [TP, D])
        eps, one = a.sb("eps", [128, 1]), a.sb("one", [1, CE])
        kind, kindf = a.sb("kind", [16, 1], I32), a.sb("kindf", [16, 1])
        ring = a.sb("ring", [TP, CT], I32)
        ga = a.sb("ga", [TP, CT, D])
        xin = a.sb("xin", [TP, 2 * CT, D])
        xs, m, S, oF = (a.sb(n, [D, CE]) for n in ("xs", "m", "S", "oF"))
        carry = a.sb("carry", [D, 1])
        dstb, same = a.sb("dstb", [D, CE + 1], I32), a.sb("same", [D, CE])
        typ, oneh = a.sb("typ", [16, CE], I32), a.sb("oneh", [16, CE])
        deg = a.sb("deg", [1, CE + 1])
        rd = a.sb("rd", [TP, CT])
        h, n1, y = (a.sb(n, [TP, 2 * CT, D]) for n in ("h", "n1", "y"))
        st, mv, sd, rs = a.sb("st", [TP, 2 * CT, 6]), a.sb("mv", [TP, 2 * CT, 2]), a.sb("sd", [TP, 2 * CT]), a.sb("rs", [TP, 2 * CT])
        pA, pM, pO, pR, pD = (a.ps(n, [128, 512]) for n in ("pA", "pM", "pO", "pR", "pD"))
        (s_w, s_go, s_ring, s_ga, s_xd, s_dstb, s_typ, s_st, s_eps, s_kind, s_init, s_tw, s_tA, s_xs, s_gac, s_mask, s_oneh,
         s_psM, s_m, s_S, s_psO, s_oF, s_psR, s_deg, s_psD, s_mv, s_sd, s_mv2, s_sd2, s_y, s_ch, s_d, s_dgo, s_h, s_twc, s_rdc) = (
            a.sem(n) for n in ("weights", "go", "ring", "ga", "xd", "dstb", "type", "stored", "eps", "kind", "init", "typeW",
                               "tA", "xs", "ga_copied", "mask", "onehot", "psM", "m", "S", "psO", "oF", "psR", "deg", "psD",
                               "mv", "sd", "mv2", "sd2", "y", "chain", "stats", "dve_go", "h", "typeW_copied", "rdeg"))
        block = ctx.enter_context(nc.Block())

        @block.sync
        def _(sp):
            for t, n in ((Wx, "Wmx"), (Wu, "Wu"), (We, "Wme"), (emb, "embT")):
                sp.dma_start(t[:], g[n]).then_inc(s_w, 16)
            for t, r in ((ub, 1), (lg, 2), (lb, 3)):
                sp.dma_start(t[:], g["rowv"][r:r + 1, :].broadcast_to([TP, D])).then_inc(s_w, 16)

            def load_masks(e0):
                sp.dma_start(dstb[:], g["dst_pad"][:, bass.ds(e0, CE + 1)].broadcast_to([D, CE + 1])).then_inc(s_dstb, 16)

            def load_types(e0):
                sp.dma_start(typ[:], g["type_row"][:, bass.ds(e0, CE)].broadcast_to([16, CE])).then_inc(s_typ, 16)

            def load_targets(e0):
                sp.dma_start(xin[:, 0:CT, :], rows_of(T["T1"], e0, CT)).then_inc(s_xd, 16)

            def store(c):
                sp.wait_ge(s_y, c + 1)
                sp.dma_start(rows_of(T["T2"], CE * c, CT), y[:, 0:CT, :]).then_inc(s_st, 16)
                sp.dma_start(rows_of(T["T2"], CE * c + E, CT), y[:, CT:2 * CT, :]).then_inc(s_st, 16)

            load_masks(0)
            load_types(0)
            load_targets(0)
            @steps(sp, NC - 1)
            def _(c):
                sp.wait_ge(s_mask, c + 1)
                load_masks(CE * c + CE)
                sp.wait_ge(s_oneh, c + 1)
                load_types(CE * c + CE)
                store(c)
                load_targets(CE * c + CE)
            store(NC - 1)
            sp.wait_ge(s_st, 32 * NC)

        @block.gpsimd
        def _(pool):
            nc.gpsimd.memset(one[:], 1.0)
            nc.gpsimd.iota(kind[:], pattern=[[0, 1]], base=0, channel_multiplier=1).then_inc(s_kind, 1)
            pool.wait_ge(s_kind, 1)
            nc.gpsimd.tensor_copy(kindf[:], kind[:])
            nc.gpsimd.memset(eps[:], EPS).then_inc(s_eps, 1)
            @steps(pool, NC)
            def _(c):
                pool.wait_ge(s_gac, c)
                pool.wait_ge(s_tA, c)
                pool.sem_inc(s_go, 1)
                gathers(pool, s_go, s_ring, s_ga, ring, K["idxS"], c, c + 1, T["T1"], ga)

        @block.tensor
        def _(pe):
            pe.wait_ge(s_w, 16 * 7)
            nc.tensor.matmul(pM[0:16, 0:D], emb[:], We[:], start=True, stop=True).then_inc(s_tw, 1)
            pe.wait_ge(s_twc, 1)
            @steps(pe, NC)
            def _(c):
                pe.wait_ge(s_ga, 64 * (c + 1))
                for k in range(CT):
                    last = nc.tensor.transpose(pA[:, k * TP:(k + 1) * TP], ga[:, k, :], K["ident"][0:TP, 0:TP])
                last.then_inc(s_tA, 1)
                pe.wait_ge(s_xs, c + 1)
                pe.wait_ge(s_oneh, c + 1)
                nc.tensor.matmul(pM[:, 0:CE], Wx[:], xs[:], start=True, stop=False)
                nc.tensor.matmul(pM[:, 0:CE], typeW[:], oneh[:], start=False, stop=True).then_inc(s_psM, 1)
                pe.wait_ge(s_deg, c + 1)
                for k in range(CT):
                    last = nc.tensor.matmul(pD[0:TP, k:k + 1], deg[0:1, 1 + k * TP:1 + (k + 1) * TP], one[0:1, 0:1], start=True, stop=True)
                last.then_inc(s_psD, 1)
                pe.wait_ge(s_S, c + 1)
                nc.tensor.matmul(pO[:, 0:CE], Wu[:], S[:], start=True, stop=True).then_inc(s_psO, 1)
                pe.wait_ge(s_oF, c + 1)
                for k in range(CT):
                    last = nc.tensor.transpose(pR[0:TP, k * D:(k + 1) * D], oF[:, k * TP:(k + 1) * TP], K["ident"][:])
                last.then_inc(s_psR, 1)

        @block.scalar
        def _(act):
            act.wait_ge(s_tw, 1)
            nc.scalar.activation(typeW[:], pM[0:16, 0:D], ACT.Copy).then_inc(s_twc, 1)
            act.wait_ge(s_eps, 1)
            act.wait_ge(s_w, 16 * 7)
            @steps(act, NC)
            def _(c):
                act.wait_ge(s_tA, c + 1)
                act.wait_ge(s_psM, c)
                nc.scalar.activation(xs[:], pA[:, 0:CE], ACT.Copy).then_inc(s_xs, 1)
                act.wait_ge(s_y, c)
                nc.scalar.activation(xin[:, CT:2 * CT, :], ga[:], ACT.Copy).then_inc(s_gac, 1)
                act.wait_ge(s_psM, c + 1)
                act.wait_ge(s_S, c)
                nc.scalar.activation(m[:], pM[:, 0:CE], ACT.Relu, bias=K["cols"][:, 4:5]).then_inc(s_m, 1)
                act.wait_ge(s_psO, c + 1)
                act.wait_ge(s_psR, c)
                nc.scalar.activation(oF[:], pO[:, 0:CE], ACT.Copy).then_inc(s_oF, 1)
                act.wait_ge(s_mv, c + 1)
                nc.scalar.activation(sd[:], mv[:, :, 1], ACT.Sqrt, bias=eps[0:TP, :]).then_inc(s_sd, 1)
                act.wait_ge(s_mv2, c + 1)
                nc.scalar.activation(sd[:], mv[:, :, 1], ACT.Sqrt, bias=eps[0:TP, :]).then_inc(s_sd2, 1)

        @block.vector
        def _(dve):
            nc.vector.memset(carry[:], 0.0)
            nc.vector.memset(deg[:], 0.0).then_inc(s_init, 1)
            dve.wait_ge(s_init, 1)
            dve.wait_ge(s_eps, 1)
            dve.wait_ge(s_w, 16 * 7)
            @steps(dve, NC)
            def _(c):
                link = Chain(dve, s_ch, c, 9)
                dve.wait_ge(s_typ, 16 * (c + 1))
                dve.wait_ge(s_psM, c)
                nc.vector.tensor_scalar(oneh[:], typ[:], kindf[:, 0:1], None, ALU.is_equal).then_inc(s_oneh, 1)
                dve.wait_ge(s_dstb, 16 * (c + 1))
                nc.vector.tensor_tensor(same[:], dstb[:, 1:CE + 1], dstb[:, 0:CE], ALU.is_equal).then_inc(s_mask, 1)
                dve.wait_ge(s_psD, c)
                link(nc.vector.tensor_copy(deg[:, 0:1], deg[:, CE:CE + 1]))
                dve.wait_ge(s_mask, c + 1)
                nc.vector.tensor_tensor_scan(deg[:, 1:CE + 1], same[0:1, :], one[:], deg[:, 0:1], ALU.mult, ALU.add).then_inc(s_deg, 1)
                dve.wait_ge(s_m, c + 1)
                dve.wait_ge(s_psO, c)
                nc.vector.tensor_tensor_scan(S[:], same[:], m[:], carry[:], ALU.mult, ALU.add).then_inc(s_S, 1)
                dve.wait_ge(s_psD, c + 1)
                nc.vector.reciprocal(rd[:], pD[0:TP, 0:CT]).then_inc(s_rdc, 1)
                dve.wait_ge(s_S, c + 1)
                nc.vector.tensor_copy(carry[:], S[:, CE - 1:CE])
                dve.wait_ge(s_xd, 16 * (c + 1))
                dve.wait_ge(s_gac, c + 1)
                link(nc.vector.tensor_tensor(h[:], xin[:], bc(ub, 2 * CT), ALU.add))
                nc.vector.tensor_copy(K["rdeg"][:, bass.ds(CT * c, CT)], rd[:])
                nc.vector.tensor_tensor(K["rdegH"][:, bass.ds(CT * c, CT)], rd[:], K["isH"][:, bass.ds(CT * c, CT)], ALU.mult)
                dve.wait_ge(s_psR, c + 1)
                for k in range(CT):
                    last = nc.vector.scalar_tensor_tensor(out=h[:, k, :], in0=pR[0:TP, k * D:(k + 1) * D], scalar=rd[:, k:k + 1],
                                                          in1=h[:, k, :], op0=ALU.mult, op1=ALU.add)
                link(last)
                row_stats(nc, h, 2 * CT, st, mv, s_d)
                dve.wait_ge(s_d, 2 * c + 1)
                dve.sem_inc(s_dgo, 1)
                row_aggr(nc, 2 * CT, st, mv).then_inc(s_mv, 1)
                dve.wait_ge(s_sd, c + 1)
                link(nc.vector.reciprocal(rs[:], sd[:]))
                link(normalize(nc, n1, h, 2 * CT, mv, rs))
                link(nc.vector.tensor_tensor(h[:], n1[:], bc(lg, 2 * CT), ALU.mult))
                link(nc.vector.tensor_tensor(n1[:], h[:], bc(lb, 2 * CT), ALU.add))
                link(nc.vector.tensor_tensor(h[:], n1[:], xin[:], ALU.add))
                row_stats(nc, h, 2 * CT, st, mv, s_d)
                dve.wait_ge(s_d, 2 * c + 2)
                dve.sem_inc(s_dgo, 1)
                row_aggr(nc, 2 * CT, st, mv).then_inc(s_mv2, 1)
                dve.wait_ge(s_sd2, c + 1)
                link(nc.vector.reciprocal(rs[:], sd[:]))
                dve.wait_ge(s_st, 32 * c)
                normalize(nc, y, h, 2 * CT, mv, rs).then_inc(s_y, 1)
                dve.wait_ge(s_y, c + 1)
                link.done()


def equivariant_phase(nc, g, K, T):
    with ExitStack() as ctx:
        a = Place(nc, ctx, "eq")
        A1, B1 = a.sb("A1", [D, D]), a.sb("B1", [D, D])
        fc1 = a.sb("fc1", [8, 64])
        fA, fB, fC = (a.sb(n, [64, D]) for n in ("fA", "fB", "fC"))
        oA, oB, oC = (a.sb(n, [D, D]) for n in ("oA", "oB", "oC"))
        eps = a.sb("eps", [128, 1])
        ring = a.sb("ring", [TP, CT], I32)
        ga = a.sb("ga", [TP, CT, D])
        z, y = a.sb("z", [TP, 2 * CT, D]), a.sb("y", [TP, 2 * CT, D])
        xs, sv, se = (a.sb(n, [D, CE]) for n in ("xs", "sv", "se"))
        u1, u2, u3, u4, u5, u6 = (a.sb(f"u{i}", [D, CE]) for i in range(1, 7))
        S, mid = a.sb("S", [D, CE]), a.sb("mid", [D, CE])
        carry = a.sb("carry", [D, 1])
        dstb, same = a.sb("dstb", [D, CE + 1], I32), a.sb("same", [D, CE])
        ea8 = a.sb("ea8", [8, CE])
        es, ev = a.sb("es", [D, CE]), a.sb("ev", [D, CE])
        hid, sg = a.sb("hid", [64, CE]), a.sb("sg", [64, CE])
        st, mv, sd, rs = a.sb("st", [TP, 2 * CT, 6]), a.sb("mv", [TP, 2 * CT, 2]), a.sb("sd", [TP, 2 * CT]), a.sb("rs", [TP, 2 * CT])
        pX, pP, pQ, pA, pB, pC, pH, pR = (a.ps(n, [128, 512]) for n in ("pX", "pP", "pQ", "pA", "pB", "pC", "pH", "pR"))
        (s_w, s_go, s_ring, s_ga, s_zd, s_dstb, s_ea8, s_es, s_st, s_eps, s_init, s_tA, s_xs, s_gac, s_psH, s_sg, s_hid, s_psW,
         s_psX, s_sv, s_u, s_psO, s_S, s_psR, s_mask, s_mv, s_sd, s_y, s_ch, s_d, s_dgo, s_z) = (
            a.sem(n) for n in ("weights", "go", "ring", "ga", "zd", "dstb", "ea8", "es", "stored", "eps", "init", "tA", "xs",
                               "ga_copied", "psH", "sg", "hid", "psW", "psX", "sv", "u", "psO", "S", "psR", "mask", "mv", "sd",
                               "y", "chain", "stats", "dve_go", "z"))
        block = ctx.enter_context(nc.Block())
        by_lin1 = 1.0 / 32.0 ** 0.5
        by_rest = SILU / (64.0 ** 0.5) / (16.0 ** 0.5) / (64.0 ** 0.5)

        @block.sync
        def _(sp):
            for t, n in ((A1, "L1A"), (B1, "L1B"), (fc1, "fc1"), (fA, "fcA"), (fB, "fcB"), (fC, "fcC"), (oA, "oA"), (oB, "oB"), (oC, "oC")):
                sp.dma_start(t[:], g[n]).then_inc(s_w, 16)

            def load_masks(e0):
                sp.dma_start(dstb[:], g["dst_pad"][:, bass.ds(e0, CE + 1)].broadcast_to([D, CE + 1])).then_inc(s_dstb, 16)

            def load_scalars(e0):
                sp.dma_start(ea8[:], g["ea8T"][:, bass.ds(e0, CE)]).then_inc(s_ea8, 16)

            def load_attr(e0):
                sp.dma_start(es[:], g["ea4T"][0:1, bass.ds(e0, CE)].broadcast_to([D, CE])).then_inc(s_es, 16)
                for j in range(4):
                    sp.dma_start(ev[32 * j:32 * j + 32, :], g["ea4T"][j:j + 1, bass.ds(e0, CE)].broadcast_to([32, CE])).then_inc(s_es, 16)

            def load_targets(e0):
                sp.dma_start(z[:, 0:CT, :], rows_of(T["T2"], e0, CT)).then_inc(s_zd, 16)

            def store(c):
                sp.wait_ge(s_y, c + 1)
                sp.dma_start(rows_of(T["T3"], CE * c, CT), y[:, 0:CT, :]).then_inc(s_st, 16)
                sp.dma_start(rows_of(T["T3"], CE * c + E, CT), y[:, CT:2 * CT, :]).then_inc(s_st, 16)

            load_masks(0)
            load_scalars(0)
            load_attr(0)
            load_targets(0)
            @steps(sp, NC - 1)
            def _(c):
                sp.wait_ge(s_psH, c + 1)
                load_scalars(CE * c + CE)
                sp.wait_ge(s_mask, c + 1)
                load_masks(CE * c + CE)
                sp.wait_ge(s_u, c + 1)
                load_attr(CE * c + CE)
                store(c)
                load_targets(CE * c + CE)
            store(NC - 1)
            sp.wait_ge(s_st, 32 * NC)

        @block.gpsimd
        def _(pool):
            nc.gpsimd.memset(eps[:], EPS).then_inc(s_eps, 1)
            @steps(pool, NC)
            def _(c):
                pool.wait_ge(s_gac, c)
                pool.wait_ge(s_tA, c)
                pool.sem_inc(s_go, 1)
                gathers(pool, s_go, s_ring, s_ga, ring, K["idxS"], c, c + 1, T["T2"], ga)

        @block.tensor
        def _(pe):
            pe.wait_ge(s_w, 16 * 9)
            @steps(pe, NC)
            def _(c):
                pe.wait_ge(s_ea8, 16 * (c + 1))
                pe.wait_ge(s_hid, c)
                nc.tensor.matmul(pH[0:64, 0:CE], fc1[:], ea8[:], start=True, stop=True).then_inc(s_psH, 1)
                pe.wait_ge(s_ga, 64 * (c + 1))
                for k in range(CT):
                    last = nc.tensor.transpose(pX[:, k * TP:(k + 1) * TP], ga[:, k, :], K["ident"][0:TP, 0:TP])
                last.then_inc(s_tA, 1)
                pe.wait_ge(s_hid, c + 1)
                pe.wait_ge(s_u, c)
                for w, p in ((fA, pA), (fB, pB), (fC, pC)):
                    last = nc.tensor.matmul(p[:, 0:CE], w[:], hid[:], start=True, stop=True)
                last.then_inc(s_psW, 1)
                pe.wait_ge(s_xs, c + 1)
                nc.tensor.matmul(pP[:, 0:CE], A1[:], xs[:], start=True, stop=True)
                nc.tensor.matmul(pQ[:, 0:CE], B1[:], xs[:], start=True, stop=True).then_inc(s_psX, 1)
                pe.wait_ge(s_u, c + 1)
                nc.tensor.matmul(pX[:, 0:CE], oA[:], u2[:], start=True, stop=False)
                nc.tensor.matmul(pX[:, 0:CE], oB[:], u4[:], start=False, stop=False)
                nc.tensor.matmul(pX[:, 0:CE], oC[:], u6[:], start=False, stop=True).then_inc(s_psO, 1)
                pe.wait_ge(s_S, c + 1)
                for k in range(CT):
                    last = nc.tensor.transpose(pR[0:TP, k * D:(k + 1) * D], S[:, k * TP:(k + 1) * TP], K["ident"][:])
                last.then_inc(s_psR, 1)

        @block.scalar
        def _(act):
            act.wait_ge(s_eps, 1)
            @steps(act, NC)
            def _(c):
                act.wait_ge(s_psH, c + 1)
                act.wait_ge(s_hid, c)
                nc.scalar.activation(sg[:], pH[0:64, 0:CE], ACT.Sigmoid, scale=1.0 / 8.0 ** 0.5).then_inc(s_sg, 1)
                act.wait_ge(s_tA, c + 1)
                act.wait_ge(s_psX, c)
                nc.scalar.activation(xs[:], pX[:, 0:CE], ACT.Copy).then_inc(s_xs, 1)
                act.wait_ge(s_y, c)
                nc.scalar.activation(z[:, CT:2 * CT, :], ga[:], ACT.Copy).then_inc(s_gac, 1)
                act.wait_ge(s_psX, c + 1)
                act.wait_ge(s_u, c)
                nc.scalar.activation(sv[:], pP[:, 0:CE], ACT.Copy, scale=by_lin1)
                nc.scalar.activation(se[:], pQ[:, 0:CE], ACT.Copy, scale=by_lin1).then_inc(s_sv, 1)
                act.wait_ge(s_mv, c + 1)
                nc.scalar.activation(sd[:], mv[:, :, 1], ACT.Sqrt, bias=eps[0:TP, :]).then_inc(s_sd, 1)

        @block.vector
        def _(dve):
            nc.vector.memset(carry[:], 0.0).then_inc(s_init, 1)
            dve.wait_ge(s_init, 1)
            dve.wait_ge(s_eps, 1)
            @steps(dve, NC)
            def _(c):
                link = Chain(dve, s_ch, c, 4)
                dve.wait_ge(s_sg, c + 1)
                dve.wait_ge(s_psW, c)
                nc.vector.scalar_tensor_tensor(out=hid[:], in0=pH[0:64, 0:CE], scalar=1.0 / 8.0 ** 0.5, in1=sg[:],
                                               op0=ALU.mult, op1=ALU.mult).then_inc(s_hid, 1)
                dve.wait_ge(s_dstb, 16 * (c + 1))
                nc.vector.tensor_tensor(same[:], dstb[:, 1:CE + 1], dstb[:, 0:CE], ALU.is_equal).then_inc(s_mask, 1)
                dve.wait_ge(s_es, 80 * (c + 1))
                dve.wait_ge(s_psW, c + 1)
                dve.wait_ge(s_psO, c)
                nc.vector.scalar_tensor_tensor(out=u1[:], in0=pA[:, 0:CE], scalar=by_rest, in1=es[:], op0=ALU.mult, op1=ALU.mult)
                nc.vector.scalar_tensor_tensor(out=u3[:], in0=pB[:, 0:CE], scalar=by_rest, in1=ev[:], op0=ALU.mult, op1=ALU.mult)
                link(nc.vector.scalar_tensor_tensor(out=u5[:], in0=pC[:, 0:CE], scalar=by_rest / 3.0 ** 0.5, in1=ev[:],
                                                    op0=ALU.mult, op1=ALU.mult))
                dve.wait_ge(s_sv, c + 1)
                nc.vector.tensor_tensor(u2[:], u1[:], sv[:], ALU.mult)
                nc.vector.tensor_tensor(u4[:], u3[:], se[:], ALU.mult)
                nc.vector.tensor_tensor(u6[:], u5[:], sv[:], ALU.mult).then_inc(s_u, 1)
                dve.wait_ge(s_psO, c + 1)
                dve.wait_ge(s_psR, c)
                nc.vector.tensor_tensor_scan(S[:], same[:], pX[:, 0:CE], carry[:], ALU.mult, ALU.add).then_inc(s_S, 1)
                dve.wait_ge(s_S, c + 1)
                nc.vector.tensor_copy(carry[:], S[:, CE - 1:CE])
                dve.wait_ge(s_zd, 16 * (c + 1))
                dve.wait_ge(s_gac, c + 1)
                dve.wait_ge(s_psR, c + 1)
                link(nc.vector.tensor_tensor(z[:, 0:CT, :], z[:, 0:CT, :], pR[0:TP, :].rearrange("p (k f) -> p k f", k=CT), ALU.add))
                row_stats(nc, z, 2 * CT, st, mv, s_d)
                dve.wait_ge(s_d, c + 1)
                dve.sem_inc(s_dgo, 1)
                row_aggr(nc, 2 * CT, st, mv).then_inc(s_mv, 1)
                dve.wait_ge(s_sd, c + 1)
                link(nc.vector.reciprocal(rs[:], sd[:]))
                dve.wait_ge(s_st, 32 * c)
                link(normalize(nc, y, z, 2 * CT, mv, rs))
                dve.sem_inc(s_y, 1)
                link.done()


def hyperedge_phase(nc, g, K, T, tag, table, index, weight, out):
    with ExitStack() as ctx:
        a = Place(nc, ctx, tag)
        W = a.sb("W", [D, D])
        ring = a.sb("ring", [TP, CT], I32)
        ga, y = a.sb("ga", [TP, CT, D]), a.sb("y", [TP, CT, D])
        xs, S = a.sb("xs", [D, CE]), a.sb("S", [D, CE])
        carry, zrow = a.sb("carry", [D, 1]), a.sb("zrow", [1, D])
        dstb, same = a.sb("dstb", [D, CE + 1], I32), a.sb("same", [D, CE])
        pX, pM, pR = (a.ps(n, [128, 512]) for n in ("pX", "pM", "pR"))
        s_w, s_go, s_ring, s_ga, s_dstb, s_st, s_init, s_tA, s_xs, s_psM, s_mask, s_S, s_psR, s_y = (
            a.sem(n) for n in ("weights", "go", "ring", "ga", "dstb", "stored", "init", "tA", "xs", "psM", "mask", "S", "psR", "y"))
        block = ctx.enter_context(nc.Block())

        @block.sync
        def _(sp):
            if weight:
                sp.dma_start(W[:], g[weight]).then_inc(s_w, 16)

            def load_masks(e0):
                sp.dma_start(dstb[:], g["dst_pad"][:, bass.ds(e0, CE + 1)].broadcast_to([D, CE + 1])).then_inc(s_dstb, 16)

            def store(c):
                sp.wait_ge(s_y, c + 1)
                sp.dma_start(rows_of(out, CE * c, CT), y[:]).then_inc(s_st, 16)

            load_masks(0)
            @steps(sp, NC - 1)
            def _(c):
                sp.wait_ge(s_mask, c + 1)
                load_masks(CE * c + CE)
                store(c)
            store(NC - 1)
            sp.wait_ge(s_init, 1)
            sp.dma_start(out[E:E + 1, :], zrow[:]).then_inc(s_st, 16)
            sp.wait_ge(s_st, 16 * (NC + 1))

        @block.gpsimd
        def _(pool):
            @steps(pool, NC)
            def _(c):
                pool.wait_ge(s_tA, c)
                pool.sem_inc(s_go, 1)
                gathers(pool, s_go, s_ring, s_ga, ring, index, c, c + 1, table, ga)

        @block.tensor
        def _(pe):
            if weight:
                pe.wait_ge(s_w, 16)
            @steps(pe, NC)
            def _(c):
                pe.wait_ge(s_ga, 64 * (c + 1))
                if not weight:
                    pe.wait_ge(s_S, c)
                for k in range(CT):
                    last = nc.tensor.transpose(pX[:, k * TP:(k + 1) * TP], ga[:, k, :], K["ident"][0:TP, 0:TP])
                last.then_inc(s_tA, 1)
                if weight:
                    pe.wait_ge(s_xs, c + 1)
                    nc.tensor.matmul(pM[:, 0:CE], W[:], xs[:], start=True, stop=True).then_inc(s_psM, 1)
                pe.wait_ge(s_S, c + 1)
                pe.wait_ge(s_y, c)
                for k in range(CT):
                    last = nc.tensor.transpose(pR[0:TP, k * D:(k + 1) * D], S[:, k * TP:(k + 1) * TP], K["ident"][:])
                last.then_inc(s_psR, 1)

        @block.scalar
        def _(act):
            if weight:
                @steps(act, NC)
                def _(c):
                    act.wait_ge(s_tA, c + 1)
                    act.wait_ge(s_psM, c)
                    nc.scalar.activation(xs[:], pX[:, 0:CE], ACT.Copy).then_inc(s_xs, 1)

        @block.vector
        def _(dve):
            nc.vector.memset(carry[:], 0.0)
            nc.vector.memset(zrow[:], 0.0).then_inc(s_init, 1)
            dve.wait_ge(s_init, 1)
            @steps(dve, NC)
            def _(c):
                dve.wait_ge(s_dstb, 16 * (c + 1))
                nc.vector.tensor_tensor(same[:], dstb[:, 1:CE + 1], dstb[:, 0:CE], ALU.is_equal).then_inc(s_mask, 1)
                dve.wait_ge(s_mask, c + 1)
                dve.wait_ge(s_psR, c)
                if weight:
                    dve.wait_ge(s_psM, c + 1)
                else:
                    dve.wait_ge(s_tA, c + 1)
                nc.vector.tensor_tensor_scan(S[:], same[:], (pM if weight else pX)[:, 0:CE], carry[:], ALU.mult, ALU.add).then_inc(s_S, 1)
                dve.wait_ge(s_S, c + 1)
                nc.vector.tensor_copy(carry[:], S[:, CE - 1:CE])
                dve.wait_ge(s_psR, c + 1)
                dve.wait_ge(s_st, 16 * c)
                for k in range(CT):
                    last = nc.vector.tensor_scalar(y[:, k, :], pR[0:TP, k * D:(k + 1) * D], K["rdegH"][:, bass.ds(CT * c + k, 1)], None, ALU.mult)
                last.then_inc(s_y, 1)
                dve.wait_ge(s_y, c + 1)


def node_phase(nc, g, K, T, H):
    with ExitStack() as ctx:
        a = Place(nc, ctx, "nd")
        ring = a.sb("ring", [TP, CT], I32)
        ga = a.sb("ga", [TP, CT, D])
        S, De, pos, sf, rc, di = (a.sb(n, [D, CE]) for n in ("S", "De", "pos", "sf", "rc", "di"))
        cS, cD = a.sb("cS", [D, 1]), a.sb("cD", [D, 1])
        srcb, same, hw = a.sb("srcb", [D, CE + 2]), a.sb("same", [D, CE]), a.sb("hw", [D, CE])
        junk = a.sb("junk", [D, CE])
        acc = a.sb("acc", [D, 2])
        pX = a.ps("pX", [128, 512])
        s_go, s_ring, s_ga, s_srcb, s_hw, s_init, s_tA, s_mask, s_S, s_D, s_ch, s_end = (
            a.sem(n) for n in ("go", "ring", "ga", "srcb", "hw", "init", "tA", "mask", "S", "D", "chain", "end"))
        block = ctx.enter_context(nc.Block())

        @block.sync
        def _(sp):
            def load_masks(e0):
                sp.dma_start(srcb[:], T["srow"][:, bass.ds(e0, CE + 2)].broadcast_to([D, CE + 2])).then_inc(s_srcb, 16)

            def load_weights(e0):
                sp.dma_start(hw[:], T["hrow"][:, bass.ds(e0, CE)].broadcast_to([D, CE])).then_inc(s_hw, 16)

            load_masks(0)
            load_weights(0)
            @steps(sp, NC - 1)
            def _(c):
                sp.wait_ge(s_end, c + 1)
                load_masks(CE * c + CE)
                sp.wait_ge(s_D, c + 1)
                load_weights(CE * c + CE)

        @block.gpsimd
        def _(pool):
            @steps(pool, NC)
            def _(c):
                pool.wait_ge(s_tA, c)
                pool.sem_inc(s_go, 1)
                gathers(pool, s_go, s_ring, s_ga, ring, K["s_idxE"], c, c + 1, T["TE"], ga)

        @block.tensor
        def _(pe):
            @steps(pe, NC)
            def _(c):
                pe.wait_ge(s_ga, 64 * (c + 1))
                pe.wait_ge(s_S, c)
                for k in range(CT):
                    last = nc.tensor.transpose(pX[:, k * TP:(k + 1) * TP], ga[:, k, :], K["ident"][0:TP, 0:TP])
                last.then_inc(s_tA, 1)

        @block.vector
        def _(dve):
            nc.vector.memset(H["sum"][:], 0.0)
            nc.vector.memset(cD[:], 0.0)
            nc.vector.memset(cS[:], 0.0).then_inc(s_init, 1)
            dve.wait_ge(s_init, 1)
            @steps(dve, NC)
            def _(c):
                link = Chain(dve, s_ch, c, 8)
                dve.wait_ge(s_srcb, 16 * (c + 1))
                nc.vector.tensor_tensor(same[:], srcb[:, 1:CE + 1], srcb[:, 0:CE], ALU.is_equal).then_inc(s_mask, 1)
                nc.vector.tensor_tensor(H["end"][:, bass.ds(CE * c, CE)], srcb[:, 2:CE + 2], srcb[:, 1:CE + 1], ALU.not_equal).then_inc(s_end, 1)
                dve.wait_ge(s_mask, c + 1)
                dve.wait_ge(s_hw, 16 * (c + 1))
                nc.vector.tensor_tensor_scan(De[:], same[:], hw[:], cD[:], ALU.mult, ALU.add).then_inc(s_D, 1)
                dve.wait_ge(s_tA, c + 1)
                nc.vector.tensor_tensor_scan(S[:], same[:], pX[:, 0:CE], cS[:], ALU.mult, ALU.add).then_inc(s_S, 1)
                dve.wait_ge(s_D, c + 1)
                nc.vector.tensor_scalar(pos[:], De[:], 0.0, None, ALU.is_gt)
                link(nc.vector.tensor_scalar(sf[:], De[:], 1.2e-38, None, ALU.max))
                nc.vector.tensor_copy(cD[:], De[:, CE - 1:CE])
                link(nc.vector.reciprocal(rc[:], sf[:]))
                link(nc.vector.tensor_tensor(di[:], rc[:], pos[:], ALU.mult))
                nc.vector.tensor_copy(H["dinv"][:, bass.ds(CE * c, CE)], di[:])
                dve.wait_ge(s_S, c + 1)
                nc.vector.tensor_copy(cS[:], S[:, CE - 1:CE])
                link(nc.vector.tensor_tensor(H["h"][:, bass.ds(CE * c, CE)], S[:], di[:], ALU.mult))
                link(nc.vector.tensor_scalar(H["h"][:, bass.ds(CE * c, CE)], H["h"][:, bass.ds(CE * c, CE)], K["cols"][:, 5:6], None, ALU.add))
                dve.wait_ge(s_end, c + 1)
                link(nc.vector.scalar_tensor_tensor(out=junk[:], in0=H["h"][:, bass.ds(CE * c, CE)], scalar=1.0, in1=H["end"][:, bass.ds(CE * c, CE)],
                                                    op0=ALU.mult, op1=ALU.mult, accum_out=acc[:, 0:1]))
                link(nc.vector.tensor_scalar(junk[:], H["end"][:, bass.ds(CE * c, CE)], 1.0, 0.0, ALU.mult, ALU.add, accum_out=acc[:, 1:2]))
                link(nc.vector.tensor_tensor(H["sum"][:], H["sum"][:], acc[:], ALU.add))
                link.done()


def batchnorm_phase(nc, g, K, T, H):
    with ExitStack() as ctx:
        a = Place(nc, ctx, "bn")
        W = a.sb("W", [D, D])
        v = a.sb("v", [D, 12])
        eps = a.sb("eps", [128, 1])
        dif, junk, hp, oF = (a.sb(n, [D, CE]) for n in ("dif", "junk", "hp", "oF"))
        y = a.sb("y", [TP, CT, D])
        pM, pR = a.ps("pM", [128, 512]), a.ps("pR", [128, 512])
        s_w, s_st, s_ch, s_dif, s_sq, s_a, s_sd, s_hp, s_psM, s_oF, s_psR, s_y, s_acc = (
            a.sem(n) for n in ("weights", "stored", "chain", "dif", "sq", "affine", "sd", "hp", "psM", "oF", "psR", "y", "acc"))
        block = ctx.enter_context(nc.Block())
        b1, gam, bet = K["cols"][:, 5:6], K["cols"][:, 6:7], K["cols"][:, 7:8]
        rest, mu, s2, part, t, var, sd, rs, scale, bias = (v[:, i:i + 1] for i in range(10))

        @block.sync
        def _(sp):
            sp.dma_start(W[:], g["W2"]).then_inc(s_w, 16)
            @steps(sp, NC)
            def _(c):
                sp.wait_ge(s_y, c + 1)
                sp.dma_start(rows_of(T["TH"], CE * c, CT), y[:]).then_inc(s_st, 16)
            sp.wait_ge(s_st, 16 * NC)

        @block.vector
        def _(dve):
            link = Chain(dve, s_ch)
            nc.vector.memset(eps[:], EPS)
            link(nc.vector.tensor_scalar(rest, H["sum"][:, 1:2], -1.0, float(N), ALU.mult, ALU.add))
            link(nc.vector.scalar_tensor_tensor(out=t, in0=rest, scalar=b1, in1=H["sum"][:, 0:1], op0=ALU.mult, op1=ALU.add))
            link(nc.vector.tensor_scalar(mu, t, 1.0 / N, None, ALU.mult))
            link(nc.vector.tensor_scalar(t, b1, mu, None, ALU.subtract))
            link(nc.vector.tensor_tensor(t, t, t, ALU.mult))
            link(nc.vector.tensor_tensor(s2, t, rest, ALU.mult))
            @steps(dve, NC)
            def _(c):
                dve.wait_ge(s_sq, c)
                nc.vector.scalar_tensor_tensor(out=dif[:], in0=H["h"][:, bass.ds(CE * c, CE)], scalar=mu, in1=H["end"][:, bass.ds(CE * c, CE)],
                                               op0=ALU.subtract, op1=ALU.mult).then_inc(s_dif, 1)
                dve.wait_ge(s_sq, c + 1)
                nc.vector.tensor_tensor(s2, s2, part, ALU.add).then_inc(s_acc, 1)
                dve.wait_ge(s_acc, c + 1)
            nc.vector.tensor_scalar(var, s2, 1.0 / N, None, ALU.mult).then_inc(s_a, 1)
            dve.wait_ge(s_sd, 1)
            link(nc.vector.reciprocal(rs, sd))
            link(nc.vector.tensor_tensor(scale, rs, gam, ALU.mult))
            link(nc.vector.tensor_tensor(t, mu, scale, ALU.mult))
            nc.vector.tensor_tensor(bias, bet, t, ALU.subtract).then_inc(s_a, 1)
            @steps(dve, NC)
            def _(c):
                dve.wait_ge(s_psR, c + 1)
                dve.wait_ge(s_st, 16 * c)
                nc.vector.tensor_copy(y[:], pR[0:TP, :].rearrange("p (k f) -> p k f", k=CT)).then_inc(s_y, 1)

        @block.scalar
        def _(act):
            @steps(act, NC)
            def _(c):
                act.wait_ge(s_dif, c + 1)
                act.wait_ge(s_acc, c)
                nc.scalar.activation(junk[:], dif[:], ACT.Square, accum_out=part).then_inc(s_sq, 1)
            act.wait_ge(s_a, 1)
            nc.scalar.activation(sd, var, ACT.Sqrt, bias=eps[:]).then_inc(s_sd, 1)
            act.wait_ge(s_a, 2)
            @steps(act, NC)
            def _(c):
                act.wait_ge(s_psM, c)
                nc.scalar.activation(hp[:], H["h"][:, bass.ds(CE * c, CE)], ACT.Identity, bias=bias, scale=scale).then_inc(s_hp, 1)
                act.wait_ge(s_psM, c + 1)
                act.wait_ge(s_psR, c)
                nc.scalar.activation(oF[:], pM[:, 0:CE], ACT.Copy).then_inc(s_oF, 1)

        @block.tensor
        def _(pe):
            pe.wait_ge(s_w, 16)
            @steps(pe, NC)
            def _(c):
                pe.wait_ge(s_hp, c + 1)
                nc.tensor.matmul(pM[:, 0:CE], W[:], hp[:], start=True, stop=True).then_inc(s_psM, 1)
                pe.wait_ge(s_oF, c + 1)
                pe.wait_ge(s_y, c)
                for k in range(CT):
                    last = nc.tensor.transpose(pR[0:TP, k * D:(k + 1) * D], oF[:, k * TP:(k + 1) * TP], K["ident"][:])
                last.then_inc(s_psR, 1)


def result_phase(nc, g, K, T, H):
    with ExitStack() as ctx:
        a = Place(nc, ctx, "rs")
        eps = a.sb("eps", [128, 1])
        ring, rinx, rout = a.sb("ring", [TP, CT], I32), a.sb("rinx", [TP, CT], I32), a.sb("rout", [TP, CT], I32)
        ga, gb = a.sb("ga", [TP, CT, D]), a.sb("gb", [TP, CT, D])
        z, y = a.sb("z", [TP, CT, D]), a.sb("y", [TP, CT, D])
        S, o, oF = (a.sb(n, [D, CE]) for n in ("S", "o", "oF"))
        cS = a.sb("cS", [D, 1])
        srcb, same = a.sb("srcb", [D, CE + 1]), a.sb("same", [D, CE])
        st, mv, sd, rs = a.sb("st", [TP, CT, 6]), a.sb("mv", [TP, CT, 2]), a.sb("sd", [TP, CT]), a.sb("rs", [TP, CT])
        pX, pR = a.ps("pX", [128, 512]), a.ps("pR", [128, 512])
        (s_go, s_ring, s_ga, s_gb, s_srcb, s_init, s_eps, s_tA, s_mask, s_S, s_o, s_oF, s_psR, s_z, s_d, s_dgo, s_mv, s_sd, s_y, s_ch,
         s_out) = (a.sem(n) for n in ("go", "ring", "ga", "gb", "srcb", "init", "eps", "tA", "mask", "S", "o", "oF", "psR", "z",
                                      "stats", "dve_go", "mv", "sd", "y", "chain", "out"))
        block = ctx.enter_context(nc.Block())

        @block.sync
        def _(sp):
            def load_masks(e0):
                sp.dma_start(srcb[:], T["srow"][:, bass.ds(e0, CE + 1)].broadcast_to([D, CE + 1])).then_inc(s_srcb, 16)

            load_masks(0)
            @steps(sp, NC - 1)
            def _(c):
                sp.wait_ge(s_mask, c + 1)
                load_masks(CE * c + CE)

        @block.gpsimd
        def _(pool):
            nc.gpsimd.memset(eps[:], EPS).then_inc(s_eps, 1)

            def load(c):
                gathers(pool, s_go, s_ring, s_ga, ring, K["s_idxE"], c, 3 * c + 1, T["TE2"], ga)
                gathers(pool, s_go, s_ring, s_gb, rinx, K["s_idxS"], c, 3 * c + 2, T["T3"], gb)

            def scatter(c):
                nc.gpsimd.tensor_copy(rout[:], K["src_end"][:, bass.ds(CT * c, CT)]).then_inc(s_ring, 1)
                pool.wait_ge(s_ring, 3 * c + 3)
                pool.wait_ge(s_y, c + 1)
                pool.sem_inc(s_go, 1)
                for k in range(CT):
                    nc.gpsimd.indirect_dma_start(out=T["out"], out_offset=bass.IndirectOffsetOnAxis(ap=rout[:, k:k + 1], axis=0),
                                                 in_=y[:, k, :], in_offset=None, bounds_check=N - 1, oob_is_err=False).then_inc(s_out, 16)

            @steps(pool, NC)
            def _(c):
                pool.wait_ge(s_tA, c)
                pool.wait_ge(s_z, c)
                pool.wait_ge(s_out, 64 * c)
                pool.sem_inc(s_go, 1)
                load(c)
                scatter(c)
            pool.wait_ge(s_out, 64 * NC)

        @block.tensor
        def _(pe):
            @steps(pe, NC)
            def _(c):
                pe.wait_ge(s_ga, 64 * (c + 1))
                for k in range(CT):
                    last = nc.tensor.transpose(pX[:, k * TP:(k + 1) * TP], ga[:, k, :], K["ident"][0:TP, 0:TP])
                last.then_inc(s_tA, 1)
                pe.wait_ge(s_oF, c + 1)
                for k in range(CT):
                    last = nc.tensor.transpose(pR[0:TP, k * D:(k + 1) * D], oF[:, k * TP:(k + 1) * TP], K["ident"][:])
                last.then_inc(s_psR, 1)

        @block.scalar
        def _(act):
            act.wait_ge(s_eps, 1)
            @steps(act, NC)
            def _(c):
                act.wait_ge(s_o, c + 1)
                act.wait_ge(s_psR, c)
                nc.scalar.activation(oF[:], o[:], ACT.Identity, bias=K["cols"][:, 8:9]).then_inc(s_oF, 1)
                act.wait_ge(s_mv, c + 1)
                nc.scalar.activation(sd[:], mv[:, :, 1], ACT.Sqrt, bias=eps[0:TP, :]).then_inc(s_sd, 1)

        @block.vector
        def _(dve):
            nc.vector.memset(cS[:], 0.0).then_inc(s_init, 1)
            dve.wait_ge(s_init, 1)
            @steps(dve, NC)
            def _(c):
                link = Chain(dve, s_ch, c, 1)
                dve.wait_ge(s_srcb, 16 * (c + 1))
                nc.vector.tensor_tensor(same[:], srcb[:, 1:CE + 1], srcb[:, 0:CE], ALU.is_equal).then_inc(s_mask, 1)
                dve.wait_ge(s_mask, c + 1)
                dve.wait_ge(s_tA, c + 1)
                nc.vector.tensor_tensor_scan(S[:], same[:], pX[:, 0:CE], cS[:], ALU.mult, ALU.add).then_inc(s_S, 1)
                dve.wait_ge(s_S, c + 1)
                dve.wait_ge(s_oF, c)
                nc.vector.tensor_copy(cS[:], S[:, CE - 1:CE])
                nc.vector.tensor_tensor(o[:], S[:], H["dinv"][:, bass.ds(CE * c, CE)], ALU.mult).then_inc(s_o, 1)
                dve.wait_ge(s_gb, 64 * (c + 1))
                dve.wait_ge(s_psR, c + 1)
                nc.vector.tensor_tensor(z[:], gb[:], pR[0:TP, :].rearrange("p (k f) -> p k f", k=CT), ALU.add).then_inc(s_z, 1)
                dve.wait_ge(s_z, c + 1)
                row_stats(nc, z, CT, st, mv, s_d)
                dve.wait_ge(s_d, c + 1)
                dve.sem_inc(s_dgo, 1)
                row_aggr(nc, CT, st, mv).then_inc(s_mv, 1)
                dve.wait_ge(s_sd, c + 1)
                link(nc.vector.reciprocal(rs[:], sd[:]))
                dve.wait_ge(s_out, 64 * c)
                normalize(nc, y, z, CT, mv, rs).then_inc(s_y, 1)
                dve.wait_ge(s_y, c + 1)
                link.done()


def target_rows_phase(nc, g, K, T):
    with ExitStack() as ctx:
        a = Place(nc, ctx, "tr")
        eps, b2 = a.sb("eps", [128, 1]), a.sb("b2", [TP, D])
        rout = a.sb("rout", [TP, CT], I32)
        x, z, y = (a.sb(n, [TP, CT, D]) for n in ("x", "z", "y"))
        st, mv, sd, rs = a.sb("st", [TP, CT, 6]), a.sb("mv", [TP, CT, 2]), a.sb("sd", [TP, CT]), a.sb("rs", [TP, CT])
        s_w, s_x, s_go, s_ring, s_eps, s_z, s_d, s_dgo, s_mv, s_sd, s_y, s_ch, s_out = (
            a.sem(n) for n in ("weights", "x", "go", "ring", "eps", "z", "stats", "dve_go", "mv", "sd", "y", "chain", "out"))
        block = ctx.enter_context(nc.Block())

        @block.sync
        def _(sp):
            sp.dma_start(b2[:], g["rowv"][4:5, :].broadcast_to([TP, D])).then_inc(s_w, 16)
            @steps(sp, NC)
            def _(c):
                sp.wait_ge(s_z, c)
                sp.dma_start(x[:], rows_of(T["T3"], CE * c, CT)).then_inc(s_x, 16)

        @block.gpsimd
        def _(pool):
            nc.gpsimd.memset(eps[:], EPS).then_inc(s_eps, 1)
            @steps(pool, NC)
            def _(c):
                pool.wait_ge(s_out, 64 * c)
                pool.sem_inc(s_go, 1)
                nc.gpsimd.tensor_copy(rout[:], K["dst_end"][:, bass.ds(CT * c, CT)]).then_inc(s_ring, 1)
                pool.wait_ge(s_ring, c + 1)
                pool.wait_ge(s_y, c + 1)
                pool.sem_inc(s_go, 1)
                for k in range(CT):
                    nc.gpsimd.indirect_dma_start(out=T["out"], out_offset=bass.IndirectOffsetOnAxis(ap=rout[:, k:k + 1], axis=0),
                                                 in_=y[:, k, :], in_offset=None, bounds_check=N - 1, oob_is_err=False).then_inc(s_out, 16)
            pool.wait_ge(s_out, 64 * NC)

        @block.scalar
        def _(act):
            act.wait_ge(s_eps, 1)
            @steps(act, NC)
            def _(c):
                act.wait_ge(s_mv, c + 1)
                nc.scalar.activation(sd[:], mv[:, :, 1], ACT.Sqrt, bias=eps[0:TP, :]).then_inc(s_sd, 1)

        @block.vector
        def _(dve):
            dve.wait_ge(s_w, 16)
            @steps(dve, NC)
            def _(c):
                link = Chain(dve, s_ch, c, 1)
                dve.wait_ge(s_x, 16 * (c + 1))
                nc.vector.tensor_tensor(z[:], x[:], bc(b2, CT), ALU.add).then_inc(s_z, 1)
                dve.wait_ge(s_z, c + 1)
                row_stats(nc, z, CT, st, mv, s_d)
                dve.wait_ge(s_d, c + 1)
                dve.sem_inc(s_dgo, 1)
                row_aggr(nc, CT, st, mv).then_inc(s_mv, 1)
                dve.wait_ge(s_sd, c + 1)
                link(nc.vector.reciprocal(rs[:], sd[:]))
                dve.wait_ge(s_out, 64 * c)
                normalize(nc, y, z, CT, mv, rs).then_inc(s_y, 1)
                dve.wait_ge(s_y, c + 1)
                link.done()


DR = 10
DP = N // 128
DS = DP // DR
DL = N - 128 * DP


def dense_phase(nc, g, K, T):
    with ExitStack() as ctx:
        a = Place(nc, ctx, "dn")
        eps = a.sb("eps", [128, 1])
        bo, ub, lg, lb, b2 = (a.sb(n, [128, D]) for n in ("bo", "ub", "lg", "lb", "b2"))
        x = a.sb("x", [128, 2, DR, D])
        z, h, n1, y = (a.sb(n, [128, DR, D]) for n in ("z", "h", "n1", "y"))
        out = a.sb("out", [128, 2, DR, D])
        st, mv, sd, rs = a.sb("st", [128, DR, 6]), a.sb("mv", [128, DR, 2]), a.sb("sd", [128, DR]), a.sb("rs", [128, DR])
        s_w, s_eps, s_mv, s_sd, s_ch, s_d, s_dgo, s_z = (a.sem(n) for n in ("weights", "eps", "mv", "sd", "chain", "stats", "dve_go", "z"))
        R2 = a.sb("rs2", [128, DR])
        s_x, s_st = [a.sem(f"x{k}") for k in range(2)], [a.sem(f"stored{k}") for k in range(2)]
        s_y = a.sem("y")
        block = ctx.enter_context(nc.Block())
        xv = g["x"][0:128 * DP, :].rearrange("(p r) f -> p r f", p=128)
        ov = T["out"][0:128 * DP, :].rearrange("(p r) f -> p r f", p=128)
        total = DS + 1
        assert DS % 2 == 1 and DP == DS * DR and DL > 0

        def left(t):
            return t[128 * DP:N, :].rearrange("p (r f) -> p r f", r=1)

        @block.sync
        def _(sp):
            for t, r in ((bo, 0), (ub, 1), (lg, 2), (lb, 3), (b2, 4)):
                sp.dma_start(t[:], g["rowv"][r:r + 1, :].broadcast_to([128, D])).then_inc(s_w, 16)

            def load(i, k):
                sp.dma_start(x[:, k], xv[:, bass.ds((2 * i + k) * DR, DR), :]).then_inc(s_x[k], 16)

            def store(i, k):
                sp.wait_ge(s_y, 2 * i + k + 1)
                sp.dma_start(ov[:, bass.ds((2 * i + k) * DR, DR), :], out[:, k]).then_inc(s_st[k], 16)

            load(0, 0)
            @steps(sp, DS // 2)
            def _(i):
                sp.wait_ge(s_z, 2 * i)
                load(i, 1)
                store(i, 0)
                sp.wait_ge(s_z, 2 * i + 1)
                load(i + 1, 0)
                store(i, 1)
            sp.wait_ge(s_z, DS - 1)
            sp.dma_start(x[0:DL, 1, 0:1, :], left(g["x"])).then_inc(s_x[1], 16)
            store(DS // 2, 0)
            sp.wait_ge(s_y, total)
            sp.dma_start(left(T["out"]), out[0:DL, 1, 0:1, :]).then_inc(s_st[1], 16)
            for k in range(2):
                sp.wait_ge(s_st[k], 16 * (total // 2))

        @block.scalar
        def _(act):
            act.wait_ge(s_eps, 1)
            @steps(act, 5 * DS)
            def _(j):
                act.wait_ge(s_mv, j + 1)
                nc.scalar.activation(sd[:], mv[:, :, 1], ACT.Sqrt, bias=eps[:]).then_inc(s_sd, 1)
            with act.Fori(5 * DS, 5 * DS + 5) as j:
                act.wait_ge(s_mv, j + 1)
                nc.scalar.activation(sd[0:DL, 0:1], mv[0:DL, 0:1, 1], ACT.Sqrt, bias=eps[0:DL, :]).then_inc(s_sd, 1)

        LINKS = 15

        @block.vector
        def _(dve):
            nc.vector.memset(eps[:], EPS).then_inc(s_eps, 1)
            dve.wait_ge(s_w, 80)

            def step(t, k, p, rows):
                link = Chain(dve, s_ch, t, LINKS)
                Z, Hh, N1, Y, X, O = z[0:p, 0:rows], h[0:p, 0:rows], n1[0:p, 0:rows], y[0:p, 0:rows], x[0:p, k, 0:rows], out[0:p, k, 0:rows]
                S, MV, SD, RS = st[0:p], mv[0:p], sd[0:p, 0:rows], rs[0:p, 0:rows]

                def stats(src, j):
                    row_stats(nc, src, rows, S, MV, s_d)
                    dve.wait_ge(s_d, 4 * t + min(j, 3) + 1)
                    dve.sem_inc(s_dgo, 1)
                    row_aggr(nc, rows, S, MV).then_inc(s_mv, 1)
                    dve.wait_ge(s_sd, 5 * t + j + 1)
                    link(nc.vector.reciprocal(RS, SD))

                nc.vector.tensor_tensor(Z, X, bc(bo[0:p], rows), ALU.add).then_inc(s_z, 1)
                dve.wait_ge(s_z, t + 1)
                stats(Z, 0)
                link(normalize(nc, N1, Z, rows, MV, RS))
                link(nc.vector.tensor_tensor(Hh, N1, bc(ub[0:p], rows), ALU.add))
                stats(Hh, 1)
                link(normalize(nc, Z, Hh, rows, MV, RS))
                link(nc.vector.tensor_tensor(Hh, Z, bc(lg[0:p], rows), ALU.mult))
                link(nc.vector.tensor_tensor(Z, Hh, bc(lb[0:p], rows), ALU.add))
                link(nc.vector.tensor_tensor(Y, Z, N1, ALU.add))
                stats(Y, 2)
                nc.vector.tensor_copy(R2[0:p, 0:rows], RS)
                link(nc.vector.tensor_tensor(SD, RS, RS, ALU.mult))
                nc.vector.tensor_tensor(MV[:, 0:rows, 1], MV[:, 0:rows, 1], SD, ALU.mult).then_inc(s_mv, 1)
                dve.wait_ge(s_sd, 5 * t + 4)
                link(nc.vector.reciprocal(RS, SD))
                link(nc.vector.tensor_tensor(RS, RS, R2[0:p, 0:rows], ALU.mult))
                link(normalize(nc, Z, Y, rows, MV, RS))
                link(nc.vector.tensor_tensor(Hh, Z, bc(b2[0:p], rows), ALU.add))
                stats(Hh, 4)
                return O, Hh, MV, RS, rows, link

            def finish(O, Hh, MV, RS, rows, link, t):
                normalize(nc, O, Hh, rows, MV, RS).then_inc(s_y, 1)
                dve.wait_ge(s_y, t + 1)
                link.done()

            @steps(dve, DS // 2)
            def _(i):
                for k in range(2):
                    t = 2 * i + k
                    dve.wait_ge(s_x[k], 16 * (i + 1))
                    dve.wait_ge(s_st[k], 16 * i)
                    finish(*step(t, k, 128, DR), t)
            for t, k, p, rows in ((DS - 1, 0, 128, DR), (DS, 1, DL, 1)):
                dve.wait_ge(s_x[k], 16 * (DS // 2 + 1))
                dve.wait_ge(s_st[k], 16 * (DS // 2))
                finish(*step(t, k, p, rows), t)


def source_state(nc, ctx):
    def sb(name, shape, dt=F32):
        return ctx.enter_context(nc.sbuf_tensor(f"src_{name}", shape, dt))

    return {"h": sb("h", [D, E]), "dinv": sb("dinv", [D, E]), "end": sb("end", [D, E], BF16), "sum": sb("sum", [D, 2])}


def layout(I):
    import numpy as np
    c = lambda v: np.ascontiguousarray(v)
    col = lambda v: c(v.reshape(NT, TP).T)
    src, dst = np.asarray(I["src"]), np.asarray(I["dst"])
    w = {k: np.asarray(v) for k, v in I.items()}
    end = np.full(1, -1, dst.dtype)
    f = np.float32
    U = 32
    A = np.zeros((D, D), f)
    B = np.zeros((D, D), f)
    A[0:U, 0:U] = w["L2_gnn_w_lin1_s"]
    for i in range(3):
        A[U + i:D:3, U * (i + 1):U * (i + 2)] = w["L2_gnn_w_lin1_v"]
        B[0:U, U * (i + 1):U * (i + 2)] = w["L2_gnn_w_lin1_s"]
    fc = w["L2_gnn_fc_w2"].reshape(64, 4, U)
    zero = np.zeros((64, U), f)
    fa = np.concatenate([fc[:, 0], fc[:, 2], fc[:, 2], fc[:, 2]], 1)
    fb = np.concatenate([zero, fc[:, 1], fc[:, 1], fc[:, 1]], 1)
    fcc = np.concatenate([zero, fc[:, 3], fc[:, 3], fc[:, 3]], 1)
    oA, oB, oC = (np.zeros((D, D), f) for _ in range(3))
    oA[0:U, 0:U] = w["L2_gnn_w_lin2_s"][0:U]
    for i in range(3):
        r = slice(U * (i + 1), U * (i + 2))
        oA[r, U + i:D:3] = w["L2_gnn_w_lin2_v"][U:2 * U]
        oB[r, U + i:D:3] = w["L2_gnn_w_lin2_v"][0:U]
        oC[r, 0:U] = w["L2_gnn_w_lin2_s"][U:2 * U]
    ptab = np.zeros((N, 2), f)
    ptab[:, 0] = E
    ptab[0:NH, 1] = w["L3_gnn_hyperedge_weight"]
    names = ("L0_gnn_bq", "L0_gnn_bk", "L0_gnn_bv", "L0_gnn_bo", "L1_gnn_msg_b", "L3_gnn_b1", "L3_gnn_gamma", "L3_gnn_beta", "L3_gnn_b2")
    rows = ("L0_gnn_bo", "L1_gnn_upd_b", "L1_gnn_ln_g", "L1_gnn_ln_b", "L3_gnn_b2")
    return dict(
        x=c(w["x"]), src_col=col(src), dst_col=col(dst), dstn_col=col(np.concatenate([dst[1:], end])),
        src_row=c(src[None]), dst_pad=c(np.concatenate([end, dst, end])[None]), type_row=c(w["edge_type_16"][None]),
        ea4T=c(w["edge_attr_4"].T), ea8T=c(w["edge_attr_8"].T), ptab0=ptab,
        tri=np.triu(np.ones((128, 128), f), 1), ident=np.eye(128, dtype=f), identb=np.eye(128, dtype=mybir.dt.np(BF16)),
        heads=(np.kron(np.eye(8), np.ones((16, 16))) * 0.25).astype(f), expand=np.kron(np.eye(8), np.ones((1, 16))).astype(f),
        cols=c(np.stack([w[n] for n in names], 1)), rowv=c(np.stack([w[n] for n in rows])),
        Wq=c(w["L0_gnn_Wq"]), Wk=c(w["L0_gnn_Wk"]), Wv=c(w["L0_gnn_Wv"]), Wo=c(w["L0_gnn_Wo"]),
        Wmx=c(w["L1_gnn_msg_W"][:, 0:D].T), Wme=c(w["L1_gnn_msg_W"][:, D:].T), embT=c(w["L1_gnn_edge_emb_W"].T), Wu=c(w["L1_gnn_upd_W"].T),
        L1A=A, L1B=B, fc1=c(w["L2_gnn_fc_w1"]), fcA=c(fa), fcB=c(fb), fcC=c(fcc), oA=oA, oB=oB, oC=oC,
        W1=c(w["L3_gnn_W1"].T), W2=c(w["L3_gnn_W2"].T),
    )


TABLES = dict(ptab=[N, 2], S4=[E, 4], srow=[1, E + 2], hrow=[1, E], T1=[2 * E, D], T2=[2 * E, D], T3=[2 * E, D],
              TE=[E + 1, D], TH=[E, D], TE2=[E + 1, D])


def program(nc, g, out):
    with ExitStack() as ctx:
        T = {n: nc.dram_tensor(f"table_{n}", tuple(s), F32).ap() for n, s in TABLES.items()}
        T["ptab1"] = T["ptab"].rearrange("a (b c) -> (a b) c", c=1)
        T["out"] = out
        K = constants(nc, ctx)
        index_phase(nc, g, K, T)
        attention_phase(nc, g, K, T)
        message_phase(nc, g, K, T)
        equivariant_phase(nc, g, K, T)
        dense_phase(nc, g, K, T)
        target_rows_phase(nc, g, K, T)
        hyperedge_phase(nc, g, K, T, "hA", T["T3"], K["idxS"], "W1", T["TE"])
        with ExitStack() as inner:
            H = source_state(nc, inner)
            node_phase(nc, g, K, T, H)
            batchnorm_phase(nc, g, K, T, H)
            hyperedge_phase(nc, g, K, T, "hB", T["TH"], K["send"], None, T["TE2"])
            result_phase(nc, g, K, T, H)


def kernel(**inputs):
    import concourse.bacc as bacc
    from concourse.bass_utils import run_bass_kernel_spmd

    nc = bacc.Bacc("TRN2", target_bir_lowering=False, num_devices=1)
    arrays = layout(inputs)
    g = {n: nc.dram_tensor(n, v.shape, mybir.dt.from_np(v.dtype), kind="ExternalInput").ap() for n, v in arrays.items()}
    out = nc.dram_tensor("result", (N, D), F32, kind="ExternalOutput").ap()
    program(nc, g, out)
    return run_bass_kernel_spmd(nc, [arrays], core_ids=[0]).results[0]["result"]
```

```python
from contextlib import ExitStack

import numpy as np
import concourse.bass as bass
from concourse import mybir

F32 = mybir.dt.float32
BF16 = mybir.dt.bfloat16
I32 = mybir.dt.int32
ALU = mybir.AluOpType
ACT = mybir.ActivationFunctionType
AX = mybir.AxisListType.X

N, D, E = 50000, 128, 12500
NH = 10000
TP = 125
NT = E // TP
CT = 4
CE = CT * TP
NC = E // CE
EPS = 1e-5
LO = (N + 127) // 128
FAR = 1 << 20
NEG = 1.0e30
SILU = 1.6791767923989418
RING = 4


class Chain:

    def __init__(self, eng, sem, i=0, per=0):
        self.eng, self.sem, self.base, self.per, self.n = eng, sem, i * per, per, 0

    def __call__(self, ins):
        self.n += 1
        ins.then_inc(self.sem, 1)
        self.eng.wait_ge(self.sem, self.base + self.n)

    def done(self):
        assert self.n == self.per, (self.n, self.per)


def steps(eng, n):
    def run(body):
        body(0)
        if n > 1:
            with eng.Fori(1, n) as i:
                body(i)
    return run


def chunks(eng, n=NC):
    def run(body):
        body(0, 0)
        pairs = (n - 3) // 2
        with eng.Fori(0, pairs) as u:
            body(u, 1)
            body(u, 2)
        for c in range(2 * pairs + 1, n):
            body(0, c)
    return run


class Place:

    def __init__(self, nc, ctx, tag):
        self.nc, self.ctx, self.tag, self.sems = nc, ctx, tag, []
        ctx.callback(self.clear)

    def sb(self, name, shape, dt=F32):
        return self.ctx.enter_context(self.nc.sbuf_tensor(f"{self.tag}_{name}", shape, dt))

    def ps(self, name, shape, dt=F32):
        return self.ctx.enter_context(self.nc.psum_tensor(f"{self.tag}_{name}", shape, dt))

    def sem(self, name):
        self.sems.append(self.nc.alloc_semaphore(f"{self.tag}_{name}"))
        return self.sems[-1]

    def clear(self):
        self.nc.clear_and_free_semaphores(self.sems)
        self.nc.all_engine_barrier()


def constants(nc, ctx):
    def sb(name, shape, dt=F32):
        return ctx.enter_context(nc.sbuf_tensor(f"k_{name}", shape, dt))

    K = {n: sb(n, s) for n, s in (("ident", [128, 128]), ("heads", [128, 128]), ("expand", [8, 128]), ("isH", [TP, NT]), ("rdeg", [TP, NT]), ("rdegH", [TP, NT]))}
    K["identb"] = sb("identb", [128, 128], BF16)
    K["iota_i"] = sb("iota_i", [128, LO], I32)
    K["cols"] = sb("cols", [D, 9])
    for n in ("dst_end", "clip", "slot", "send", "idxS", "s_idxE", "s_idxS", "src_end"):
        K[n] = sb(n, [TP, NT], I32)
    K["pay"] = sb("pay", [TP, NT, 4])
    return K


def rows_of(table, first, n):
    return table[bass.ds(first, n * TP), :].rearrange("(t p) f -> p t f", p=TP)


def index_phase(nc, g, K, T):
    with ExitStack() as ctx:
        a = Place(nc, ctx, "ix")
        src, dst, dstn = (a.sb(n, [TP, NT], I32) for n in ("src", "dst", "dstn"))
        srcf, dstf, dstnf, hif, lof, ef, tmp, endf = (
            a.sb(n, [TP, NT]) for n in ("srcf", "dstf", "dstnf", "hif", "lof", "ef", "tmp", "endf"))
        hii, loi, ei, scatI = (a.sb(n, [TP, NT], I32) for n in ("hii", "loi", "ei", "scatI"))
        iot = a.sb("iot", [TP, LO])
        tri, triL = a.sb("tri", [128, 128]), a.sb("triL", [TP, TP])
        ohi, olo = a.sb("ohi", [TP, RING, 128], BF16), a.sb("olo", [TP, RING, LO], BF16)
        zero = a.sb("zero", [TP, LO], BF16)
        hiT, hiTb = a.sb("hiT", [128, 2, TP]), a.sb("hiTb", [128, 2, TP], BF16)
        endh, endl = a.sb("endh", [128, LO], BF16), a.sb("endl", [128, LO], BF16)
        cnt, inc, end = a.sb("cnt", [128, LO]), a.sb("inc", [128, LO]), a.sb("end", [128, LO])
        cur = a.sb("cur", [128, 2, LO])
        ones, start = a.sb("ones", [128, LO]), a.sb("start", [128, LO])
        offs = a.sb("offs", [128, 1])
        junk = a.sb("junk", [TP, 2, 3, LO])
        srcb = a.sb("srcb", [TP, 2, RING * TP], I32)
        hit = a.sb("hit", [TP, 3, 2, RING])
        slotf, sendf = a.sb("slotf", [TP, NT]), a.sb("sendf", [TP, NT])
        ri, re, rj, pq = ([a.sb(f"{n}{p}", s, d) for p in range(2)]
                          for n, s, d in (("ri", [TP, CT], I32), ("re", [TP, CT], F32), ("rj", [TP, CT], I32), ("pq", [TP, CT, 2], F32)))
        posS, idxSf = a.sb("posS", [TP, NT]), a.sb("idxSf", [TP, NT])
        drow, drowP, rowD = a.sb("drow", [NT, TP], I32), a.sb("drowP", [NT, TP], I32), a.sb("rowD", [NT, TP])

        pC = a.ps("pC", [128, 512])
        pL, pE = (a.ps(n, [128, 2, 512]) for n in ("pL", "pE"))
        pT = a.ps("pT", [128, 2, 1024], BF16)
        pR = a.ps("pR", [128, 512])

        s_in, s_tab, s_cst, s_dv, s_pl, s_dsame, s_ds = (a.sem(n) for n in ("in", "tab", "cst", "dvchain", "plchain", "dsame", "dsame_stored"))
        s_ends_idx, s_ringA, s_ringB, s_pos = (a.sem(n) for n in ("ends_idx", "ringA", "ringB", "pos"))
        s_ohA, s_hist, s_hist_all, s_tot, s_off, s_first = (a.sem(n) for n in ("ohA", "hist", "hist_all", "tot", "off", "first"))
        s_acc, s_cur, s_ohB, s_tr, s_hiT, s_look, s_used, s_hit = (
            a.sem(n) for n in ("acc", "cur", "ohB", "transposed", "hiT", "looked", "lookup_used", "hit"))
        s_srcb, s_scat, s_gat = ([a.sem(f"{n}{p}") for p in range(2)] for n in ("srcb", "scat", "gat"))
        s_go = a.sem("go")
        block = ctx.enter_context(nc.Block())
        NR = NT // RING

        @block.sync
        def _(sp):
            for t, d in ((src, g["src_col"]), (dst, g["dst_col"]), (dstn, g["dstn_col"]),
                         (drow, g["dst_pad"][:, 1:E + 1].rearrange("a (t p) -> (a t) p", p=TP)),
                         (drowP, g["dst_pad"][:, 0:E].rearrange("a (t p) -> (a t) p", p=TP))):
                sp.dma_start(t[:], d).then_inc(s_in, 16)
            sp.dma_start(tri[:], g["tri"]).then_inc(s_in, 16)
            sp.dma_start(triL[:], g["tri"][0:TP, 0:TP]).then_inc(s_in, 16)
            for name in ("ident", "identb", "heads", "expand", "cols"):
                sp.dma_start(K[name][:], g[name]).then_inc(s_in, 16)
            sp.dma_start(T["ptab"].rearrange("(a b) c -> a (b c)", a=16), g["ptab0"].rearrange("(a b) c -> a (b c)", a=16)).then_inc(s_tab, 16)

            def load_sources(first, p):
                sp.dma_start(srcb[:, p, :], g["src_row"][:, bass.ds(first, RING * TP)].broadcast_to([TP, RING * TP])).then_inc(s_srcb[p], 16)

            load_sources(0, 0)
            load_sources(RING * TP, 1)
            sp.wait_ge(s_dsame, 1)
            sp.dma_start(T["dsame"].rearrange("a (t p) -> (a t) p", p=TP), rowD[:]).then_inc(s_ds, 16)
            @chunks(sp, NR - 2)
            def _(u, a):
                r = 2 * u + a
                sp.wait_ge(s_used, RING * r + RING)
                load_sources((r + 2) * (RING * TP), a % 2)
            sp.wait_ge(s_ds, 16)

        @block.gpsimd
        def _(pool):
            plink = Chain(pool, s_pl)
            nc.gpsimd.iota(ei[:], pattern=[[TP, NT]], base=0, channel_multiplier=1)
            plink(nc.gpsimd.iota(K["iota_i"][:], pattern=[[1, LO]], base=0, channel_multiplier=0))
            nc.gpsimd.tensor_copy(iot[:], K["iota_i"][0:TP, :])
            nc.gpsimd.tensor_copy(ef[:], ei[:])
            nc.gpsimd.memset(ones[:], 1.0)
            nc.gpsimd.memset(zero[:], 0.0).then_inc(s_cst, 1)
            pool.wait_ge(s_cst, 1)
            pool.wait_ge(s_tab, 16)
            pool.wait_ge(s_ends_idx, 1)
            @chunks(pool)
            def _(u, a):
                c, p = 2 * u + a, a % 2
                need(pool, s_scat[p], 64 * (u + a // 2))
                pool.sem_inc(s_go, 1)
                nc.gpsimd.tensor_copy(re[p][:], ef[:, bass.ds(CT * c, CT)])
                nc.gpsimd.tensor_copy(ri[p][:], scatI[:, bass.ds(CT * c, CT)]).then_inc(s_ringA, 1)
                pool.wait_ge(s_ringA, c + 1)
                pool.sem_inc(s_go, 1)
                for k in range(CT):
                    nc.gpsimd.indirect_dma_start(
                        out=T["ptab1"], out_offset=bass.IndirectOffsetOnAxis(ap=ri[p][:, k:k + 1], axis=0),
                        in_=re[p][:, k:k + 1], in_offset=None, bounds_check=2 * N - 1, oob_is_err=False).then_inc(s_scat[p], 16)
            for s in s_scat:
                pool.wait_ge(s, 64 * (NC // 2 + (s is s_scat[0])))

            def take(u, a):
                p = a % 2
                pool.wait_ge(s_gat[p], 64 * (u + a // 2 + 1))
                pool.sem_inc(s_go, 1)
                nc.gpsimd.tensor_copy(posS[:, bass.ds(CT * (2 * u + a), CT)], pq[p][:, :, 0]).then_inc(s_pos, 1)

            @chunks(pool)
            def _(u, a):
                c, p = 2 * u + a, a % 2
                need(pool, s_pos, c - 1)
                pool.sem_inc(s_go, 1)
                nc.gpsimd.tensor_copy(rj[p][:], src[:, bass.ds(CT * c, CT)]).then_inc(s_ringB, 1)
                pool.wait_ge(s_ringB, c + 1)
                pool.sem_inc(s_go, 1)
                for k in range(CT):
                    nc.gpsimd.indirect_dma_start(out=pq[p][:, k, :], out_offset=None, in_=T["ptab"],
                                                 in_offset=bass.IndirectOffsetOnAxis(ap=rj[p][:, k:k + 1], axis=0)).then_inc(s_gat[p], 16)
                if not (isinstance(c, int) and c == 0):
                    take(u, a - 1)
            take(0, NC - 1)

        @block.vector
        def _(dve):
            link = Chain(dve, s_dv)
            dve.wait_ge(s_in, 16 * 12)
            nc.vector.tensor_copy(srcf[:], src[:])
            nc.vector.tensor_copy(dstf[:], dst[:])
            nc.vector.tensor_copy(dstnf[:], dstn[:])
            nc.vector.tensor_tensor(rowD[:], drow[:], drowP[:], ALU.is_equal).then_inc(s_dsame, 1)
            nc.vector.tensor_scalar(hii[:], src[:], 127, None, ALU.bitwise_and)
            link(nc.vector.tensor_scalar(loi[:], src[:], 7, None, ALU.logical_shift_right))
            nc.vector.tensor_copy(hif[:], hii[:])
            nc.vector.tensor_copy(lof[:], loi[:])
            nc.vector.tensor_scalar(K["clip"][:], dstf[:], float(NH - 1), None, ALU.min)
            nc.vector.tensor_scalar(K["isH"][:], dstf[:], float(NH), None, ALU.is_lt)
            link(nc.vector.tensor_tensor(endf[:], dstf[:], dstnf[:], ALU.is_equal))
            nc.vector.tensor_scalar(endf[:], endf[:], float(FAR), None, ALU.mult)
            link(nc.vector.tensor_scalar(tmp[:], dstf[:], 2.0, None, ALU.mult))
            nc.vector.tensor_tensor(K["dst_end"][:], endf[:], dstf[:], ALU.add)
            nc.vector.tensor_tensor(scatI[:], endf[:], tmp[:], ALU.add).then_inc(s_ends_idx, 1)

            def one_hots(t, k, sem):
                nc.vector.tensor_scalar(ohi[:, k, :], iot[:, 0:128], hif[:, bass.ds(t, 1)], None, ALU.is_equal)
                nc.vector.tensor_scalar(olo[:, k, :], iot[:], lof[:, bass.ds(t, 1)], None, ALU.is_equal).then_inc(sem, 1)

            dve.wait_ge(s_cst, 1)
            @steps(dve, NR)
            def _(r):
                for k in range(RING):
                    need(dve, s_hist, RING * r + k - RING + 1)
                    one_hots(RING * r + k, k, s_ohA)
            dve.wait_ge(s_hist_all, 1)
            link(nc.vector.tensor_copy(cnt[:], pC[:, 0:LO]))
            nc.vector.tensor_tensor_scan(inc[:], ones[:], cnt[:], 0.0, ALU.mult, ALU.add).then_inc(s_tot, 1)
            dve.wait_ge(s_off, 1)
            link(nc.vector.tensor_copy(offs[:], pR[:, 0:1]))
            nc.vector.tensor_scalar(end[:], inc[:], offs[:], -1.0, ALU.add, ALU.add)
            link(nc.vector.tensor_scalar(start[:], inc[:], offs[:], None, ALU.add))
            link(nc.vector.tensor_copy(endh[:], end[:]))
            nc.vector.tensor_tensor(endl[:], end[:], endh[:], ALU.subtract)
            nc.vector.tensor_tensor(cur[:, 0, :], start[:], cnt[:], ALU.subtract).then_inc(s_first, 1)
            dve.wait_ge(s_first, 1)

            def rank(r, k, w):
                t = RING * r + k
                dve.wait_ge(s_look, t + 1)
                nc.vector.scalar_tensor_tensor(out=junk[:, k % 2, 0, 0:TP], in0=srcb[:, w, k * TP:(k + 1) * TP], scalar=srcf[:, bass.ds(t, 1)],
                                               in1=triL[:], op0=ALU.is_equal, op1=ALU.mult, accum_out=hit[:, 0, w, k:k + 1])
                nc.vector.scalar_tensor_tensor(out=junk[:, k % 2, 1, :], in0=pL[0:TP, k % 2, 0:LO], scalar=1.0, in1=olo[:, k, :],
                                               op0=ALU.mult, op1=ALU.mult, accum_out=hit[:, 1, w, k:k + 1])
                nc.vector.scalar_tensor_tensor(out=junk[:, k % 2, 2, :], in0=pE[0:TP, k % 2, 0:LO], scalar=1.0, in1=olo[:, k, :],
                                               op0=ALU.mult, op1=ALU.mult, accum_out=hit[:, 2, w, k:k + 1]).then_inc(s_used, 1)

            def keep(r, w):
                dve.wait_ge(s_used, RING * r + RING)
                nc.vector.tensor_tensor(slotf[:, bass.ds(RING * r, RING)], hit[:, 0, w, :], hit[:, 1, w, :], ALU.add)
                nc.vector.tensor_copy(sendf[:, bass.ds(RING * r, RING)], hit[:, 2, w, :]).then_inc(s_hit, 1)

            AHEAD = RING - 2
            for k in range(AHEAD):
                one_hots(k, k, s_ohB)

            @chunks(dve, NR)
            def _(u, a):
                r, w = 2 * u + a, a % 2
                dve.wait_ge(s_srcb[w], 16 * (u + a // 2 + 1))
                need(dve, s_hit, r - 1)
                for k in range(RING):
                    t = RING * r + k
                    if not (isinstance(t, int) and t < 2):
                        dve.wait_ge(s_look, t - 1)
                        dve.wait_ge(s_used, t - 1)
                    if not (isinstance(t, int) and t + AHEAD >= NT):
                        one_hots(t + AHEAD, (k + AHEAD) % RING, s_ohB)
                    dve.wait_ge(s_acc, t + 1)
                    if not (isinstance(t, int) and t < 1):
                        dve.wait_ge(s_look, t)
                        dve.wait_ge(s_cur, t)
                    nc.vector.tensor_tensor(cur[:, 1 - k % 2, :], cur[:, k % 2, :], pC[:, 0:LO], ALU.add).then_inc(s_cur, 1)
                    rank(r, k, w)
                keep(r, w)
            dve.wait_ge(s_hit, NR)
            dve.wait_ge(s_pos, NC)
            link(nc.vector.tensor_scalar(tmp[:], posS[:], float(E), None, ALU.is_equal))
            link(nc.vector.tensor_tensor(tmp[:], tmp[:], ef[:], ALU.mult))
            link(nc.vector.tensor_tensor(idxSf[:], posS[:], tmp[:], ALU.add))
            nc.vector.tensor_copy(K["slot"][:], slotf[:])
            nc.vector.tensor_copy(K["send"][:], sendf[:])
            nc.vector.tensor_copy(K["idxS"][:], idxSf[:])
            nc.vector.tensor_copy(K["pay"][:, :, 0], srcf[:])
            link(nc.vector.tensor_copy(K["pay"][:, :, 1], idxSf[:]))

        @block.tensor
        def _(pe):
            pe.wait_ge(s_cst, 1)
            nc.tensor.matmul(pC[:, 0:LO], zero[:, 0:128], zero[:], start=True, stop=False)
            @steps(pe, NR)
            def _(r):
                for k in range(RING):
                    pe.wait_ge(s_ohA, RING * r + k + 1)
                    nc.tensor.matmul(pC[:, 0:LO], ohi[:, k, :], olo[:, k, :], start=False, stop=False).then_inc(s_hist, 1)
            nc.tensor.matmul(pC[:, 0:LO], zero[:, 0:128], zero[:], start=False, stop=True).then_inc(s_hist_all, 1)
            pe.wait_ge(s_tot, 1)
            nc.tensor.matmul(pR[:, 0:1], tri[:], inc[:, LO - 1:LO], start=True, stop=True).then_inc(s_off, 1)
            pe.wait_ge(s_first, 1)

            def turn(t, k):
                pe.wait_ge(s_ohB, t + 1)
                need(pe, s_hiT, t - 1)
                nc.tensor.transpose(pT[:, k % 2, 0:TP], ohi[:, k, :], K["identb"][0:TP, 0:TP]).then_inc(s_tr, 1)

            turn(0, 0)
            @chunks(pe, NR)
            def _(u, a):
                r = 2 * u + a
                for k in range(RING):
                    t = RING * r + k
                    if not (isinstance(t, int) and t + 1 >= NT):
                        turn(t + 1, (k + 1) % RING)
                    need(pe, s_cur, t)
                    nc.tensor.matmul(pC[:, 0:LO], ohi[:, k, :], olo[:, k, :], start=True, stop=True).then_inc(s_acc, 1)
                    pe.wait_ge(s_hiT, t + 1)
                    if not (isinstance(t, int) and t < 2):
                        pe.wait_ge(s_used, t - 1)
                    nc.tensor.matmul(pL[0:TP, k % 2, 0:LO], hiT[:, k % 2, :], cur[:, k % 2, :], start=True, stop=True)
                    nc.tensor.matmul(pE[0:TP, k % 2, 0:LO], hiTb[:, k % 2, :], endh[:], start=True, stop=False)
                    nc.tensor.matmul(pE[0:TP, k % 2, 0:LO], hiTb[:, k % 2, :], endl[:], start=False, stop=True).then_inc(s_look, 1)

        @block.scalar
        def _(act):
            @chunks(act, NR)
            def _(u, a):
                r = 2 * u + a
                for k in range(RING):
                    t = RING * r + k
                    act.wait_ge(s_tr, t + 1)
                    if not (isinstance(t, int) and t < 2):
                        act.wait_ge(s_look, t - 1)
                    nc.scalar.activation(hiTb[:, k % 2, :], pT[:, k % 2, 0:TP], ACT.Copy)
                    nc.scalar.activation(hiT[:, k % 2, :], pT[:, k % 2, 0:TP], ACT.Copy).then_inc(s_hiT, 1)


def slots_phase(nc, g, K, T):
    with ExitStack() as ctx:
        a = Place(nc, ctx, "sl")
        s4 = a.sb("s4", [TP, NT, 4])
        rowS, rowN, rowP, rowI, rowE, rowH, rowM, rowV, zeros, run, pref = (
            a.sb(n, [NT, TP]) for n in ("rowS", "rowN", "rowP", "rowI", "rowE", "rowH", "rowM", "rowV", "zeros", "run", "pref"))
        lastr, crow, ccol = a.sb("lastr", [1, 2, NT]), a.sb("crow", [1, NT + 1]), a.sb("ccol", [NT, 1])
        cap = a.sb("cap", [1, 1])
        pR, pL, pC = (a.ps(n, [128, 512]) for n in ("pR", "pL", "pC"))
        s_s4, s_rowT, s_row, s_rowst, s_rown, s_rowi, s_colT, s_dv, s_runs, s_runT, s_carry, s_carryT, s_dinv = (
            a.sem(n) for n in ("s4", "rowT", "row", "row_stored", "row_next", "row_idx", "colT", "chain", "runs", "runs_rows",
                               "carry", "carry_col", "dinv"))
        block = ctx.enter_context(nc.Block())

        @block.sync
        def _(sp):
            sp.dma_start(s4[:], T["S4"].rearrange("(t p) c -> p t c", p=TP)).then_inc(s_s4, 16)
            sp.wait_ge(s_row, 1)
            sp.dma_start(T["srow"][:, 1:E + 1].rearrange("a (t p) -> (a t) p", p=TP), rowS[:]).then_inc(s_rowst, 16)
            sp.dma_start(T["srow"][:, 0:1], cap[:]).then_inc(s_rowst, 16)
            sp.dma_start(T["srow"][:, E + 1:E + 2], cap[:]).then_inc(s_rowst, 16)
            sp.wait_ge(s_rowst, 48)
            sp.dma_start(rowN[:], T["srow"][:, 2:E + 2].rearrange("a (t p) -> (a t) p", p=TP)).then_inc(s_rown, 16)
            sp.dma_start(rowP[:], T["srow"][:, 0:E].rearrange("a (t p) -> (a t) p", p=TP)).then_inc(s_rown, 16)
            sp.wait_ge(s_dinv, 1)
            for name, t in (("ssame", rowM), ("dinv", rowV)):
                sp.dma_start(T[name].rearrange("a (t p) -> (a t) p", p=TP), t[:]).then_inc(s_rowst, 16)
            sp.wait_ge(s_rowst, 80)

        @block.vector
        def _(dve):
            link = Chain(dve, s_dv)
            nc.vector.memset(cap[:], -1.0)
            nc.vector.memset(zeros[:], 0.0)
            nc.vector.memset(crow[:], 0.0)
            dve.wait_ge(s_s4, 16)
            nc.vector.tensor_copy(K["s_idxE"][:], s4[:, :, 2])
            nc.vector.tensor_copy(K["s_idxS"][:], s4[:, :, 1])
            dve.wait_ge(s_rowT, 1)
            nc.vector.tensor_copy(rowS[:], pR[0:NT, 0:TP])
            nc.vector.tensor_copy(rowH[:], pR[0:NT, TP:2 * TP]).then_inc(s_row, 1)
            dve.wait_ge(s_row, 1)
            dve.wait_ge(s_rown, 32)
            nc.vector.tensor_tensor(rowM[:], rowS[:], rowP[:], ALU.is_equal)
            link(nc.vector.tensor_tensor(rowE[:], rowS[:], rowN[:], ALU.is_equal))
            nc.vector.tensor_tensor_scan(run[:], rowM[:], rowH[:], 0.0, ALU.mult, ALU.add)
            nc.vector.tensor_tensor_scan(pref[:], rowM[:], zeros[:], 1.0, ALU.mult, ALU.add).then_inc(s_runs, 1)
            nc.vector.scalar_tensor_tensor(out=rowI[:], in0=rowE[:], scalar=float(FAR), in1=rowS[:],
                                           op0=ALU.mult, op1=ALU.add).then_inc(s_rowi, 1)
            dve.wait_ge(s_colT, 1)
            nc.vector.tensor_copy(K["src_end"][:], pR[0:TP, 256:256 + NT])
            dve.wait_ge(s_runT, 1)
            link(nc.vector.tensor_copy(lastr[:], pL[0:1, 0:2 * NT].rearrange("p (k t) -> p k t", k=2)))
            nc.vector.tensor_tensor_scan(crow[:, 1:NT + 1], lastr[:, 1, :], lastr[:, 0, :], 0.0, ALU.mult, ALU.add).then_inc(s_carry, 1)
            dve.wait_ge(s_carryT, 1)
            link(nc.vector.tensor_copy(ccol[:], pC[0:NT, 0:1]))
            link(nc.vector.scalar_tensor_tensor(out=run[:], in0=pref[:], scalar=ccol[:, 0:1], in1=run[:], op0=ALU.mult, op1=ALU.add))
            nc.vector.tensor_scalar(pref[:], run[:], 0.0, None, ALU.is_gt)
            link(nc.vector.tensor_scalar(rowV[:], run[:], 1.2e-38, None, ALU.max))
            nc.vector.tensor_scalar(rowE[:], rowE[:], -1.0, 1.0, ALU.mult, ALU.add)
            link(nc.vector.reciprocal(run[:], rowV[:]))
            link(nc.vector.tensor_tensor(pref[:], pref[:], rowE[:], ALU.mult))
            nc.vector.tensor_tensor(rowV[:], run[:], pref[:], ALU.mult).then_inc(s_dinv, 1)

        @block.tensor
        def _(pe):
            pe.wait_ge(s_s4, 16)
            nc.tensor.transpose(pR[0:NT, 0:TP], s4[:, :, 0], K["ident"][0:TP, 0:TP])
            nc.tensor.transpose(pR[0:NT, TP:2 * TP], s4[:, :, 3], K["ident"][0:TP, 0:TP]).then_inc(s_rowT, 1)
            pe.wait_ge(s_rowi, 1)
            nc.tensor.transpose(pR[0:TP, 256:256 + NT], rowI[:], K["ident"][0:NT, 0:NT]).then_inc(s_colT, 1)
            pe.wait_ge(s_runs, 1)
            nc.tensor.transpose(pL[0:1, 0:NT], run[:, TP - 1:TP], K["ident"][0:NT, 0:NT])
            nc.tensor.transpose(pL[0:1, NT:2 * NT], pref[:, TP - 1:TP], K["ident"][0:NT, 0:NT]).then_inc(s_runT, 1)
            pe.wait_ge(s_carry, 1)
            nc.tensor.transpose(pC[0:NT, 0:1], crow[:, 0:NT], K["ident"][0:1, 0:1]).then_inc(s_carryT, 1)


def gathers(pool, s_go, s_ring, s_full, ring, index, c, n, table, buf):
    nc = pool.bass
    nc.gpsimd.tensor_copy(ring[:], index[:, bass.ds(CT * c, CT)]).then_inc(s_ring, 1)
    pool.wait_ge(s_ring, n)
    pool.sem_inc(s_go, 1)
    for k in range(CT):
        nc.gpsimd.indirect_dma_start(out=buf[:, k, :], out_offset=None, in_=table,
                                     in_offset=bass.IndirectOffsetOnAxis(ap=ring[:, k:k + 1], axis=0)).then_inc(s_full, 16)


def row_stats(nc, z, rows, st, mv, s_stats):
    for r in range(rows):
        last = nc.vector.bn_stats(st[:, r, :], z[:, r, :])
    last.then_inc(s_stats, 1)


def row_aggr(nc, rows, st, mv):
    for r in range(rows):
        last = nc.vector.bn_aggr(mv[:, r, :], st[:, r, :])
    return last


def normalize(nc, out, z, rows, mv, rs):
    for r in range(rows):
        last = nc.vector.tensor_scalar(out[:, r, :], z[:, r, :], mv[:, r, 0:1], rs[:, r:r + 1], ALU.subtract, ALU.mult)
    return last


def bc(vec, rows):
    p = vec.shape[0]
    return vec[:, :].rearrange("p (o f) -> p o f", o=1).broadcast_to([p, rows, D])


def attention_phase(nc, g, K, T, dn, off):
    with ExitStack() as ctx:
        a = Place(nc, ctx, "at")
        W = {n: a.sb(n, [D, D]) for n in ("Wq", "Wk", "Wv", "Wo")}
        cols = K["cols"]
        bo = a.sb("bo", [TP, D])
        eps = a.sb("eps", [128, 1])
        rs_, rd_ = a.sb("ring_s", [TP, CT], I32), a.sb("ring_d", [TP, CT], I32)
        srcI, dstI = a.sb("srcI", [TP, NT], I32), a.sb("dstI", [TP, NT], I32)
        re_, pg = a.sb("ring_e", [TP, CT], I32), a.sb("pg", [TP, CT, 2])
        ga, gb = a.sb("ga", [TP, CT, D]), a.sb("gb", [TP, CT, D])
        xs, xd, q, prod, f, p, pv, dif, o, oF = (a.sb(n, [D, CE]) for n in ("xs", "xd", "q", "prod", "f", "p", "pv", "dif", "o", "oF"))
        dr, rc = a.sb("dr", [D, CE]), a.sb("rc", [D, CE])
        t1, t2 = a.sb("t1", [D, CE]), a.sb("t2", [D, CE])
        dstb = a.sb("dstb", [D, CE + 1], I32)
        same, pen = a.sb("same", [D, CE]), a.sb("pen", [D, CE])
        eb = a.sb("eb", [8, CE])
        M, Nu, De = (a.sb(n, [D, CE + 1]) for n in ("M", "Nu", "De"))
        z, y = a.sb("z", [TP, 2 * CT, D]), a.sb("y", [TP, 2 * CT, D])
        st, mv, sd, rs = a.sb("st", [TP, 2 * CT, 6]), a.sb("mv", [TP, 2 * CT, 2]), a.sb("sd", [TP, 2 * CT]), a.sb("rs", [TP, 2 * CT])
        pA, pB, pQ, pK, pV, pAt, pO, pR = (a.ps(n, [128, 512]) for n in ("pA", "pB", "pQ", "pK", "pV", "pAt", "pO", "pR"))
        (s_w, s_go, s_ring, s_ga, s_gb, s_tA, s_tB, s_xs, s_xd, s_psQ, s_psK, s_psV, s_q, s_prod, s_att, s_args, s_exp, s_pv,
         s_o, s_psO, s_oF, s_psR, s_z, s_gbc, s_mask, s_sd, s_mv, s_y, s_eb, s_dstb, s_st, s_zs, s_dgo, s_ch, s_d, s_eps, s_init) = (
            a.sem(n) for n in ("weights", "go", "ring", "ga", "gb", "tA", "tB", "xs", "xd", "psQ", "psK", "psV", "q", "prod", "att",
                               "args", "exp", "pv", "o", "psO", "oF", "psR", "z", "gb_copied", "mask", "sd", "mv", "y", "eb",
                               "dstb", "stored", "zs", "dve_go", "chain", "stats", "eps", "init"))
        s_ringE, s_pg, s_pay = (a.sem(n) for n in ("ringE", "pg", "pay"))
        block = ctx.enter_context(nc.Block())

        @block.sync
        def _(sp):
            for n in W:
                sp.dma_start(W[n][:], g[n]).then_inc(s_w, 16)
            sp.dma_start(bo[:], g["rowv"][0:1, :].broadcast_to([TP, D])).then_inc(s_w, 16)
            sp.dma_start(srcI[:], g["src_col"]).then_inc(s_w, 16)
            sp.dma_start(dstI[:], g["dst_col"]).then_inc(s_w, 16)
            sp.dma_start(dstb[:], g["dst_pad"][:, 0:CE + 1].broadcast_to([D, CE + 1])).then_inc(s_dstb, 16)
            sp.dma_start(eb[:], g["ea8T"][:, 0:CE]).then_inc(s_eb, 16)

            def store(c):
                sp.wait_ge(s_y, c + 1)
                sp.dma_start(rows_of(T["T1"], CE * c, CT), y[:, 0:CT, :]).then_inc(s_st, 16)
                sp.dma_start(rows_of(T["T1"], CE * c + E, CT), y[:, CT:2 * CT, :]).then_inc(s_st, 16)

            def chunk(u, a, last=False):
                c = 2 * u + a
                dn.load(sp, u, a + off + 1)
                if not last:
                    sp.wait_ge(s_mask, c + 1)
                    sp.dma_start(dstb[:], g["dst_pad"][:, bass.ds(CE * c + CE, CE + 1)].broadcast_to([D, CE + 1])).then_inc(s_dstb, 16)
                    sp.wait_ge(s_att, c + 1)
                    sp.dma_start(eb[:], g["ea8T"][:, bass.ds(CE * c + CE, CE)]).then_inc(s_eb, 16)
                dn.store(sp, u, a + off - LAG_W)
                store(c)

            chunks(sp, NC - 1)(chunk)
            chunk(0, NC - 1, last=True)
            sp.wait_ge(s_st, 32 * NC)

        @block.gpsimd
        def _(pool):
            pool.wait_ge(s_w, 16 * 7)
            nc.gpsimd.memset(eps[:], EPS).then_inc(s_eps, 1)

            def keep(u, a):
                c = 2 * u + a
                pool.wait_ge(s_pg, 64 * (c + 1))
                pool.sem_inc(s_go, 1)
                nc.gpsimd.tensor_copy(K["pay"][:, bass.ds(CT * c, CT), 2:4], pg[:]).then_inc(s_pay, 1)
                pool.wait_ge(s_pay, c + 1)
                pool.sem_inc(s_go, 1)

            @chunks(pool)
            def _(u, a):
                c = 2 * u + a
                pool.wait_ge(s_zs, c)
                pool.wait_ge(s_tA, c)
                pool.sem_inc(s_go, 1)
                gathers(pool, s_go, s_ring, s_ga, rs_, srcI, c, 2 * c + 1, g["x"], ga)
                pool.wait_ge(s_gbc, c)
                pool.wait_ge(s_tB, c)
                pool.sem_inc(s_go, 1)
                gathers(pool, s_go, s_ring, s_gb, rd_, dstI, c, 2 * c + 2, g["x"], gb)
                if not (isinstance(c, int) and c == 0):
                    keep(u, a - 1)
                gathers(pool, s_go, s_ringE, s_pg, re_, K["clip"], c, c + 1, T["ptab"], pg)
                dn.pool_z(pool, u, a + off)
                dn.pool_q(pool, u, a + off - LAG_Y)
                dn.pool_w(pool, u, a + off - LAG_W)
            keep(0, NC - 1)

        @block.tensor
        def _(pe):
            pe.wait_ge(s_w, 16 * 7)
            @chunks(pe)
            def _(u, a):
                c = 2 * u + a
                pe.wait_ge(s_ga, 64 * (c + 1))
                for k in range(CT):
                    last = nc.tensor.transpose(pA[:, k * TP:(k + 1) * TP], ga[:, k, :], K["ident"][0:TP, 0:TP])
                last.then_inc(s_tA, 1)
                pe.wait_ge(s_gb, 64 * (c + 1))
                for k in range(CT):
                    last = nc.tensor.transpose(pB[:, k * TP:(k + 1) * TP], gb[:, k, :], K["ident"][0:TP, 0:TP])
                last.then_inc(s_tB, 1)
                pe.wait_ge(s_xd, c + 1)
                nc.tensor.matmul(pQ[:, 0:CE], W["Wq"][:], xd[:], start=True, stop=True).then_inc(s_psQ, 1)
                pe.wait_ge(s_xs, c + 1)
                nc.tensor.matmul(pK[:, 0:CE], W["Wk"][:], xs[:], start=True, stop=True).then_inc(s_psK, 1)
                nc.tensor.matmul(pV[:, 0:CE], W["Wv"][:], xs[:], start=True, stop=True).then_inc(s_psV, 1)
                pe.wait_ge(s_prod, c + 1)
                pe.wait_ge(s_eb, 16 * (c + 1))
                nc.tensor.matmul(pAt[:, 0:CE], K["heads"][:], prod[:], start=True, stop=False)
                nc.tensor.matmul(pAt[:, 0:CE], K["expand"][:], eb[:], start=False, stop=True).then_inc(s_att, 1)
                pe.wait_ge(s_o, c + 1)
                nc.tensor.matmul(pO[:, 0:CE], W["Wo"][:], o[:], start=True, stop=True).then_inc(s_psO, 1)
                pe.wait_ge(s_oF, c + 1)
                for k in range(CT):
                    last = nc.tensor.transpose(pR[0:TP, k * D:(k + 1) * D], oF[:, k * TP:(k + 1) * TP], K["ident"][:])
                last.then_inc(s_psR, 1)

        @block.scalar
        def _(act):
            act.wait_ge(s_eps, 1)
            act.wait_ge(s_w, 16 * 7)
            @chunks(act)
            def _(u, a):
                c = 2 * u + a
                act.wait_ge(s_tA, c + 1)
                act.wait_ge(s_psV, c)
                nc.scalar.activation(xs[:], pA[:, 0:CE], ACT.Copy).then_inc(s_xs, 1)
                act.wait_ge(s_tB, c + 1)
                act.wait_ge(s_psQ, c)
                nc.scalar.activation(xd[:], pB[:, 0:CE], ACT.Copy).then_inc(s_xd, 1)
                act.wait_ge(s_y, c)
                nc.scalar.activation(z[:, 0:CT, :], gb[:], ACT.Copy).then_inc(s_gbc, 1)
                act.wait_ge(s_psQ, c + 1)
                act.wait_ge(s_prod, c)
                nc.scalar.activation(q[:], pQ[:, 0:CE], ACT.Identity, bias=cols[:, 0:1]).then_inc(s_q, 1)
                dn.act_root3(act, u, a + off - LAG_Y)
                dn.act_root4(act, u, a + off - LAG_W)
                dn.act_root1(act, u, a + off - 1)
                act.wait_ge(s_args, c + 1)
                nc.scalar.activation(f[:], t2[:], ACT.Exp)
                nc.scalar.activation(p[:], dif[:], ACT.Exp).then_inc(s_exp, 1)
                dn.act_out(act, u, a + off - LAG_W)
                dn.act_x3(act, u, a + off - LAG_Y)
                dn.act_root2(act, u, a + off - 1)
                act.wait_ge(s_psO, c + 1)
                act.wait_ge(s_psR, c)
                nc.scalar.activation(oF[:], pO[:, 0:CE], ACT.Identity, bias=cols[:, 3:4]).then_inc(s_oF, 1)
                dn.act_n(act, u, a + off - 1)
                act.wait_ge(s_mv, c + 1)
                nc.scalar.activation(sd[:], mv[:, :, 1], ACT.Sqrt, bias=eps[0:TP, :]).then_inc(s_sd, 1)

        @block.vector
        def _(dve):
            nc.vector.memset(M[:], -NEG)
            nc.vector.memset(Nu[:], 0.0)
            first = nc.vector.memset(De[:], 0.0)
            first.then_inc(s_init, 1)
            dve.wait_ge(s_init, 1)
            dve.wait_ge(s_w, 16 * 7)
            @chunks(dve)
            def _(u, a):
                c = 2 * u + a
                link = Chain(dve, s_ch, c, 9)
                dve.wait_ge(s_dstb, 16 * (c + 1))
                nc.vector.tensor_tensor(same[:], dstb[:, 1:CE + 1], dstb[:, 0:CE], ALU.is_equal).then_inc(s_mask, 1)
                dve.wait_ge(s_mask, c + 1)
                nc.vector.tensor_scalar(pen[:], same[:], NEG, -NEG, ALU.mult, ALU.add)
                dve.wait_ge(s_ga, 64 * (c + 1))
                nc.vector.tensor_tensor(z[:, CT:2 * CT, :], ga[:], bc(bo, CT), ALU.add).then_inc(s_zs, 1)
                dn.dve_y(dve, u, a + off - LAG_Y)
                dn.dve_w(dve, u, a + off - LAG_W)
                dve.wait_ge(s_psK, c + 1)
                dve.wait_ge(s_q, c + 1)
                nc.vector.scalar_tensor_tensor(out=prod[:], in0=pK[:, 0:CE], scalar=cols[:, 1:2], in1=q[:],
                                               op0=ALU.add, op1=ALU.mult).then_inc(s_prod, 1)
                dn.dve_z(dve, u, a + off - 1)
                nc.vector.tensor_copy(M[:, 0:1], M[:, CE:CE + 1])
                nc.vector.tensor_copy(Nu[:, 0:1], Nu[:, CE:CE + 1])
                link(nc.vector.tensor_copy(De[:, 0:1], De[:, CE:CE + 1]))
                dve.wait_ge(s_att, c + 1)
                link(nc.vector.tensor_tensor_scan(M[:, 1:CE + 1], pen[:], pAt[:, 0:CE], M[:, 0:1], ALU.add, ALU.max))
                nc.vector.tensor_tensor(dif[:], pAt[:, 0:CE], M[:, 1:CE + 1], ALU.subtract)
                link(nc.vector.tensor_tensor(t1[:], M[:, 0:CE], M[:, 1:CE + 1], ALU.subtract))
                nc.vector.scalar_tensor_tensor(out=t2[:], in0=t1[:], scalar=0.0, in1=pen[:], op0=ALU.min, op1=ALU.add).then_inc(s_args, 1)
                dn.dve_h(dve, u, a + off - 1)
                dn.dve_x3(dve, u, a + off - LAG_Y)
                dn.dve_o(dve, u, a + off - LAG_W)
                dve.wait_ge(s_exp, c + 1)
                dve.wait_ge(s_psV, c + 1)
                link(nc.vector.scalar_tensor_tensor(out=pv[:], in0=pV[:, 0:CE], scalar=cols[:, 2:3], in1=p[:], op0=ALU.add, op1=ALU.mult))
                nc.vector.tensor_tensor_scan(De[:, 1:CE + 1], f[:], p[:], De[:, 0:1], ALU.mult, ALU.add)
                link(nc.vector.tensor_tensor_scan(Nu[:, 1:CE + 1], f[:], pv[:], Nu[:, 0:1], ALU.mult, ALU.add))
                link(nc.vector.tensor_scalar(dr[:], De[:, 1:CE + 1], 1e-16, None, ALU.add))
                link(nc.vector.reciprocal(rc[:], dr[:]))
                nc.vector.tensor_tensor(o[:], Nu[:, 1:CE + 1], rc[:], ALU.mult).then_inc(s_o, 1)
                dn.dve_n(dve, u, a + off - 1)
                dve.wait_ge(s_gbc, c + 1)
                dve.wait_ge(s_psR, c + 1)
                link(nc.vector.tensor_tensor(z[:, 0:CT, :], z[:, 0:CT, :], pR[0:TP, :].rearrange("p (k f) -> p k f", k=CT), ALU.add))
                row_stats(nc, z, 2 * CT, st, mv, s_d)
                dve.wait_ge(s_d, c + 1)
                dve.sem_inc(s_dgo, 1)
                row_aggr(nc, 2 * CT, st, mv).then_inc(s_mv, 1)
                dve.wait_ge(s_sd, c + 1)
                link(nc.vector.reciprocal(rs[:], sd[:]))
                dve.wait_ge(s_st, 32 * c)
                normalize(nc, y, z, 2 * CT, mv, rs).then_inc(s_y, 1)
                dve.wait_ge(s_y, c + 1)
                link.done()


DR = 5
DP = N // 128
DS = DP // DR
DL = N - 128 * DP
LAG_Y, LAG_W = 3, 5
assert DP == DS * DR and DL > 0 and LAG_W + 3 * NC == DS + 2


def outside(t):
    return isinstance(t, int) and not 0 <= t <= DS


def need(eng, sem, n):
    if not isinstance(n, int) or n > 0:
        eng.wait_ge(sem, n)


class Dense:

    def __init__(self, nc, ctx, g, T):
        self.nc, self.g, self.T = nc, g, T
        a = self.place = Place(nc, ctx, "dn")
        self.bo, self.ub, self.lg, self.lb, self.b2, self.cb = (a.sb(n, [128, D]) for n in ("bo", "ub", "lg", "lb", "b2", "cb"))
        self.eps = a.sb("eps", [128, 1])
        self.x, self.z, self.h, self.n, self.q, self.y, self.x3, self.w, self.o = (
            a.sb(n, [128, 2, DR, D]) for n in ("x", "z", "h", "n", "q", "y", "x3", "w", "o"))
        self.ng = a.sb("ng", [128, DR, D])
        self.st = a.sb("st", [128, 4, DR, 6])
        self.mv = a.sb("mv", [128, 4, DR, 2])
        self.sd, self.rs, self.nb = (a.sb(n, [128, 4, DR]) for n in ("sd", "rs", "nb"))
        self.t3, self.v3 = a.sb("t3", [128, DR]), a.sb("v3", [128, DR])
        self.s_w = a.sem("weights")
        self.s_c = a.sem("consts")
        self.s_x = [a.sem(f"x{k}") for k in range(2)]
        self.s_st = [a.sem(f"stored{k}") for k in range(2)]
        (self.s_z, self.s_m1, self.s_sd1, self.s_h, self.s_m2, self.s_sd2, self.s_r2, self.s_n, self.s_ng, self.s_q, self.s_y,
         self.s_m3, self.s_sd3, self.s_r3, self.s_x3, self.s_w4, self.s_m4, self.s_sd4, self.s_r4, self.s_o, self.s_go) = (
            a.sem(n) for n in ("z", "stats1", "sd1", "h", "stats2", "sd2", "scale2", "n", "ng", "q", "y", "stats3", "sd3", "scale3",
                               "x3", "w", "stats4", "sd4", "scale4", "out", "dve_go"))
        self.s_l = [a.sem(f"chain{j}") for j in range(4)]
        self.xv = g["x"][0:128 * DP, :].rearrange("(p r) f -> p r f", p=128)
        self.ov = T["out"][0:128 * DP, :].rearrange("(p r) f -> p r f", p=128)

    def rows(self, t):
        return (DL, 1) if isinstance(t, int) and t == DS else (128, DR)

    def cut(self, buf, t, k):
        p, r = self.rows(t)
        return buf[0:p, k, 0:r]

    def vec(self, v, t):
        p, r = self.rows(t)
        return bc(v[0:p], r)

    def weights(self, sp):
        for v, r in ((self.bo, 0), (self.ub, 1), (self.lg, 2), (self.lb, 3), (self.b2, 4)):
            sp.dma_start(v[:], self.g["rowv"][r:r + 1, :].broadcast_to([128, D])).then_inc(self.s_w, 16)

    def side(self, view, tensor, t):
        if isinstance(t, int) and t == DS:
            return tensor[128 * DP:N, :].rearrange("p (r f) -> p r f", r=1)
        return view[:, bass.ds(t * DR, DR), :]

    def load(self, sp, u, a):
        t, k = 2 * u + a, a % 2
        if outside(t):
            return
        need(sp, self.s_z, t - 1)
        sp.dma_start(self.cut(self.x, t, k), self.side(self.xv, self.g["x"], t)).then_inc(self.s_x[k], 16)

    def store(self, sp, u, a):
        t, k = 2 * u + a, a % 2
        if outside(t):
            return
        sp.wait_ge(self.s_o, t + 1)
        sp.dma_start(self.side(self.ov, self.T["out"], t), self.cut(self.o, t, k)).then_inc(self.s_st[k], 16)

    def pool_z(self, pool, u, a):
        t, k = 2 * u + a, a % 2
        if outside(t):
            return
        pool.wait_ge(self.s_x[k], 16 * (u + a // 2 + 1))
        need(pool, self.s_h, t - 1)
        self.nc.gpsimd.tensor_tensor(self.cut(self.z, t, k), self.cut(self.x, t, k), self.vec(self.bo, t), ALU.add).then_inc(self.s_z, 1)

    def pool_q(self, pool, u, a):
        t, k = 2 * u + a, a % 2
        if outside(t):
            return
        p, r = self.rows(t)
        pool.wait_ge(self.s_n, t + 1)
        need(pool, self.s_q, t)
        self.nc.gpsimd.tensor_tensor(self.ng[0:p, 0:r], self.cut(self.n, t, k), self.vec(self.lg, t), ALU.mult).then_inc(self.s_ng, 1)
        need(pool, self.s_y, t - 1)
        pool.wait_ge(self.s_ng, t + 1)
        self.nc.gpsimd.tensor_tensor(self.cut(self.q, t, k), self.ng[0:p, 0:r], self.vec(self.cb, t), ALU.add).then_inc(self.s_q, 1)

    def pool_w(self, pool, u, a):
        t, k = 2 * u + a, a % 2
        if outside(t):
            return
        pool.wait_ge(self.s_x3, t + 1)
        need(pool, self.s_o, t - 1)
        self.nc.gpsimd.tensor_tensor(self.cut(self.w, t, k), self.cut(self.x3, t, k), self.vec(self.b2, t), ALU.add).then_inc(self.s_w4, 1)

    def consts(self, dve):
        nc = self.nc
        nc.vector.memset(self.eps[:], EPS)
        dve.wait_ge(self.s_w, 80)
        nc.vector.tensor_tensor(self.cb[:], self.lb[:], self.ub[:], ALU.subtract).then_inc(self.s_c, 1)

    def stats(self, dve, buf, t, k, j, s_chain, n):
        nc = self.nc
        p, r = self.rows(t)
        for i in range(r):
            last = nc.vector.bn_stats(self.st[0:p, j, i, :], buf[0:p, k, i, :])
        last.then_inc(s_chain, 1)
        dve.wait_ge(s_chain, n)
        dve.sem_inc(self.s_go, 1)
        for i in range(r):
            last = nc.vector.bn_aggr(self.mv[0:p, j, i, :], self.st[0:p, j, i, :])
        return last

    def scale(self, dve, t, j, s_chain, n, s_done):
        nc = self.nc
        p, r = self.rows(t)
        nc.vector.reciprocal(self.rs[0:p, j, 0:r], self.sd[0:p, j, 0:r]).then_inc(s_chain, 1)
        dve.wait_ge(s_chain, n)
        nc.vector.scalar_tensor_tensor(out=self.nb[0:p, j, 0:r], in0=self.mv[0:p, j, 0:r, 0], scalar=-1.0, in1=self.rs[0:p, j, 0:r],
                                       op0=ALU.mult, op1=ALU.mult).then_inc(s_done, 1)

    def dve_z(self, dve, u, a):
        t, k = 2 * u + a, a % 2
        if outside(t):
            return
        dve.wait_ge(self.s_z, t + 1)
        self.stats(dve, self.z, t, k, 0, self.s_l[0], 2 * t + 1).then_inc(self.s_m1, 1)

    def dve_h(self, dve, u, a):
        nc = self.nc
        t, k = 2 * u + a, a % 2
        if outside(t):
            return
        p, r = self.rows(t)
        dve.wait_ge(self.s_sd1, t + 1)
        nc.vector.reciprocal(self.rs[0:p, 0, 0:r], self.sd[0:p, 0, 0:r]).then_inc(self.s_l[0], 1)
        need(dve, self.s_n, t - 1)
        need(dve, self.s_y, t - 1)
        dve.wait_ge(self.s_l[0], 2 * t + 2)
        for i in range(r):
            last = nc.vector.scalar_tensor_tensor(out=self.h[0:p, k, i, :], in0=self.z[0:p, k, i, :], scalar=self.rs[0:p, 0, i:i + 1],
                                                  in1=self.ub[0:p, :], op0=ALU.mult, op1=ALU.add)
        last.then_inc(self.s_h, 1)
        dve.wait_ge(self.s_h, t + 1)
        self.stats(dve, self.h, t, k, 1, self.s_l[1], 2 * t + 1).then_inc(self.s_m2, 1)

    def dve_n(self, dve, u, a):
        t = 2 * u + a
        if outside(t):
            return
        dve.wait_ge(self.s_sd2, t + 1)
        need(dve, self.s_n, t)
        self.scale(dve, t, 1, self.s_l[1], 2 * t + 2, self.s_r2)

    def dve_y(self, dve, u, a):
        nc = self.nc
        t, k = 2 * u + a, a % 2
        if outside(t):
            return
        p, r = self.rows(t)
        dve.wait_ge(self.s_q, t + 1)
        need(dve, self.s_x3, t - 1)
        nc.vector.tensor_tensor(self.cut(self.y, t, k), self.cut(self.h, t, k), self.cut(self.q, t, k), ALU.add).then_inc(self.s_y, 1)
        dve.wait_ge(self.s_y, t + 1)
        self.stats(dve, self.y, t, k, 2, self.s_l[2], 4 * t + 1).then_inc(self.s_l[2], 1)
        dve.wait_ge(self.s_l[2], 4 * t + 2)
        var = self.mv[0:p, 2, 0:r, 1]
        nc.vector.tensor_scalar(self.t3[0:p, 0:r], var, EPS, EPS, ALU.add, ALU.mult).then_inc(self.s_l[2], 1)
        dve.wait_ge(self.s_l[2], 4 * t + 3)
        nc.vector.tensor_tensor(self.v3[0:p, 0:r], self.t3[0:p, 0:r], var, ALU.add).then_inc(self.s_m3, 1)

    def dve_x3(self, dve, u, a):
        t = 2 * u + a
        if outside(t):
            return
        dve.wait_ge(self.s_sd3, t + 1)
        need(dve, self.s_x3, t)
        self.scale(dve, t, 2, self.s_l[2], 4 * t + 4, self.s_r3)

    def dve_w(self, dve, u, a):
        t, k = 2 * u + a, a % 2
        if outside(t):
            return
        dve.wait_ge(self.s_w4, t + 1)
        self.stats(dve, self.w, t, k, 3, self.s_l[3], 2 * t + 1).then_inc(self.s_m4, 1)

    def dve_o(self, dve, u, a):
        t = 2 * u + a
        if outside(t):
            return
        dve.wait_ge(self.s_sd4, t + 1)
        need(dve, self.s_o, t)
        self.scale(dve, t, 3, self.s_l[3], 2 * t + 2, self.s_r4)

    def root(self, act, u, a, j, s_from, s_to):
        t = 2 * u + a
        if outside(t):
            return
        p, r = self.rows(t)
        act.wait_ge(s_from, t + 1)
        if j == 2:
            last = self.nc.scalar.activation(self.sd[0:p, j, 0:r], self.v3[0:p, 0:r], ACT.Sqrt)
        else:
            last = self.nc.scalar.activation(self.sd[0:p, j, 0:r], self.mv[0:p, j, 0:r, 1], ACT.Sqrt, bias=self.eps[0:p, :])
        last.then_inc(s_to, 1)

    def act_root1(self, act, u, a):
        self.root(act, u, a, 0, self.s_m1, self.s_sd1)

    def act_root2(self, act, u, a):
        self.root(act, u, a, 1, self.s_m2, self.s_sd2)

    def act_root3(self, act, u, a):
        self.root(act, u, a, 2, self.s_m3, self.s_sd3)

    def act_root4(self, act, u, a):
        self.root(act, u, a, 3, self.s_m4, self.s_sd4)

    def norm(self, act, t, k, j, out, src, s_done):
        p, r = self.rows(t)
        for i in range(r):
            last = self.nc.scalar.activation(out[0:p, k, i, :], src[0:p, k, i, :], ACT.Identity,
                                             bias=self.nb[0:p, j, i:i + 1], scale=self.rs[0:p, j, i:i + 1])
        last.then_inc(s_done, 1)

    def act_n(self, act, u, a):
        t, k = 2 * u + a, a % 2
        if outside(t):
            return
        act.wait_ge(self.s_r2, t + 1)
        need(act, self.s_q, t - 1)
        self.norm(act, t, k, 1, self.n, self.h, self.s_n)

    def act_x3(self, act, u, a):
        t, k = 2 * u + a, a % 2
        if outside(t):
            return
        act.wait_ge(self.s_r3, t + 1)
        need(act, self.s_w4, t - 1)
        self.norm(act, t, k, 2, self.x3, self.y, self.s_x3)

    def act_out(self, act, u, a):
        t, k = 2 * u + a, a % 2
        if outside(t):
            return
        act.wait_ge(self.s_r4, t + 1)
        need(act, self.s_st[k], 16 * (u + a // 2))
        self.norm(act, t, k, 3, self.o, self.w, self.s_o)


def dense_alone(nc, dn, first, last):
    with nc.Block() as block:
        def each(eng, *stages):
            for j in range(first, last):
                for stage, lag in stages:
                    stage(eng, 0, j - lag)

        @block.sync
        def _(sp):
            if first == 0:
                dn.weights(sp)
                dn.load(sp, 0, 0)
            each(sp, (dn.load, -1), (dn.store, LAG_W))
            if last > DS:
                for k in range(2):
                    sp.wait_ge(dn.s_st[k], 16 * ((DS + 2 - k) // 2))

        @block.gpsimd
        def _(pool):
            if first == 0:
                pool.wait_ge(dn.s_c, 1)
            each(pool, (dn.pool_z, 0), (dn.pool_q, LAG_Y), (dn.pool_w, LAG_W))

        @block.vector
        def _(dve):
            if first == 0:
                dn.consts(dve)
                dve.wait_ge(dn.s_c, 1)
            each(dve, (dn.dve_y, LAG_Y), (dn.dve_w, LAG_W), (dn.dve_z, 1), (dn.dve_h, 1), (dn.dve_x3, LAG_Y), (dn.dve_o, LAG_W), (dn.dve_n, 1))

        @block.scalar
        def _(act):
            each(act, (dn.act_root3, LAG_Y), (dn.act_root4, LAG_W), (dn.act_root1, 1), (dn.act_root2, 1), (dn.act_out, LAG_W), (dn.act_x3, LAG_Y), (dn.act_n, 1))


def message_phase(nc, g, K, T, dn, off):
    with ExitStack() as ctx:
        a = Place(nc, ctx, "ms")
        Wx, Wu = a.sb("Wx", [D, D]), a.sb("Wu", [D, D])
        We, emb = a.sb("We", [32, D]), a.sb("emb", [32, 16])
        typeW = a.sb("typeW", [16, D])
        ub, lg, lb = a.sb("ub", [TP, D]), a.sb("lg", [TP, D]), a.sb("lb", [TP, D])
        eps, one = a.sb("eps", [128, 1]), a.sb("one", [1, CE])
        kind, kindf = a.sb("kind", [16, 1], I32), a.sb("kindf", [16, 1])
        ring = a.sb("ring", [TP, CT], I32)
        ga = a.sb("ga", [TP, CT, D])
        xin = a.sb("xin", [TP, 2 * CT, D])
        xs, m, S, oF = (a.sb(n, [D, CE]) for n in ("xs", "m", "S", "oF"))
        carry = a.sb("carry", [D, 1])
        dstb, same = a.sb("dstb", [D, CE + 1], I32), a.sb("same", [D, CE])
        typ, oneh = a.sb("typ", [16, CE], I32), a.sb("oneh", [16, CE])
        deg = a.sb("deg", [1, CE + 1])
        rd = a.sb("rd", [TP, CT])
        h, n1, y = (a.sb(n, [TP, 2 * CT, D]) for n in ("h", "n1", "y"))
        st, mv, sd, rs = a.sb("st", [TP, 2 * CT, 6]), a.sb("mv", [TP, 2 * CT, 2]), a.sb("sd", [TP, 2 * CT]), a.sb("rs", [TP, 2 * CT])
        pA, pM, pO, pR, pD = (a.ps(n, [128, 512]) for n in ("pA", "pM", "pO", "pR", "pD"))
        (s_w, s_go, s_ring, s_ga, s_xd, s_dstb, s_typ, s_st, s_eps, s_kind, s_init, s_tw, s_tA, s_xs, s_gac, s_mask, s_oneh,
         s_psM, s_m, s_S, s_psO, s_oF, s_psR, s_deg, s_psD, s_mv, s_sd, s_mv2, s_sd2, s_y, s_ch, s_d, s_dgo, s_h, s_twc, s_rdc) = (
            a.sem(n) for n in ("weights", "go", "ring", "ga", "xd", "dstb", "type", "stored", "eps", "kind", "init", "typeW",
                               "tA", "xs", "ga_copied", "mask", "onehot", "psM", "m", "S", "psO", "oF", "psR", "deg", "psD",
                               "mv", "sd", "mv2", "sd2", "y", "chain", "stats", "dve_go", "h", "typeW_copied", "rdeg"))
        rslot, rpay = a.sb("rslot", [TP, CT], I32), a.sb("rpay", [TP, CT, 4])
        s_ringP, s_pay = a.sem("ringP"), a.sem("pay")
        block = ctx.enter_context(nc.Block())

        @block.sync
        def _(sp):
            for t, n in ((Wx, "Wmx"), (Wu, "Wu"), (We, "Wme"), (emb, "embT")):
                sp.dma_start(t[:], g[n]).then_inc(s_w, 16)
            for t, r in ((ub, 1), (lg, 2), (lb, 3)):
                sp.dma_start(t[:], g["rowv"][r:r + 1, :].broadcast_to([TP, D])).then_inc(s_w, 16)

            def load_masks(e0):
                sp.dma_start(dstb[:], g["dst_pad"][:, bass.ds(e0, CE + 1)].broadcast_to([D, CE + 1])).then_inc(s_dstb, 16)

            def load_types(e0):
                sp.dma_start(typ[:], g["type_row"][:, bass.ds(e0, CE)].broadcast_to([16, CE])).then_inc(s_typ, 16)

            def load_targets(e0):
                sp.dma_start(xin[:, 0:CT, :], rows_of(T["T1"], e0, CT)).then_inc(s_xd, 16)

            def store(c):
                sp.wait_ge(s_y, c + 1)
                sp.dma_start(rows_of(T["T2"], CE * c, CT), y[:, 0:CT, :]).then_inc(s_st, 16)
                sp.dma_start(rows_of(T["T2"], CE * c + E, CT), y[:, CT:2 * CT, :]).then_inc(s_st, 16)

            load_masks(0)
            load_types(0)
            load_targets(0)
            def chunk(u, a, last=False):
                c = 2 * u + a
                dn.load(sp, u, a + off + 1)
                if not last:
                    sp.wait_ge(s_mask, c + 1)
                    load_masks(CE * c + CE)
                    sp.wait_ge(s_oneh, c + 1)
                    load_types(CE * c + CE)
                dn.store(sp, u, a + off - LAG_W)
                store(c)
                if not last:
                    load_targets(CE * c + CE)

            chunks(sp, NC - 1)(chunk)
            chunk(0, NC - 1, last=True)
            sp.wait_ge(s_st, 32 * NC)

        @block.gpsimd
        def _(pool):
            nc.gpsimd.memset(one[:], 1.0)
            nc.gpsimd.iota(kind[:], pattern=[[0, 1]], base=0, channel_multiplier=1).then_inc(s_kind, 1)
            pool.wait_ge(s_kind, 1)
            nc.gpsimd.tensor_copy(kindf[:], kind[:])
            nc.gpsimd.memset(eps[:], EPS).then_inc(s_eps, 1)
            @chunks(pool)
            def _(u, a):
                c = 2 * u + a
                pool.wait_ge(s_gac, c)
                pool.wait_ge(s_tA, c)
                pool.sem_inc(s_go, 1)
                gathers(pool, s_go, s_ring, s_ga, ring, K["idxS"], c, c + 1, T["T1"], ga)
                pool.wait_ge(s_pay, 64 * c)
                pool.sem_inc(s_go, 1)
                nc.gpsimd.tensor_copy(rpay[:], K["pay"][:, bass.ds(CT * c, CT), :])
                nc.gpsimd.tensor_copy(rslot[:], K["slot"][:, bass.ds(CT * c, CT)]).then_inc(s_ringP, 1)
                pool.wait_ge(s_ringP, c + 1)
                pool.sem_inc(s_go, 1)
                for k in range(CT):
                    nc.gpsimd.indirect_dma_start(out=T["S4"], out_offset=bass.IndirectOffsetOnAxis(ap=rslot[:, k:k + 1], axis=0),
                                                 in_=rpay[:, k, :], in_offset=None).then_inc(s_pay, 16)
                dn.pool_z(pool, u, a + off)
                dn.pool_q(pool, u, a + off - LAG_Y)
                dn.pool_w(pool, u, a + off - LAG_W)
            pool.wait_ge(s_pay, 16 * NT)

        @block.tensor
        def _(pe):
            pe.wait_ge(s_w, 16 * 7)
            nc.tensor.matmul(pM[0:16, 0:D], emb[:], We[:], start=True, stop=True).then_inc(s_tw, 1)
            pe.wait_ge(s_twc, 1)
            @chunks(pe)
            def _(u, a):
                c = 2 * u + a
                pe.wait_ge(s_ga, 64 * (c + 1))
                for k in range(CT):
                    last = nc.tensor.transpose(pA[:, k * TP:(k + 1) * TP], ga[:, k, :], K["ident"][0:TP, 0:TP])
                last.then_inc(s_tA, 1)
                pe.wait_ge(s_xs, c + 1)
                pe.wait_ge(s_oneh, c + 1)
                nc.tensor.matmul(pM[:, 0:CE], Wx[:], xs[:], start=True, stop=False)
                nc.tensor.matmul(pM[:, 0:CE], typeW[:], oneh[:], start=False, stop=True).then_inc(s_psM, 1)
                pe.wait_ge(s_deg, c + 1)
                for k in range(CT):
                    last = nc.tensor.matmul(pD[0:TP, k:k + 1], deg[0:1, 1 + k * TP:1 + (k + 1) * TP], one[0:1, 0:1], start=True, stop=True)
                last.then_inc(s_psD, 1)
                pe.wait_ge(s_S, c + 1)
                nc.tensor.matmul(pO[:, 0:CE], Wu[:], S[:], start=True, stop=True).then_inc(s_psO, 1)
                pe.wait_ge(s_oF, c + 1)
                for k in range(CT):
                    last = nc.tensor.transpose(pR[0:TP, k * D:(k + 1) * D], oF[:, k * TP:(k + 1) * TP], K["ident"][:])
                last.then_inc(s_psR, 1)

        @block.scalar
        def _(act):
            act.wait_ge(s_tw, 1)
            nc.scalar.activation(typeW[:], pM[0:16, 0:D], ACT.Copy).then_inc(s_twc, 1)
            act.wait_ge(s_eps, 1)
            act.wait_ge(s_w, 16 * 7)
            @chunks(act)
            def _(u, a):
                c = 2 * u + a
                act.wait_ge(s_tA, c + 1)
                act.wait_ge(s_psM, c)
                nc.scalar.activation(xs[:], pA[:, 0:CE], ACT.Copy).then_inc(s_xs, 1)
                act.wait_ge(s_y, c)
                nc.scalar.activation(xin[:, CT:2 * CT, :], ga[:], ACT.Copy).then_inc(s_gac, 1)
                dn.act_root3(act, u, a + off - LAG_Y)
                dn.act_root4(act, u, a + off - LAG_W)
                act.wait_ge(s_psM, c + 1)
                act.wait_ge(s_S, c)
                nc.scalar.activation(m[:], pM[:, 0:CE], ACT.Relu, bias=K["cols"][:, 4:5]).then_inc(s_m, 1)
                dn.act_root1(act, u, a + off - 1)
                act.wait_ge(s_psO, c + 1)
                act.wait_ge(s_psR, c)
                nc.scalar.activation(oF[:], pO[:, 0:CE], ACT.Copy).then_inc(s_oF, 1)
                dn.act_out(act, u, a + off - LAG_W)
                dn.act_x3(act, u, a + off - LAG_Y)
                act.wait_ge(s_mv, c + 1)
                nc.scalar.activation(sd[:], mv[:, :, 1], ACT.Sqrt, bias=eps[0:TP, :]).then_inc(s_sd, 1)
                dn.act_root2(act, u, a + off - 1)
                act.wait_ge(s_mv2, c + 1)
                nc.scalar.activation(sd[:], mv[:, :, 1], ACT.Sqrt, bias=eps[0:TP, :]).then_inc(s_sd2, 1)
                dn.act_n(act, u, a + off - 1)

        @block.vector
        def _(dve):
            nc.vector.memset(carry[:], 0.0)
            nc.vector.memset(deg[:], 0.0).then_inc(s_init, 1)
            dve.wait_ge(s_init, 1)
            dve.wait_ge(s_eps, 1)
            dve.wait_ge(s_w, 16 * 7)
            @chunks(dve)
            def _(u, a):
                c = 2 * u + a
                link = Chain(dve, s_ch, c, 9)
                dve.wait_ge(s_typ, 16 * (c + 1))
                dve.wait_ge(s_psM, c)
                nc.vector.tensor_scalar(oneh[:], typ[:], kindf[:, 0:1], None, ALU.is_equal).then_inc(s_oneh, 1)
                dve.wait_ge(s_dstb, 16 * (c + 1))
                nc.vector.tensor_tensor(same[:], dstb[:, 1:CE + 1], dstb[:, 0:CE], ALU.is_equal).then_inc(s_mask, 1)
                dve.wait_ge(s_psD, c)
                link(nc.vector.tensor_copy(deg[:, 0:1], deg[:, CE:CE + 1]))
                dve.wait_ge(s_mask, c + 1)
                nc.vector.tensor_tensor_scan(deg[:, 1:CE + 1], same[0:1, :], one[:], deg[:, 0:1], ALU.mult, ALU.add).then_inc(s_deg, 1)
                dn.dve_y(dve, u, a + off - LAG_Y)
                dn.dve_w(dve, u, a + off - LAG_W)
                dve.wait_ge(s_m, c + 1)
                dve.wait_ge(s_psO, c)
                nc.vector.tensor_tensor_scan(S[:], same[:], m[:], carry[:], ALU.mult, ALU.add).then_inc(s_S, 1)
                dn.dve_z(dve, u, a + off - 1)
                dve.wait_ge(s_psD, c + 1)
                nc.vector.reciprocal(rd[:], pD[0:TP, 0:CT]).then_inc(s_rdc, 1)
                dve.wait_ge(s_S, c + 1)
                nc.vector.tensor_copy(carry[:], S[:, CE - 1:CE])
                dve.wait_ge(s_xd, 16 * (c + 1))
                dve.wait_ge(s_gac, c + 1)
                link(nc.vector.tensor_tensor(h[:], xin[:], bc(ub, 2 * CT), ALU.add))
                nc.vector.tensor_copy(K["rdeg"][:, bass.ds(CT * c, CT)], rd[:])
                nc.vector.tensor_tensor(K["rdegH"][:, bass.ds(CT * c, CT)], rd[:], K["isH"][:, bass.ds(CT * c, CT)], ALU.mult)
                dn.dve_x3(dve, u, a + off - LAG_Y)
                dn.dve_o(dve, u, a + off - LAG_W)
                dve.wait_ge(s_psR, c + 1)
                for k in range(CT):
                    last = nc.vector.scalar_tensor_tensor(out=h[:, k, :], in0=pR[0:TP, k * D:(k + 1) * D], scalar=rd[:, k:k + 1],
                                                          in1=h[:, k, :], op0=ALU.mult, op1=ALU.add)
                link(last)
                row_stats(nc, h, 2 * CT, st, mv, s_d)
                dve.wait_ge(s_d, 2 * c + 1)
                dve.sem_inc(s_dgo, 1)
                row_aggr(nc, 2 * CT, st, mv).then_inc(s_mv, 1)
                dn.dve_h(dve, u, a + off - 1)
                dve.wait_ge(s_sd, c + 1)
                link(nc.vector.reciprocal(rs[:], sd[:]))
                link(normalize(nc, n1, h, 2 * CT, mv, rs))
                link(nc.vector.tensor_tensor(h[:], n1[:], bc(lg, 2 * CT), ALU.mult))
                link(nc.vector.tensor_tensor(n1[:], h[:], bc(lb, 2 * CT), ALU.add))
                link(nc.vector.tensor_tensor(h[:], n1[:], xin[:], ALU.add))
                row_stats(nc, h, 2 * CT, st, mv, s_d)
                dve.wait_ge(s_d, 2 * c + 2)
                dve.sem_inc(s_dgo, 1)
                row_aggr(nc, 2 * CT, st, mv).then_inc(s_mv2, 1)
                dn.dve_n(dve, u, a + off - 1)
                dve.wait_ge(s_sd2, c + 1)
                link(nc.vector.reciprocal(rs[:], sd[:]))
                dve.wait_ge(s_st, 32 * c)
                normalize(nc, y, h, 2 * CT, mv, rs).then_inc(s_y, 1)
                dve.wait_ge(s_y, c + 1)
                link.done()


def equivariant_phase(nc, g, K, T, dn, off):
    with ExitStack() as ctx:
        a = Place(nc, ctx, "eq")
        A1, B1 = a.sb("A1", [D, D]), a.sb("B1", [D, D])
        fc1 = a.sb("fc1", [8, 64])
        fA, fB, fC = (a.sb(n, [64, D]) for n in ("fA", "fB", "fC"))
        oA, oB, oC = (a.sb(n, [D, D]) for n in ("oA", "oB", "oC"))
        eps = a.sb("eps", [128, 1])
        ring = a.sb("ring", [TP, CT], I32)
        ga = a.sb("ga", [TP, CT, D])
        z, y = a.sb("z", [TP, 2 * CT, D]), a.sb("y", [TP, 2 * CT, D])
        xs, sv, se = (a.sb(n, [D, CE]) for n in ("xs", "sv", "se"))
        u1, u2, u3, u4, u5, u6 = (a.sb(f"u{i}", [D, CE]) for i in range(1, 7))
        S, mid = a.sb("S", [D, CE]), a.sb("mid", [D, CE])
        carry = a.sb("carry", [D, 1])
        dstb, same = a.sb("dstb", [D, CE + 1], I32), a.sb("same", [D, CE])
        ea8 = a.sb("ea8", [8, CE])
        es, ev = a.sb("es", [D, CE]), a.sb("ev", [D, CE])
        hid, sg = a.sb("hid", [64, CE]), a.sb("sg", [64, CE])
        st, mv, sd, rs = a.sb("st", [TP, 2 * CT, 6]), a.sb("mv", [TP, 2 * CT, 2]), a.sb("sd", [TP, 2 * CT]), a.sb("rs", [TP, 2 * CT])
        pX, pP, pQ, pA, pB, pC, pH, pR = (a.ps(n, [128, 512]) for n in ("pX", "pP", "pQ", "pA", "pB", "pC", "pH", "pR"))
        (s_w, s_go, s_ring, s_ga, s_zd, s_dstb, s_ea8, s_es, s_st, s_eps, s_init, s_tA, s_xs, s_gac, s_psH, s_sg, s_hid, s_psW,
         s_psX, s_sv, s_u, s_psO, s_S, s_psR, s_mask, s_mv, s_sd, s_y, s_ch, s_d, s_dgo, s_z) = (
            a.sem(n) for n in ("weights", "go", "ring", "ga", "zd", "dstb", "ea8", "es", "stored", "eps", "init", "tA", "xs",
                               "ga_copied", "psH", "sg", "hid", "psW", "psX", "sv", "u", "psO", "S", "psR", "mask", "mv", "sd",
                               "y", "chain", "stats", "dve_go", "z"))
        block = ctx.enter_context(nc.Block())
        by_lin1 = 1.0 / 32.0 ** 0.5
        by_rest = SILU / (64.0 ** 0.5) / (16.0 ** 0.5) / (64.0 ** 0.5)

        @block.sync
        def _(sp):
            for t, n in ((A1, "L1A"), (B1, "L1B"), (fc1, "fc1"), (fA, "fcA"), (fB, "fcB"), (fC, "fcC"), (oA, "oA"), (oB, "oB"), (oC, "oC")):
                sp.dma_start(t[:], g[n]).then_inc(s_w, 16)

            def load_masks(e0):
                sp.dma_start(dstb[:], g["dst_pad"][:, bass.ds(e0, CE + 1)].broadcast_to([D, CE + 1])).then_inc(s_dstb, 16)

            def load_scalars(e0):
                sp.dma_start(ea8[:], g["ea8T"][:, bass.ds(e0, CE)]).then_inc(s_ea8, 16)

            def load_attr(e0):
                sp.dma_start(es[:], g["ea4T"][0:1, bass.ds(e0, CE)].broadcast_to([D, CE])).then_inc(s_es, 16)
                for j in range(4):
                    sp.dma_start(ev[32 * j:32 * j + 32, :], g["ea4T"][j:j + 1, bass.ds(e0, CE)].broadcast_to([32, CE])).then_inc(s_es, 16)

            def load_targets(e0):
                sp.dma_start(z[:, 0:CT, :], rows_of(T["T2"], e0, CT)).then_inc(s_zd, 16)

            def store(c):
                sp.wait_ge(s_y, c + 1)
                sp.dma_start(rows_of(T["T3"], CE * c, CT), y[:, 0:CT, :]).then_inc(s_st, 16)
                sp.dma_start(rows_of(T["T3"], CE * c + E, CT), y[:, CT:2 * CT, :]).then_inc(s_st, 16)

            load_masks(0)
            load_scalars(0)
            load_attr(0)
            load_targets(0)
            def chunk(u, a, last=False):
                c = 2 * u + a
                dn.load(sp, u, a + off + 1)
                if not last:
                    sp.wait_ge(s_psH, c + 1)
                    load_scalars(CE * c + CE)
                    sp.wait_ge(s_mask, c + 1)
                    load_masks(CE * c + CE)
                    sp.wait_ge(s_u, c + 1)
                    load_attr(CE * c + CE)
                dn.store(sp, u, a + off - LAG_W)
                store(c)
                if not last:
                    load_targets(CE * c + CE)

            chunks(sp, NC - 1)(chunk)
            chunk(0, NC - 1, last=True)
            sp.wait_ge(s_st, 32 * NC)

        @block.gpsimd
        def _(pool):
            nc.gpsimd.memset(eps[:], EPS).then_inc(s_eps, 1)
            @chunks(pool)
            def _(u, a):
                c = 2 * u + a
                pool.wait_ge(s_gac, c)
                pool.wait_ge(s_tA, c)
                pool.sem_inc(s_go, 1)
                gathers(pool, s_go, s_ring, s_ga, ring, K["idxS"], c, c + 1, T["T2"], ga)
                dn.pool_z(pool, u, a + off)
                dn.pool_q(pool, u, a + off - LAG_Y)
                dn.pool_w(pool, u, a + off - LAG_W)

        @block.tensor
        def _(pe):
            pe.wait_ge(s_w, 16 * 9)
            @chunks(pe)
            def _(u, a):
                c = 2 * u + a
                pe.wait_ge(s_ea8, 16 * (c + 1))
                pe.wait_ge(s_hid, c)
                nc.tensor.matmul(pH[0:64, 0:CE], fc1[:], ea8[:], start=True, stop=True).then_inc(s_psH, 1)
                pe.wait_ge(s_ga, 64 * (c + 1))
                for k in range(CT):
                    last = nc.tensor.transpose(pX[:, k * TP:(k + 1) * TP], ga[:, k, :], K["ident"][0:TP, 0:TP])
                last.then_inc(s_tA, 1)
                pe.wait_ge(s_hid, c + 1)
                pe.wait_ge(s_u, c)
                for w, p in ((fA, pA), (fB, pB), (fC, pC)):
                    last = nc.tensor.matmul(p[:, 0:CE], w[:], hid[:], start=True, stop=True)
                last.then_inc(s_psW, 1)
                pe.wait_ge(s_xs, c + 1)
                nc.tensor.matmul(pP[:, 0:CE], A1[:], xs[:], start=True, stop=True)
                nc.tensor.matmul(pQ[:, 0:CE], B1[:], xs[:], start=True, stop=True).then_inc(s_psX, 1)
                pe.wait_ge(s_u, c + 1)
                nc.tensor.matmul(pX[:, 0:CE], oA[:], u2[:], start=True, stop=False)
                nc.tensor.matmul(pX[:, 0:CE], oB[:], u4[:], start=False, stop=False)
                nc.tensor.matmul(pX[:, 0:CE], oC[:], u6[:], start=False, stop=True).then_inc(s_psO, 1)
                pe.wait_ge(s_S, c + 1)
                for k in range(CT):
                    last = nc.tensor.transpose(pR[0:TP, k * D:(k + 1) * D], S[:, k * TP:(k + 1) * TP], K["ident"][:])
                last.then_inc(s_psR, 1)

        @block.scalar
        def _(act):
            act.wait_ge(s_eps, 1)
            @chunks(act)
            def _(u, a):
                c = 2 * u + a
                act.wait_ge(s_psH, c + 1)
                act.wait_ge(s_hid, c)
                nc.scalar.activation(sg[:], pH[0:64, 0:CE], ACT.Sigmoid, scale=1.0 / 8.0 ** 0.5).then_inc(s_sg, 1)
                act.wait_ge(s_tA, c + 1)
                act.wait_ge(s_psX, c)
                nc.scalar.activation(xs[:], pX[:, 0:CE], ACT.Copy).then_inc(s_xs, 1)
                act.wait_ge(s_y, c)
                nc.scalar.activation(z[:, CT:2 * CT, :], ga[:], ACT.Copy).then_inc(s_gac, 1)
                dn.act_root3(act, u, a + off - LAG_Y)
                act.wait_ge(s_psX, c + 1)
                act.wait_ge(s_u, c)
                nc.scalar.activation(sv[:], pP[:, 0:CE], ACT.Copy, scale=by_lin1)
                nc.scalar.activation(se[:], pQ[:, 0:CE], ACT.Copy, scale=by_lin1).then_inc(s_sv, 1)
                dn.act_root4(act, u, a + off - LAG_W)
                dn.act_root1(act, u, a + off - 1)
                dn.act_out(act, u, a + off - LAG_W)
                dn.act_x3(act, u, a + off - LAG_Y)
                act.wait_ge(s_mv, c + 1)
                nc.scalar.activation(sd[:], mv[:, :, 1], ACT.Sqrt, bias=eps[0:TP, :]).then_inc(s_sd, 1)
                dn.act_root2(act, u, a + off - 1)
                dn.act_n(act, u, a + off - 1)

        @block.vector
        def _(dve):
            nc.vector.memset(carry[:], 0.0).then_inc(s_init, 1)
            dve.wait_ge(s_init, 1)
            dve.wait_ge(s_eps, 1)
            @chunks(dve)
            def _(u, a):
                c = 2 * u + a
                link = Chain(dve, s_ch, c, 4)
                dve.wait_ge(s_sg, c + 1)
                dve.wait_ge(s_psW, c)
                nc.vector.scalar_tensor_tensor(out=hid[:], in0=pH[0:64, 0:CE], scalar=1.0 / 8.0 ** 0.5, in1=sg[:],
                                               op0=ALU.mult, op1=ALU.mult).then_inc(s_hid, 1)
                dve.wait_ge(s_dstb, 16 * (c + 1))
                nc.vector.tensor_tensor(same[:], dstb[:, 1:CE + 1], dstb[:, 0:CE], ALU.is_equal).then_inc(s_mask, 1)
                dn.dve_y(dve, u, a + off - LAG_Y)
                dve.wait_ge(s_es, 80 * (c + 1))
                dve.wait_ge(s_psW, c + 1)
                dve.wait_ge(s_psO, c)
                nc.vector.scalar_tensor_tensor(out=u1[:], in0=pA[:, 0:CE], scalar=by_rest, in1=es[:], op0=ALU.mult, op1=ALU.mult)
                nc.vector.scalar_tensor_tensor(out=u3[:], in0=pB[:, 0:CE], scalar=by_rest, in1=ev[:], op0=ALU.mult, op1=ALU.mult)
                link(nc.vector.scalar_tensor_tensor(out=u5[:], in0=pC[:, 0:CE], scalar=by_rest / 3.0 ** 0.5, in1=ev[:],
                                                    op0=ALU.mult, op1=ALU.mult))
                dn.dve_w(dve, u, a + off - LAG_W)
                dve.wait_ge(s_sv, c + 1)
                nc.vector.tensor_tensor(u2[:], u1[:], sv[:], ALU.mult)
                nc.vector.tensor_tensor(u4[:], u3[:], se[:], ALU.mult)
                nc.vector.tensor_tensor(u6[:], u5[:], sv[:], ALU.mult).then_inc(s_u, 1)
                dn.dve_z(dve, u, a + off - 1)
                dve.wait_ge(s_psO, c + 1)
                dve.wait_ge(s_psR, c)
                nc.vector.tensor_tensor_scan(S[:], same[:], pX[:, 0:CE], carry[:], ALU.mult, ALU.add).then_inc(s_S, 1)
                dve.wait_ge(s_S, c + 1)
                nc.vector.tensor_copy(carry[:], S[:, CE - 1:CE])
                dn.dve_x3(dve, u, a + off - LAG_Y)
                dn.dve_o(dve, u, a + off - LAG_W)
                dve.wait_ge(s_zd, 16 * (c + 1))
                dve.wait_ge(s_gac, c + 1)
                dve.wait_ge(s_psR, c + 1)
                link(nc.vector.tensor_tensor(z[:, 0:CT, :], z[:, 0:CT, :], pR[0:TP, :].rearrange("p (k f) -> p k f", k=CT), ALU.add))
                row_stats(nc, z, 2 * CT, st, mv, s_d)
                dve.wait_ge(s_d, c + 1)
                dve.sem_inc(s_dgo, 1)
                row_aggr(nc, 2 * CT, st, mv).then_inc(s_mv, 1)
                dn.dve_h(dve, u, a + off - 1)
                dve.wait_ge(s_sd, c + 1)
                link(nc.vector.reciprocal(rs[:], sd[:]))
                dve.wait_ge(s_st, 32 * c)
                link(normalize(nc, y, z, 2 * CT, mv, rs))
                dve.sem_inc(s_y, 1)
                dn.dve_n(dve, u, a + off - 1)
                link.done()


def hyperedge_phase(nc, g, K, T, tag, table, index, weight, out):
    with ExitStack() as ctx:
        a = Place(nc, ctx, tag)
        W = a.sb("W", [D, D])
        ring = [a.sb(f"ring{p}", [TP, CT], I32) for p in range(2)]
        ga = [a.sb(f"ga{p}", [TP, CT, D]) for p in range(2)]
        y = [a.sb(f"y{p}", [TP, CT, D]) for p in range(2)]
        same = [a.sb(f"same{p}", [D, CE]) for p in range(2)]
        xs, S = a.sb("xs", [D, CE]), a.sb("S", [D, CE])
        carry, zrow = a.sb("carry", [D, 1]), a.sb("zrow", [1, D])
        pX = [a.ps(f"pX{p}", [128, 512]) for p in range(2)]
        pM = [a.ps(f"pM{p}", [128, 512]) for p in range(2)]
        pR = [a.ps(f"pR{p}", [128, 512]) for p in range(2)]
        s_w, s_go, s_ring, s_init, s_tA, s_xs, s_psM, s_S, s_psR, s_y = (
            a.sem(n) for n in ("weights", "go", "ring", "init", "tA", "xs", "psM", "S", "psR", "y"))
        s_ga, s_same, s_st = ([a.sem(f"{n}{p}") for p in range(2)] for n in ("ga", "same", "stored"))
        block = ctx.enter_context(nc.Block())

        @block.sync
        def _(sp):
            if weight:
                sp.dma_start(W[:], g[weight]).then_inc(s_w, 16)

            def load_mask(c, p):
                sp.dma_start(same[p][:], T["dsame"][:, bass.ds(CE * c, CE)].broadcast_to([D, CE])).then_inc(s_same[p], 16)

            load_mask(0, 0)
            load_mask(1, 1)
            @chunks(sp)
            def _(u, a):
                c, p = 2 * u + a, a % 2
                if not (isinstance(c, int) and c + 2 >= NC):
                    sp.wait_ge(s_S, c + 1)
                    load_mask(c + 2, p)
                sp.wait_ge(s_y, c + 1)
                sp.dma_start(rows_of(out, CE * c, CT), y[p][:]).then_inc(s_st[p], 16)
            sp.dma_start(out[E:E + 1, :], zrow[:]).then_inc(s_w, 16)
            sp.wait_ge(s_st[0], 16 * (NC // 2 + 1))
            sp.wait_ge(s_st[1], 16 * (NC // 2))
            sp.wait_ge(s_w, 32 if weight else 16)

        @block.gpsimd
        def _(pool):
            @chunks(pool)
            def _(u, a):
                c, p = 2 * u + a, a % 2
                need(pool, s_tA, c - 1)
                pool.sem_inc(s_go, 1)
                gathers(pool, s_go, s_ring, s_ga[p], ring[p], index, c, c + 1, table, ga[p])

        @block.tensor
        def _(pe):
            if weight:
                pe.wait_ge(s_w, 16)

            def back(u, a):
                c, p = 2 * u + a, a % 2
                pe.wait_ge(s_S, c + 1)
                need(pe, s_y, c)
                for k in range(CT):
                    last = nc.tensor.transpose(pR[p][0:TP, k * D:(k + 1) * D], S[:, k * TP:(k + 1) * TP], K["ident"][:])
                last.then_inc(s_psR, 1)

            @chunks(pe)
            def _(u, a):
                c, p = 2 * u + a, a % 2
                pe.wait_ge(s_ga[p], 64 * (u + a // 2 + 1))
                if weight:
                    need(pe, s_xs, c - 1)
                else:
                    need(pe, s_S, c - 1)
                for k in range(CT):
                    last = nc.tensor.transpose(pX[p][:, k * TP:(k + 1) * TP], ga[p][:, k, :], K["ident"][0:TP, 0:TP])
                last.then_inc(s_tA, 1)
                if not (isinstance(c, int) and c == 0):
                    back(u, a - 1)
                if weight:
                    pe.wait_ge(s_xs, c + 1)
                    need(pe, s_S, c - 1)
                    nc.tensor.matmul(pM[p][:, 0:CE], W[:], xs[:], start=True, stop=True).then_inc(s_psM, 1)
            back(0, NC - 1)

        @block.scalar
        def _(act):
            if weight:
                @chunks(act)
                def _(u, a):
                    c, p = 2 * u + a, a % 2
                    act.wait_ge(s_tA, c + 1)
                    need(act, s_psM, c)
                    nc.scalar.activation(xs[:], pX[p][:, 0:CE], ACT.Copy).then_inc(s_xs, 1)

        @block.vector
        def _(dve):
            nc.vector.memset(carry[:], 0.0)
            nc.vector.memset(zrow[:], 0.0).then_inc(s_init, 1)
            dve.wait_ge(s_init, 1)
            @chunks(dve)
            def _(u, a):
                c, p = 2 * u + a, a % 2
                dve.wait_ge(s_same[p], 16 * (u + a // 2 + 1))
                need(dve, s_psR, c)
                if weight:
                    dve.wait_ge(s_psM, c + 1)
                else:
                    dve.wait_ge(s_tA, c + 1)
                nc.vector.tensor_tensor_scan(S[:], same[p][:], (pM if weight else pX)[p][:, 0:CE], carry[:], ALU.mult, ALU.add).then_inc(s_S, 1)
                dve.wait_ge(s_S, c + 1)
                nc.vector.tensor_copy(carry[:], S[:, CE - 1:CE])
                dve.wait_ge(s_psR, c + 1)
                need(dve, s_st[p], 16 * (u + a // 2))
                for k in range(CT):
                    last = nc.vector.tensor_scalar(y[p][:, k, :], pR[p][0:TP, k * D:(k + 1) * D], K["rdegH"][:, bass.ds(CT * c + k, 1)], None, ALU.mult)
                last.then_inc(s_y, 1)
                dve.wait_ge(s_y, c + 1)


def node_phase(nc, g, K, T, H):
    with ExitStack() as ctx:
        a = Place(nc, ctx, "nd")
        ring, rinx = ([a.sb(f"{n}{p}", [TP, CT], I32) for p in range(2)] for n in ("ring", "rinx"))
        ga, gb = ([a.sb(f"{n}{p}", [TP, CT, D]) for p in range(2)] for n in ("ga", "gb"))
        same, dinv = ([a.sb(f"{n}{p}", [D, CE]) for p in range(2)] for n in ("same", "dinv"))
        S, sq, h = a.sb("S", [D, CE]), a.sb("sq", [D, CE]), [a.sb(f"h{p}", [D, CE]) for p in range(2)]
        cS = a.sb("cS", [D, 1])
        acc = [a.sb(f"acc{p}", [D, 2]) for p in range(2)]
        pX = [a.ps(f"pX{p}", [128, 512]) for p in range(2)]
        s_go, s_ringA, s_ringB, s_init, s_tA, s_S, s_h, s_sq, s_sum = (
            a.sem(n) for n in ("go", "ringA", "ringB", "init", "tA", "S", "h", "sq", "sum"))
        s_ga, s_gb, s_rows, s_st, s_hst = ([a.sem(f"{n}{p}") for p in range(2)] for n in ("ga", "gb", "rows", "stored", "h_stored"))
        block = ctx.enter_context(nc.Block())

        @block.sync
        def _(sp):
            def load_rows(c, p):
                sp.dma_start(same[p][:], T["ssame"][:, bass.ds(CE * c, CE)].broadcast_to([D, CE])).then_inc(s_rows[p], 16)
                sp.dma_start(dinv[p][:], T["dinv"][:, bass.ds(CE * c, CE)].broadcast_to([D, CE])).then_inc(s_rows[p], 16)

            load_rows(0, 0)
            load_rows(1, 1)
            @chunks(sp)
            def _(u, a):
                c, p = 2 * u + a, a % 2
                sp.wait_ge(s_gb[p], 64 * (u + a // 2 + 1))
                sp.dma_start(rows_of(T["TS"], CE * c, CT), gb[p][:]).then_inc(s_st[p], 16)
                if not (isinstance(c, int) and c + 2 >= NC):
                    sp.wait_ge(s_h, c + 1)
                    load_rows(c + 2, p)
            for s in s_st:
                sp.wait_ge(s, 16 * (NC // 2 + (s is s_st[0])))

        @block.gpsimd
        def _(pool):
            @chunks(pool)
            def _(u, a):
                c, p = 2 * u + a, a % 2
                need(pool, s_tA, c - 1)
                pool.sem_inc(s_go, 1)
                gathers(pool, s_go, s_ringA, s_ga[p], ring[p], K["s_idxE"], c, c + 1, T["TE"], ga[p])
                need(pool, s_st[p], 16 * (u + a // 2))
                pool.sem_inc(s_go, 1)
                gathers(pool, s_go, s_ringB, s_gb[p], rinx[p], K["s_idxS"], c, c + 1, T["T3"], gb[p])

        @block.tensor
        def _(pe):
            @chunks(pe)
            def _(u, a):
                c, p = 2 * u + a, a % 2
                pe.wait_ge(s_ga[p], 64 * (u + a // 2 + 1))
                need(pe, s_S, c - 1)
                for k in range(CT):
                    last = nc.tensor.transpose(pX[p][:, k * TP:(k + 1) * TP], ga[p][:, k, :], K["ident"][0:TP, 0:TP])
                last.then_inc(s_tA, 1)

        @block.scalar
        def _(act):
            @chunks(act)
            def _(u, a):
                c, p = 2 * u + a, a % 2
                act.wait_ge(s_h, c + 1)
                need(act, s_sum, c - 1)
                need(act, s_sq, c)
                nc.scalar.activation(sq[:], h[p][:], ACT.Square, accum_out=acc[p][:, 1:2])
                nc.scalar.activation(H["h"][:, bass.ds(CE * c, CE)], h[p][:], ACT.Copy).then_inc(s_sq, 1)

        @block.vector
        def _(dve):
            nc.vector.memset(H["sum"][:], 0.0)
            nc.vector.memset(cS[:], 0.0).then_inc(s_init, 1)
            dve.wait_ge(s_init, 1)

            def total(u, a):
                c, p = 2 * u + a, a % 2
                dve.wait_ge(s_sq, c + 1)
                need(dve, s_sum, c)
                nc.vector.tensor_tensor(H["sum"][:], H["sum"][:], acc[p][:], ALU.add).then_inc(s_sum, 1)

            @chunks(dve)
            def _(u, a):
                c, p = 2 * u + a, a % 2
                dve.wait_ge(s_rows[p], 32 * (u + a // 2 + 1))
                dve.wait_ge(s_tA, c + 1)
                need(dve, s_h, c)
                nc.vector.tensor_tensor_scan(S[:], same[p][:], pX[p][:, 0:CE], cS[:], ALU.mult, ALU.add).then_inc(s_S, 1)
                if not (isinstance(c, int) and c == 0):
                    total(u, a - 1)
                dve.wait_ge(s_S, c + 1)
                nc.vector.tensor_copy(cS[:], S[:, CE - 1:CE])
                nc.vector.scalar_tensor_tensor(out=h[p][:], in0=S[:], scalar=1.0, in1=dinv[p][:],
                                               op0=ALU.mult, op1=ALU.mult, accum_out=acc[p][:, 0:1]).then_inc(s_h, 1)
            total(0, NC - 1)


def batchnorm_phase(nc, g, K, T, H):
    with ExitStack() as ctx:
        a = Place(nc, ctx, "bn")
        W = a.sb("W", [D, D])
        v = a.sb("v", [D, 12])
        eps, b2 = a.sb("eps", [128, 1]), a.sb("b2", [TP, D])
        hp, oF = a.sb("hp", [D, CE]), a.sb("oF", [D, CE])
        y, x, z, o = ([a.sb(f"{n}{p}", [TP, CT, D]) for p in range(2)] for n in ("y", "x", "z", "o"))
        rout = [a.sb(f"rout{p}", [TP, CT], I32) for p in range(2)]
        st, mv, tsd, trs = a.sb("st", [TP, CT, 6]), a.sb("mv", [TP, CT, 2]), a.sb("tsd", [TP, CT]), a.sb("trs", [TP, CT])
        pM, pR = (([a.ps(f"{n}{p}", [128, 512]) for p in range(2)]) for n in ("pM", "pR"))
        s_w, s_ch, s_a, s_sd, s_hp, s_psM, s_oF, s_psR, s_y, s_go, s_ring, s_z, s_d, s_dgo, s_mv, s_tsd, s_rs, s_o = (
            a.sem(n) for n in ("weights", "chain", "affine", "sd", "hp", "psM", "oF", "psR", "y", "go", "ring", "z", "stats", "dve_go",
                               "mv", "target_sd", "rs", "o"))
        s_st, s_x, s_out = ([a.sem(f"{n}{p}") for p in range(2)] for n in ("stored", "x", "out"))
        block = ctx.enter_context(nc.Block())
        b1, gam, bet = K["cols"][:, 5:6], K["cols"][:, 6:7], K["cols"][:, 7:8]
        m, m2, var, sd, rs, scale, t, bias = (v[:, i:i + 1] for i in range(8))

        @block.sync
        def _(sp):
            sp.dma_start(W[:], g["W2"]).then_inc(s_w, 16)
            sp.dma_start(b2[:], g["rowv"][4:5, :].broadcast_to([TP, D])).then_inc(s_w, 16)
            for p in range(2):
                sp.dma_start(x[p][:], rows_of(T["T3"], CE * p, CT)).then_inc(s_x[p], 16)
            @chunks(sp)
            def _(u, a):
                c, p = 2 * u + a, a % 2
                sp.wait_ge(s_y, c + 1)
                sp.dma_start(rows_of(T["TH"], CE * c, CT), y[p][:]).then_inc(s_st[p], 16)
                if not (isinstance(c, int) and c + 2 >= NC):
                    sp.wait_ge(s_z, c + 1)
                    sp.dma_start(x[p][:], rows_of(T["T3"], CE * c + 2 * CE, CT)).then_inc(s_x[p], 16)
            for s in s_st:
                sp.wait_ge(s, 16 * (NC // 2 + (s is s_st[0])))

        @block.gpsimd
        def _(pool):
            @chunks(pool)
            def _(u, a):
                c, p = 2 * u + a, a % 2
                need(pool, s_out[p], 64 * (u + a // 2))
                pool.sem_inc(s_go, 1)
                nc.gpsimd.tensor_copy(rout[p][:], K["dst_end"][:, bass.ds(CT * c, CT)]).then_inc(s_ring, 1)
                pool.wait_ge(s_ring, c + 1)
                pool.wait_ge(s_o, c + 1)
                pool.sem_inc(s_go, 1)
                for k in range(CT):
                    nc.gpsimd.indirect_dma_start(out=T["out"], out_offset=bass.IndirectOffsetOnAxis(ap=rout[p][:, k:k + 1], axis=0),
                                                 in_=o[p][:, k, :], in_offset=None, bounds_check=N - 1, oob_is_err=False).then_inc(s_out[p], 16)
            for s in s_out:
                pool.wait_ge(s, 64 * (NC // 2 + (s is s_out[0])))

        @block.vector
        def _(dve):
            link = Chain(dve, s_ch)
            nc.vector.memset(eps[:], EPS)
            link(nc.vector.tensor_scalar(m, H["sum"][:, 0:1], 1.0 / N, None, ALU.mult))
            link(nc.vector.tensor_tensor(m2, m, m, ALU.mult))
            nc.vector.scalar_tensor_tensor(out=var, in0=H["sum"][:, 1:2], scalar=1.0 / N, in1=m2, op0=ALU.mult, op1=ALU.subtract).then_inc(s_a, 1)
            dve.wait_ge(s_sd, 1)
            link(nc.vector.reciprocal(rs, sd))
            link(nc.vector.tensor_tensor(scale, rs, gam, ALU.mult))
            link(nc.vector.tensor_tensor(t, m, scale, ALU.mult))
            nc.vector.tensor_tensor(bias, bet, t, ALU.subtract).then_inc(s_a, 1)
            dve.wait_ge(s_w, 32)
            @chunks(dve)
            def _(u, a):
                c, p = 2 * u + a, a % 2
                dve.wait_ge(s_x[p], 16 * (u + a // 2 + 1))
                need(dve, s_o, c - 1)
                nc.vector.tensor_tensor(z[p][:], x[p][:], bc(b2, CT), ALU.add).then_inc(s_z, 1)
                dve.wait_ge(s_z, c + 1)
                row_stats(nc, z[p], CT, st, mv, s_d)
                dve.wait_ge(s_d, c + 1)
                need(dve, s_o, c)
                dve.sem_inc(s_dgo, 1)
                row_aggr(nc, CT, st, mv).then_inc(s_mv, 1)
                dve.wait_ge(s_psR, c + 1)
                need(dve, s_st[p], 16 * (u + a // 2))
                nc.vector.tensor_copy(y[p][:], pR[p][0:TP, :].rearrange("p (k f) -> p k f", k=CT)).then_inc(s_y, 1)
                dve.wait_ge(s_tsd, c + 1)
                nc.vector.reciprocal(trs[:], tsd[:]).then_inc(s_rs, 1)
                dve.wait_ge(s_rs, c + 1)
                need(dve, s_out[p], 64 * (u + a // 2))
                normalize(nc, o[p], z[p], CT, mv, trs).then_inc(s_o, 1)
                dve.wait_ge(s_o, c + 1)

        @block.scalar
        def _(act):
            act.wait_ge(s_a, 1)
            nc.scalar.activation(sd, var, ACT.Sqrt, bias=eps[:]).then_inc(s_sd, 1)
            act.wait_ge(s_a, 2)
            @chunks(act)
            def _(u, a):
                c, p = 2 * u + a, a % 2
                need(act, s_psM, c)
                nc.scalar.activation(hp[:], H["h"][:, bass.ds(CE * c, CE)], ACT.Identity, bias=bias, scale=scale).then_inc(s_hp, 1)
                act.wait_ge(s_psM, c + 1)
                need(act, s_psR, c)
                nc.scalar.activation(oF[:], pM[p][:, 0:CE], ACT.Copy).then_inc(s_oF, 1)
                act.wait_ge(s_mv, c + 1)
                nc.scalar.activation(tsd[:], mv[:, :, 1], ACT.Sqrt, bias=eps[0:TP, :]).then_inc(s_tsd, 1)

        @block.tensor
        def _(pe):
            pe.wait_ge(s_w, 32)
            @chunks(pe)
            def _(u, a):
                c, p = 2 * u + a, a % 2
                pe.wait_ge(s_hp, c + 1)
                need(pe, s_oF, c - 1)
                nc.tensor.matmul(pM[p][:, 0:CE], W[:], hp[:], start=True, stop=True).then_inc(s_psM, 1)
                pe.wait_ge(s_oF, c + 1)
                need(pe, s_y, c - 1)
                for k in range(CT):
                    last = nc.tensor.transpose(pR[p][0:TP, k * D:(k + 1) * D], oF[:, k * TP:(k + 1) * TP], K["ident"][:])
                last.then_inc(s_psR, 1)


def result_phase(nc, g, K, T):
    with ExitStack() as ctx:
        a = Place(nc, ctx, "rs")
        eps = a.sb("eps", [128, 1])
        ring, rout = ([a.sb(f"{n}{p}", [TP, CT], I32) for p in range(2)] for n in ("ring", "rout"))
        ga, x, y = ([a.sb(f"{n}{p}", [TP, CT, D]) for p in range(2)] for n in ("ga", "x", "y"))
        same, dinv = ([a.sb(f"{n}{p}", [D, CE]) for p in range(2)] for n in ("same", "dinv"))
        z = a.sb("z", [TP, CT, D])
        S, o, oF = (a.sb(n, [D, CE]) for n in ("S", "o", "oF"))
        cS = a.sb("cS", [D, 1])
        st, mv, sd, rs = a.sb("st", [TP, CT, 6]), a.sb("mv", [TP, CT, 2]), a.sb("sd", [TP, CT]), a.sb("rs", [TP, CT])
        pX, pR = ([a.ps(f"{n}{p}", [128, 512]) for p in range(2)] for n in ("pX", "pR"))
        (s_go, s_ringA, s_ringO, s_init, s_eps, s_tA, s_S, s_o, s_oF, s_psR, s_z, s_d, s_dgo, s_mv, s_sd, s_y, s_rs) = (
            a.sem(n) for n in ("go", "ringA", "ringO", "init", "eps", "tA", "S", "o", "oF", "psR", "z", "stats", "dve_go", "mv", "sd", "y", "rs"))
        s_ga, s_x, s_rows, s_out = ([a.sem(f"{n}{p}") for p in range(2)] for n in ("ga", "x", "rows", "out"))
        block = ctx.enter_context(nc.Block())

        @block.sync
        def _(sp):
            def load_rows(c, p):
                sp.dma_start(same[p][:], T["ssame"][:, bass.ds(CE * c, CE)].broadcast_to([D, CE])).then_inc(s_rows[p], 16)
                sp.dma_start(dinv[p][:], T["dinv"][:, bass.ds(CE * c, CE)].broadcast_to([D, CE])).then_inc(s_rows[p], 16)

            def load_states(c, p):
                sp.dma_start(x[p][:], rows_of(T["TS"], CE * c, CT)).then_inc(s_x[p], 16)

            for p in range(2):
                load_rows(p, p)
                load_states(p, p)
            @chunks(sp, NC - 2)
            def _(u, a):
                c, p = 2 * u + a, a % 2
                sp.wait_ge(s_o, c + 1)
                load_rows(c + 2, p)
                sp.wait_ge(s_z, c + 1)
                load_states(c + 2, p)

        @block.gpsimd
        def _(pool):
            nc.gpsimd.memset(eps[:], EPS).then_inc(s_eps, 1)

            def scatter(u, a):
                c, p = 2 * u + a, a % 2
                need(pool, s_out[p], 64 * (u + a // 2))
                pool.sem_inc(s_go, 1)
                nc.gpsimd.tensor_copy(rout[p][:], K["src_end"][:, bass.ds(CT * c, CT)]).then_inc(s_ringO, 1)
                pool.wait_ge(s_ringO, c + 1)
                pool.wait_ge(s_y, c + 1)
                pool.sem_inc(s_go, 1)
                for k in range(CT):
                    nc.gpsimd.indirect_dma_start(out=T["out"], out_offset=bass.IndirectOffsetOnAxis(ap=rout[p][:, k:k + 1], axis=0),
                                                 in_=y[p][:, k, :], in_offset=None, bounds_check=N - 1, oob_is_err=False).then_inc(s_out[p], 16)

            @chunks(pool)
            def _(u, a):
                c, p = 2 * u + a, a % 2
                need(pool, s_tA, c - 1)
                pool.sem_inc(s_go, 1)
                gathers(pool, s_go, s_ringA, s_ga[p], ring[p], K["s_idxE"], c, c + 1, T["TE2"], ga[p])
                if not (isinstance(c, int) and c == 0):
                    scatter(u, a - 1)
            scatter(0, NC - 1)
            for s in s_out:
                pool.wait_ge(s, 64 * (NC // 2 + (s is s_out[0])))

        @block.tensor
        def _(pe):
            @chunks(pe)
            def _(u, a):
                c, p = 2 * u + a, a % 2
                pe.wait_ge(s_ga[p], 64 * (u + a // 2 + 1))
                need(pe, s_S, c - 1)
                for k in range(CT):
                    last = nc.tensor.transpose(pX[p][:, k * TP:(k + 1) * TP], ga[p][:, k, :], K["ident"][0:TP, 0:TP])
                last.then_inc(s_tA, 1)
                pe.wait_ge(s_oF, c + 1)
                need(pe, s_z, c - 1)
                for k in range(CT):
                    last = nc.tensor.transpose(pR[p][0:TP, k * D:(k + 1) * D], oF[:, k * TP:(k + 1) * TP], K["ident"][:])
                last.then_inc(s_psR, 1)

        @block.scalar
        def _(act):
            act.wait_ge(s_eps, 1)
            @chunks(act)
            def _(u, a):
                c = 2 * u + a
                act.wait_ge(s_o, c + 1)
                need(act, s_psR, c)
                nc.scalar.activation(oF[:], o[:], ACT.Identity, bias=K["cols"][:, 8:9]).then_inc(s_oF, 1)
                act.wait_ge(s_mv, c + 1)
                nc.scalar.activation(sd[:], mv[:, :, 1], ACT.Sqrt, bias=eps[0:TP, :]).then_inc(s_sd, 1)

        @block.vector
        def _(dve):
            nc.vector.memset(cS[:], 0.0).then_inc(s_init, 1)
            dve.wait_ge(s_init, 1)
            @chunks(dve)
            def _(u, a):
                c, p = 2 * u + a, a % 2
                dve.wait_ge(s_rows[p], 32 * (u + a // 2 + 1))
                dve.wait_ge(s_tA, c + 1)
                need(dve, s_o, c)
                nc.vector.tensor_tensor_scan(S[:], same[p][:], pX[p][:, 0:CE], cS[:], ALU.mult, ALU.add).then_inc(s_S, 1)
                dve.wait_ge(s_S, c + 1)
                need(dve, s_oF, c)
                nc.vector.tensor_copy(cS[:], S[:, CE - 1:CE])
                nc.vector.tensor_tensor(o[:], S[:], dinv[p][:], ALU.mult).then_inc(s_o, 1)
                dve.wait_ge(s_x[p], 16 * (u + a // 2 + 1))
                dve.wait_ge(s_psR, c + 1)
                need(dve, s_y, c)
                nc.vector.tensor_tensor(z[:], x[p][:], pR[p][0:TP, :].rearrange("p (k f) -> p k f", k=CT), ALU.add).then_inc(s_z, 1)
                dve.wait_ge(s_z, c + 1)
                row_stats(nc, z, CT, st, mv, s_d)
                dve.wait_ge(s_d, c + 1)
                dve.sem_inc(s_dgo, 1)
                row_aggr(nc, CT, st, mv).then_inc(s_mv, 1)
                dve.wait_ge(s_sd, c + 1)
                nc.vector.reciprocal(rs[:], sd[:]).then_inc(s_rs, 1)
                dve.wait_ge(s_rs, c + 1)
                need(dve, s_out[p], 64 * (u + a // 2))
                normalize(nc, y[p], z, CT, mv, rs).then_inc(s_y, 1)
                dve.wait_ge(s_y, c + 1)


def source_state(nc, ctx):
    def sb(name, shape, dt=F32):
        return ctx.enter_context(nc.sbuf_tensor(f"src_{name}", shape, dt))

    return {"h": sb("h", [D, E]), "sum": sb("sum", [D, 2])}


def layout(I):
    import numpy as np
    c = lambda v: np.ascontiguousarray(v)
    col = lambda v: c(v.reshape(NT, TP).T)
    src, dst = np.asarray(I["src"]), np.asarray(I["dst"])
    w = {k: np.asarray(v) for k, v in I.items()}
    end = np.full(1, -1, dst.dtype)
    f = np.float32
    U = 32
    A = np.zeros((D, D), f)
    B = np.zeros((D, D), f)
    A[0:U, 0:U] = w["L2_gnn_w_lin1_s"]
    for i in range(3):
        A[U + i:D:3, U * (i + 1):U * (i + 2)] = w["L2_gnn_w_lin1_v"]
        B[0:U, U * (i + 1):U * (i + 2)] = w["L2_gnn_w_lin1_s"]
    fc = w["L2_gnn_fc_w2"].reshape(64, 4, U)
    zero = np.zeros((64, U), f)
    fa = np.concatenate([fc[:, 0], fc[:, 2], fc[:, 2], fc[:, 2]], 1)
    fb = np.concatenate([zero, fc[:, 1], fc[:, 1], fc[:, 1]], 1)
    fcc = np.concatenate([zero, fc[:, 3], fc[:, 3], fc[:, 3]], 1)
    oA, oB, oC = (np.zeros((D, D), f) for _ in range(3))
    oA[0:U, 0:U] = w["L2_gnn_w_lin2_s"][0:U]
    for i in range(3):
        r = slice(U * (i + 1), U * (i + 2))
        oA[r, U + i:D:3] = w["L2_gnn_w_lin2_v"][U:2 * U]
        oB[r, U + i:D:3] = w["L2_gnn_w_lin2_v"][0:U]
        oC[r, 0:U] = w["L2_gnn_w_lin2_s"][U:2 * U]
    ptab = np.zeros((N, 2), f)
    ptab[:, 0] = E
    ptab[0:NH, 1] = w["L3_gnn_hyperedge_weight"]
    names = ("L0_gnn_bq", "L0_gnn_bk", "L0_gnn_bv", "L0_gnn_bo", "L1_gnn_msg_b", "L3_gnn_b1", "L3_gnn_gamma", "L3_gnn_beta", "L3_gnn_b2")
    rows = ("L0_gnn_bo", "L1_gnn_upd_b", "L1_gnn_ln_g", "L1_gnn_ln_b", "L3_gnn_b2")
    return dict(
        x=c(w["x"]), src_col=col(src), dst_col=col(dst), dstn_col=col(np.concatenate([dst[1:], end])),
        src_row=c(src[None]), dst_pad=c(np.concatenate([end, dst, end])[None]), type_row=c(w["edge_type_16"][None]),
        ea4T=c(w["edge_attr_4"].T), ea8T=c(w["edge_attr_8"].T), ptab0=ptab,
        tri=np.triu(np.ones((128, 128), f), 1), ident=np.eye(128, dtype=f), identb=np.eye(128, dtype=mybir.dt.np(BF16)),
        heads=(np.kron(np.eye(8), np.ones((16, 16))) * 0.25).astype(f), expand=np.kron(np.eye(8), np.ones((1, 16))).astype(f),
        cols=c(np.stack([w[n] for n in names], 1)), rowv=c(np.stack([w[n] for n in rows])),
        Wq=c(w["L0_gnn_Wq"]), Wk=c(w["L0_gnn_Wk"]), Wv=c(w["L0_gnn_Wv"]), Wo=c(w["L0_gnn_Wo"]),
        Wmx=c(w["L1_gnn_msg_W"][:, 0:D].T), Wme=c(w["L1_gnn_msg_W"][:, D:].T), embT=c(w["L1_gnn_edge_emb_W"].T), Wu=c(w["L1_gnn_upd_W"].T),
        L1A=A, L1B=B, fc1=c(w["L2_gnn_fc_w1"]), fcA=c(fa), fcB=c(fb), fcC=c(fcc), oA=oA, oB=oB, oC=oC,
        W1=c(w["L3_gnn_W1"].T), W2=c(w["L3_gnn_W2"].T),
    )


TABLES = dict(ptab=[N, 2], S4=[E, 4], srow=[1, E + 2], T1=[2 * E, D], T2=[2 * E, D], T3=[2 * E, D],
              TE=[E + 1, D], TH=[E, D], TE2=[E + 1, D], TS=[E, D],
              dsame=[1, E], ssame=[1, E], dinv=[1, E])


def program(nc, g, out):
    with ExitStack() as ctx:
        T = {n: nc.dram_tensor(f"table_{n}", tuple(s), F32).ap() for n, s in TABLES.items()}
        T["ptab1"] = T["ptab"].rearrange("a (b c) -> (a b) c", c=1)
        T["out"] = out
        K = constants(nc, ctx)
        index_phase(nc, g, K, T)
        with ExitStack() as inner:
            dn = Dense(nc, inner, g, T)
            dense_alone(nc, dn, 0, LAG_W)
            attention_phase(nc, g, K, T, dn, LAG_W)
            message_phase(nc, g, K, T, dn, LAG_W + NC)
            equivariant_phase(nc, g, K, T, dn, LAG_W + 2 * NC)
            dense_alone(nc, dn, LAG_W + 3 * NC, DS + LAG_W + 1)
        slots_phase(nc, g, K, T)
        hyperedge_phase(nc, g, K, T, "hA", T["T3"], K["idxS"], "W1", T["TE"])
        with ExitStack() as inner:
            H = source_state(nc, inner)
            node_phase(nc, g, K, T, H)
            batchnorm_phase(nc, g, K, T, H)
            hyperedge_phase(nc, g, K, T, "hB", T["TH"], K["send"], None, T["TE2"])
            result_phase(nc, g, K, T)


def kernel(**inputs):
    import concourse.bacc as bacc
    from concourse.bass_utils import run_bass_kernel_spmd

    nc = bacc.Bacc("TRN2", target_bir_lowering=False, num_devices=1)
    arrays = layout(inputs)
    g = {n: nc.dram_tensor(n, v.shape, mybir.dt.from_np(v.dtype), kind="ExternalInput").ap() for n, v in arrays.items()}
    out = nc.dram_tensor("result", (N, D), F32, kind="ExternalOutput").ap()
    program(nc, g, out)
    return run_bass_kernel_spmd(nc, [arrays], core_ids=[0]).results[0]["result"]
```

```python
from contextlib import ExitStack

import numpy as np
import concourse.bass as bass
from concourse import mybir

F32 = mybir.dt.float32
BF16 = mybir.dt.bfloat16
I32 = mybir.dt.int32
ALU = mybir.AluOpType
ACT = mybir.ActivationFunctionType
AX = mybir.AxisListType.X

N, D, E = 50000, 128, 12500
NH = 10000
TP = 125
NT = E // TP
CT = 4
CE = CT * TP
NC = E // CE
EPS = 1e-5
LO = (N + 127) // 128
FAR = 1 << 20
NEG = 1.0e30
SILU = 1.6791767923989418
RING = 4


class Chain:

    def __init__(self, eng, sem, i=0, per=0):
        self.eng, self.sem, self.base, self.per, self.n = eng, sem, i * per, per, 0

    def __call__(self, ins):
        self.n += 1
        ins.then_inc(self.sem, 1)
        self.eng.wait_ge(self.sem, self.base + self.n)

    def done(self):
        assert self.n == self.per, (self.n, self.per)


def steps(eng, n):
    def run(body):
        body(0)
        if n > 1:
            with eng.Fori(1, n) as i:
                body(i)
    return run


def chunks(eng, n=NC):
    def run(body):
        body(0, 0)
        pairs = (n - 3) // 2
        with eng.Fori(0, pairs) as u:
            body(u, 1)
            body(u, 2)
        for c in range(2 * pairs + 1, n):
            body(0, c)
    return run


class Place:

    def __init__(self, nc, ctx, tag):
        self.nc, self.ctx, self.tag, self.sems = nc, ctx, tag, []
        ctx.callback(self.clear)

    def sb(self, name, shape, dt=F32):
        return self.ctx.enter_context(self.nc.sbuf_tensor(f"{self.tag}_{name}", shape, dt))

    def ps(self, name, shape, dt=F32):
        return self.ctx.enter_context(self.nc.psum_tensor(f"{self.tag}_{name}", shape, dt))

    def sem(self, name):
        self.sems.append(self.nc.alloc_semaphore(f"{self.tag}_{name}"))
        return self.sems[-1]

    def clear(self):
        self.nc.clear_and_free_semaphores(self.sems)
        self.nc.all_engine_barrier()


def constants(nc, ctx):
    def sb(name, shape, dt=F32):
        return ctx.enter_context(nc.sbuf_tensor(f"k_{name}", shape, dt))

    K = {n: sb(n, s) for n, s in (("ident", [128, 128]), ("heads", [128, 128]), ("expand", [8, 128]), ("isH", [TP, NT]), ("rdeg", [TP, NT]), ("rdegH", [TP, NT]))}
    K["identb"] = sb("identb", [128, 128], BF16)
    K["iota_i"] = sb("iota_i", [128, LO], I32)
    K["cols"] = sb("cols", [D, 9])
    for n in ("dst_end", "clip", "slot", "send", "idxS", "s_idxE", "s_idxS", "src_end"):
        K[n] = sb(n, [TP, NT], I32)
    K["pay"] = sb("pay", [TP, NT, 4])
    return K


def rows_of(table, first, n):
    return table[bass.ds(first, n * TP), :].rearrange("(t p) f -> p t f", p=TP)


class RowRuns:

    def __init__(self, nc, a, ps, ps2):
        self.nc, self.ps, self.ps2 = nc, ps, ps2
        self.run, self.pref, self.zeros = (a.sb(n, [NT, TP]) for n in ("run", "pref", "zeros"))
        self.lastr, self.crow, self.ccol = a.sb("lastr", [1, 2, NT]), a.sb("crow", [1, NT + 1]), a.sb("ccol", [NT, 1])
        self.s_runs, self.s_runT, self.s_carry, self.s_carryT = (a.sem(n) for n in ("runs", "runs_rows", "carry", "carry_col"))

    def init(self):
        self.nc.vector.memset(self.zeros[:], 0.0)
        self.nc.vector.memset(self.crow[:], 0.0)

    def rows(self, mask, value):
        nc = self.nc
        nc.vector.tensor_tensor_scan(self.run[:], mask[:], value[:], 0.0, ALU.mult, ALU.add)
        nc.vector.tensor_tensor_scan(self.pref[:], mask[:], self.zeros[:], 1.0, ALU.mult, ALU.add).then_inc(self.s_runs, 1)

    def finish(self, dve, link):
        nc = self.nc
        dve.wait_ge(self.s_runT, 1)
        link(nc.vector.tensor_copy(self.lastr[:], self.ps[0:1, 0:2 * NT].rearrange("p (k t) -> p k t", k=2)))
        nc.vector.tensor_tensor_scan(self.crow[:, 1:NT + 1], self.lastr[:, 1, :], self.lastr[:, 0, :], 0.0, ALU.mult, ALU.add).then_inc(self.s_carry, 1)
        dve.wait_ge(self.s_carryT, 1)
        link(nc.vector.tensor_copy(self.ccol[:], self.ps2[0:NT, 0:1]))
        link(nc.vector.scalar_tensor_tensor(out=self.run[:], in0=self.pref[:], scalar=self.ccol[:, 0:1], in1=self.run[:],
                                            op0=ALU.mult, op1=ALU.add))

    def tensor(self, pe, ident):
        nc = self.nc
        pe.wait_ge(self.s_runs, 1)
        nc.tensor.transpose(self.ps[0:1, 0:NT], self.run[:, TP - 1:TP], ident[0:NT, 0:NT])
        nc.tensor.transpose(self.ps[0:1, NT:2 * NT], self.pref[:, TP - 1:TP], ident[0:NT, 0:NT]).then_inc(self.s_runT, 1)
        pe.wait_ge(self.s_carry, 1)
        nc.tensor.transpose(self.ps2[0:NT, 0:1], self.crow[:, 0:NT], ident[0:1, 0:1]).then_inc(self.s_carryT, 1)


def index_phase(nc, g, K, T):
    with ExitStack() as ctx:
        a = Place(nc, ctx, "ix")
        src, dst, dstn = (a.sb(n, [TP, NT], I32) for n in ("src", "dst", "dstn"))
        srcf, dstf, dstnf, hif, lof, ef, tmp, endf = (
            a.sb(n, [TP, NT]) for n in ("srcf", "dstf", "dstnf", "hif", "lof", "ef", "tmp", "endf"))
        hii, loi, ei, scatI = (a.sb(n, [TP, NT], I32) for n in ("hii", "loi", "ei", "scatI"))
        iot = a.sb("iot", [TP, LO])
        tri, triL = a.sb("tri", [128, 128]), a.sb("triL", [TP, TP])
        ohi, olo = a.sb("ohi", [TP, RING, 128], BF16), a.sb("olo", [TP, RING, LO], BF16)
        zero = a.sb("zero", [TP, LO], BF16)
        hiT, hiTb = a.sb("hiT", [128, 2, TP]), a.sb("hiTb", [128, 2, TP], BF16)
        endh, endl = a.sb("endh", [128, LO], BF16), a.sb("endl", [128, LO], BF16)
        cnt, inc, end = a.sb("cnt", [128, LO]), a.sb("inc", [128, LO]), a.sb("end", [128, LO])
        cur = a.sb("cur", [128, 2, LO])
        ones, start = a.sb("ones", [128, LO]), a.sb("start", [128, LO])
        offs = a.sb("offs", [128, 1])
        junk = a.sb("junk", [TP, 2, 3, LO])
        srcb = a.sb("srcb", [TP, 2, RING * TP], I32)
        hit = a.sb("hit", [TP, 3, 2, RING])
        slotf, sendf = a.sb("slotf", [TP, NT]), a.sb("sendf", [TP, NT])
        ri, re, rj, pq = ([a.sb(f"{n}{p}", s, d) for p in range(2)]
                          for n, s, d in (("ri", [TP, CT], I32), ("re", [TP, CT], F32), ("rj", [TP, CT], I32), ("pq", [TP, CT, 2], F32)))
        posS, idxSf = a.sb("posS", [TP, NT]), a.sb("idxSf", [TP, NT])
        drow, drowP, rowD, rowQ = (a.sb(n, [NT, TP], t) for n, t in (("drow", I32), ("drowP", I32), ("rowD", F32), ("rowQ", F32)))

        pC = a.ps("pC", [128, 512])
        pL, pE = (a.ps(n, [128, 2, 512]) for n in ("pL", "pE"))
        pT = a.ps("pT", [128, 2, 1024], BF16)
        pR = a.ps("pR", [128, 512])

        rr = RowRuns(nc, a, pC, pR)
        one = a.sb("one", [NT, TP])
        s_deg, s_degT = a.sem("deg"), a.sem("deg_cols")
        s_in, s_tab, s_cst, s_dv, s_pl, s_dsame, s_ds = (a.sem(n) for n in ("in", "tab", "cst", "dvchain", "plchain", "dsame", "dsame_stored"))
        s_ends_idx, s_ringA, s_ringB, s_pos = (a.sem(n) for n in ("ends_idx", "ringA", "ringB", "pos"))
        s_ohA, s_hist, s_hist_all, s_tot, s_off, s_first = (a.sem(n) for n in ("ohA", "hist", "hist_all", "tot", "off", "first"))
        s_acc, s_cur, s_ohB, s_tr, s_hiT, s_look, s_used, s_hit = (
            a.sem(n) for n in ("acc", "cur", "ohB", "transposed", "hiT", "looked", "lookup_used", "hit"))
        s_srcb, s_scat, s_gat = ([a.sem(f"{n}{p}") for p in range(2)] for n in ("srcb", "scat", "gat"))
        s_go = a.sem("go")
        block = ctx.enter_context(nc.Block())
        NR = NT // RING

        @block.sync
        def _(sp):
            for t, d in ((src, g["src_col"]), (dst, g["dst_col"]), (dstn, g["dstn_col"]),
                         (drow, g["dst_pad"][:, 1:E + 1].rearrange("a (t p) -> (a t) p", p=TP)),
                         (drowP, g["dst_pad"][:, 0:E].rearrange("a (t p) -> (a t) p", p=TP))):
                sp.dma_start(t[:], d).then_inc(s_in, 16)
            sp.dma_start(tri[:], g["tri"]).then_inc(s_in, 16)
            sp.dma_start(triL[:], g["tri"][0:TP, 0:TP]).then_inc(s_in, 16)
            for name in ("ident", "identb", "heads", "expand", "cols"):
                sp.dma_start(K[name][:], g[name]).then_inc(s_in, 16)
            sp.dma_start(T["ptab"].rearrange("(a b) c -> a (b c)", a=16), g["ptab0"].rearrange("(a b) c -> a (b c)", a=16)).then_inc(s_tab, 16)

            def load_sources(first, p):
                sp.dma_start(srcb[:, p, :], g["src_row"][:, bass.ds(first, RING * TP)].broadcast_to([TP, RING * TP])).then_inc(s_srcb[p], 16)

            load_sources(0, 0)
            load_sources(RING * TP, 1)
            sp.wait_ge(s_dsame, 1)
            sp.dma_start(T["dsame"].rearrange("a (t p) -> (a t) p", p=TP), rowD[:]).then_inc(s_ds, 16)
            sp.dma_start(T["dpen"].rearrange("a (t p) -> (a t) p", p=TP), rowQ[:]).then_inc(s_ds, 16)
            @chunks(sp, NR - 2)
            def _(u, a):
                r = 2 * u + a
                sp.wait_ge(s_used, RING * r + RING)
                load_sources((r + 2) * (RING * TP), a % 2)
            sp.wait_ge(s_ds, 32)

        @block.gpsimd
        def _(pool):
            plink = Chain(pool, s_pl)
            nc.gpsimd.iota(ei[:], pattern=[[TP, NT]], base=0, channel_multiplier=1)
            plink(nc.gpsimd.iota(K["iota_i"][:], pattern=[[1, LO]], base=0, channel_multiplier=0))
            nc.gpsimd.tensor_copy(iot[:], K["iota_i"][0:TP, :])
            nc.gpsimd.tensor_copy(ef[:], ei[:])
            nc.gpsimd.memset(ones[:], 1.0)
            nc.gpsimd.memset(zero[:], 0.0).then_inc(s_cst, 1)
            pool.wait_ge(s_cst, 1)
            pool.wait_ge(s_tab, 16)
            pool.wait_ge(s_ends_idx, 1)
            @chunks(pool)
            def _(u, a):
                c, p = 2 * u + a, a % 2
                need(pool, s_scat[p], 64 * (u + a // 2))
                pool.sem_inc(s_go, 1)
                nc.gpsimd.tensor_copy(re[p][:], ef[:, bass.ds(CT * c, CT)])
                nc.gpsimd.tensor_copy(ri[p][:], scatI[:, bass.ds(CT * c, CT)]).then_inc(s_ringA, 1)
                pool.wait_ge(s_ringA, c + 1)
                pool.sem_inc(s_go, 1)
                for k in range(CT):
                    nc.gpsimd.indirect_dma_start(
                        out=T["ptab1"], out_offset=bass.IndirectOffsetOnAxis(ap=ri[p][:, k:k + 1], axis=0),
                        in_=re[p][:, k:k + 1], in_offset=None, bounds_check=2 * N - 1, oob_is_err=False).then_inc(s_scat[p], 16)
            for s in s_scat:
                pool.wait_ge(s, 64 * (NC // 2 + (s is s_scat[0])))

            def take(u, a):
                p = a % 2
                pool.wait_ge(s_gat[p], 64 * (u + a // 2 + 1))
                pool.sem_inc(s_go, 1)
                nc.gpsimd.tensor_copy(posS[:, bass.ds(CT * (2 * u + a), CT)], pq[p][:, :, 0]).then_inc(s_pos, 1)

            @chunks(pool)
            def _(u, a):
                c, p = 2 * u + a, a % 2
                need(pool, s_pos, c - 1)
                pool.sem_inc(s_go, 1)
                nc.gpsimd.tensor_copy(rj[p][:], src[:, bass.ds(CT * c, CT)]).then_inc(s_ringB, 1)
                pool.wait_ge(s_ringB, c + 1)
                pool.sem_inc(s_go, 1)
                for k in range(CT):
                    nc.gpsimd.indirect_dma_start(out=pq[p][:, k, :], out_offset=None, in_=T["ptab"],
                                                 in_offset=bass.IndirectOffsetOnAxis(ap=rj[p][:, k:k + 1], axis=0)).then_inc(s_gat[p], 16)
                if not (isinstance(c, int) and c == 0):
                    take(u, a - 1)
            take(0, NC - 1)

        @block.vector
        def _(dve):
            link = Chain(dve, s_dv)
            dve.wait_ge(s_in, 16 * 12)
            nc.vector.tensor_copy(srcf[:], src[:])
            nc.vector.tensor_copy(dstf[:], dst[:])
            nc.vector.tensor_copy(dstnf[:], dstn[:])
            link(nc.vector.tensor_tensor(rowD[:], drow[:], drowP[:], ALU.is_equal))
            nc.vector.tensor_scalar(rowQ[:], rowD[:], NEG, -NEG, ALU.mult, ALU.add).then_inc(s_dsame, 1)
            nc.vector.tensor_scalar(hii[:], src[:], 127, None, ALU.bitwise_and)
            link(nc.vector.tensor_scalar(loi[:], src[:], 7, None, ALU.logical_shift_right))
            nc.vector.tensor_copy(hif[:], hii[:])
            nc.vector.tensor_copy(lof[:], loi[:])
            nc.vector.tensor_scalar(K["clip"][:], dstf[:], float(NH - 1), None, ALU.min)
            nc.vector.tensor_scalar(K["isH"][:], dstf[:], float(NH), None, ALU.is_lt)
            link(nc.vector.tensor_tensor(endf[:], dstf[:], dstnf[:], ALU.is_equal))
            nc.vector.tensor_scalar(endf[:], endf[:], float(FAR), None, ALU.mult)
            link(nc.vector.tensor_scalar(tmp[:], dstf[:], 2.0, None, ALU.mult))
            nc.vector.tensor_tensor(K["dst_end"][:], endf[:], dstf[:], ALU.add)
            nc.vector.tensor_tensor(scatI[:], endf[:], tmp[:], ALU.add).then_inc(s_ends_idx, 1)

            def one_hots(t, k, sem):
                nc.vector.tensor_scalar(ohi[:, k, :], iot[:, 0:128], hif[:, bass.ds(t, 1)], None, ALU.is_equal)
                nc.vector.tensor_scalar(olo[:, k, :], iot[:], lof[:, bass.ds(t, 1)], None, ALU.is_equal).then_inc(sem, 1)

            dve.wait_ge(s_cst, 1)
            @steps(dve, NR)
            def _(r):
                for k in range(RING):
                    need(dve, s_hist, RING * r + k - RING + 1)
                    one_hots(RING * r + k, k, s_ohA)
            dve.wait_ge(s_hist_all, 1)
            link(nc.vector.tensor_copy(cnt[:], pC[:, 0:LO]))
            nc.vector.tensor_tensor_scan(inc[:], ones[:], cnt[:], 0.0, ALU.mult, ALU.add).then_inc(s_tot, 1)
            dve.wait_ge(s_off, 1)
            link(nc.vector.tensor_copy(offs[:], pR[:, 0:1]))
            nc.vector.tensor_scalar(end[:], inc[:], offs[:], -1.0, ALU.add, ALU.add)
            link(nc.vector.tensor_scalar(start[:], inc[:], offs[:], None, ALU.add))
            link(nc.vector.tensor_copy(endh[:], end[:]))
            nc.vector.tensor_tensor(endl[:], end[:], endh[:], ALU.subtract)
            nc.vector.tensor_tensor(cur[:, 0, :], start[:], cnt[:], ALU.subtract).then_inc(s_first, 1)
            dve.wait_ge(s_first, 1)

            def rank(r, k, w):
                t = RING * r + k
                dve.wait_ge(s_look, t + 1)
                nc.vector.scalar_tensor_tensor(out=junk[:, k % 2, 0, 0:TP], in0=srcb[:, w, k * TP:(k + 1) * TP], scalar=srcf[:, bass.ds(t, 1)],
                                               in1=triL[:], op0=ALU.is_equal, op1=ALU.mult, accum_out=hit[:, 0, w, k:k + 1])
                nc.vector.scalar_tensor_tensor(out=junk[:, k % 2, 1, :], in0=pL[0:TP, k % 2, 0:LO], scalar=1.0, in1=olo[:, k, :],
                                               op0=ALU.mult, op1=ALU.mult, accum_out=hit[:, 1, w, k:k + 1])
                nc.vector.scalar_tensor_tensor(out=junk[:, k % 2, 2, :], in0=pE[0:TP, k % 2, 0:LO], scalar=1.0, in1=olo[:, k, :],
                                               op0=ALU.mult, op1=ALU.mult, accum_out=hit[:, 2, w, k:k + 1]).then_inc(s_used, 1)

            def keep(r, w):
                dve.wait_ge(s_used, RING * r + RING)
                nc.vector.tensor_tensor(slotf[:, bass.ds(RING * r, RING)], hit[:, 0, w, :], hit[:, 1, w, :], ALU.add)
                nc.vector.tensor_copy(sendf[:, bass.ds(RING * r, RING)], hit[:, 2, w, :]).then_inc(s_hit, 1)

            AHEAD = RING - 2
            for k in range(AHEAD):
                one_hots(k, k, s_ohB)

            @chunks(dve, NR)
            def _(u, a):
                r, w = 2 * u + a, a % 2
                dve.wait_ge(s_srcb[w], 16 * (u + a // 2 + 1))
                need(dve, s_hit, r - 1)
                for k in range(RING):
                    t = RING * r + k
                    if not (isinstance(t, int) and t < 2):
                        dve.wait_ge(s_look, t - 1)
                        dve.wait_ge(s_used, t - 1)
                    if not (isinstance(t, int) and t + AHEAD >= NT):
                        one_hots(t + AHEAD, (k + AHEAD) % RING, s_ohB)
                    dve.wait_ge(s_acc, t + 1)
                    if not (isinstance(t, int) and t < 1):
                        dve.wait_ge(s_look, t)
                        dve.wait_ge(s_cur, t)
                    nc.vector.tensor_tensor(cur[:, 1 - k % 2, :], cur[:, k % 2, :], pC[:, 0:LO], ALU.add).then_inc(s_cur, 1)
                    rank(r, k, w)
                keep(r, w)
            dve.wait_ge(s_hit, NR)
            rr.init()
            link(nc.vector.memset(one[:], 1.0))
            rr.rows(rowD, one)
            dve.wait_ge(s_pos, NC)
            link(nc.vector.tensor_scalar(tmp[:], posS[:], float(E), None, ALU.is_equal))
            link(nc.vector.tensor_tensor(tmp[:], tmp[:], ef[:], ALU.mult))
            link(nc.vector.tensor_tensor(idxSf[:], posS[:], tmp[:], ALU.add))
            nc.vector.tensor_copy(K["slot"][:], slotf[:])
            nc.vector.tensor_copy(K["send"][:], sendf[:])
            nc.vector.tensor_copy(K["idxS"][:], idxSf[:])
            nc.vector.tensor_copy(K["pay"][:, :, 0], srcf[:])
            link(nc.vector.tensor_copy(K["pay"][:, :, 1], idxSf[:]))
            rr.finish(dve, link)
            nc.vector.tensor_copy(one[:], rr.run[:]).then_inc(s_deg, 1)
            dve.wait_ge(s_degT, 1)
            link(nc.vector.reciprocal(K["rdeg"][:], pR[0:TP, 128:128 + NT]))
            link(nc.vector.tensor_tensor(K["rdegH"][:], K["rdeg"][:], K["isH"][:], ALU.mult))

        @block.tensor
        def _(pe):
            pe.wait_ge(s_cst, 1)
            nc.tensor.matmul(pC[:, 0:LO], zero[:, 0:128], zero[:], start=True, stop=False)
            @steps(pe, NR)
            def _(r):
                for k in range(RING):
                    pe.wait_ge(s_ohA, RING * r + k + 1)
                    nc.tensor.matmul(pC[:, 0:LO], ohi[:, k, :], olo[:, k, :], start=False, stop=False).then_inc(s_hist, 1)
            nc.tensor.matmul(pC[:, 0:LO], zero[:, 0:128], zero[:], start=False, stop=True).then_inc(s_hist_all, 1)
            pe.wait_ge(s_tot, 1)
            nc.tensor.matmul(pR[:, 0:1], tri[:], inc[:, LO - 1:LO], start=True, stop=True).then_inc(s_off, 1)
            pe.wait_ge(s_first, 1)

            def turn(t, k):
                pe.wait_ge(s_ohB, t + 1)
                need(pe, s_hiT, t - 1)
                nc.tensor.transpose(pT[:, k % 2, 0:TP], ohi[:, k, :], K["identb"][0:TP, 0:TP]).then_inc(s_tr, 1)

            turn(0, 0)
            @chunks(pe, NR)
            def _(u, a):
                r = 2 * u + a
                for k in range(RING):
                    t = RING * r + k
                    if not (isinstance(t, int) and t + 1 >= NT):
                        turn(t + 1, (k + 1) % RING)
                    need(pe, s_cur, t)
                    nc.tensor.matmul(pC[:, 0:LO], ohi[:, k, :], olo[:, k, :], start=True, stop=True).then_inc(s_acc, 1)
                    pe.wait_ge(s_hiT, t + 1)
                    if not (isinstance(t, int) and t < 2):
                        pe.wait_ge(s_used, t - 1)
                    nc.tensor.matmul(pL[0:TP, k % 2, 0:LO], hiT[:, k % 2, :], cur[:, k % 2, :], start=True, stop=True)
                    nc.tensor.matmul(pE[0:TP, k % 2, 0:LO], hiTb[:, k % 2, :], endh[:], start=True, stop=False)
                    nc.tensor.matmul(pE[0:TP, k % 2, 0:LO], hiTb[:, k % 2, :], endl[:], start=False, stop=True).then_inc(s_look, 1)
            rr.tensor(pe, K["ident"])
            pe.wait_ge(s_deg, 1)
            nc.tensor.transpose(pR[0:TP, 128:128 + NT], one[:], K["ident"][0:NT, 0:NT]).then_inc(s_degT, 1)

        @block.scalar
        def _(act):
            @chunks(act, NR)
            def _(u, a):
                r = 2 * u + a
                for k in range(RING):
                    t = RING * r + k
                    act.wait_ge(s_tr, t + 1)
                    if not (isinstance(t, int) and t < 2):
                        act.wait_ge(s_look, t - 1)
                    nc.scalar.activation(hiTb[:, k % 2, :], pT[:, k % 2, 0:TP], ACT.Copy)
                    nc.scalar.activation(hiT[:, k % 2, :], pT[:, k % 2, 0:TP], ACT.Copy).then_inc(s_hiT, 1)


def slots_phase(nc, g, K, T):
    with ExitStack() as ctx:
        a = Place(nc, ctx, "sl")
        s4 = a.sb("s4", [TP, NT, 4])
        rowS, rowN, rowP, rowI, rowE, rowH, rowM, rowV = (
            a.sb(n, [NT, TP]) for n in ("rowS", "rowN", "rowP", "rowI", "rowE", "rowH", "rowM", "rowV"))
        cap = a.sb("cap", [1, 1])
        pR, pL, pC = (a.ps(n, [128, 512]) for n in ("pR", "pL", "pC"))
        rr = RowRuns(nc, a, pL, pC)
        run, pref = rr.run, rr.pref
        s_s4, s_rowT, s_row, s_rowst, s_rown, s_rowi, s_colT, s_dv, s_dinv = (
            a.sem(n) for n in ("s4", "rowT", "row", "row_stored", "row_next", "row_idx", "colT", "chain", "dinv"))
        block = ctx.enter_context(nc.Block())

        @block.sync
        def _(sp):
            sp.dma_start(s4[:], T["S4"].rearrange("(t p) c -> p t c", p=TP)).then_inc(s_s4, 16)
            sp.wait_ge(s_row, 1)
            sp.dma_start(T["srow"][:, 1:E + 1].rearrange("a (t p) -> (a t) p", p=TP), rowS[:]).then_inc(s_rowst, 16)
            sp.dma_start(T["srow"][:, 0:1], cap[:]).then_inc(s_rowst, 16)
            sp.dma_start(T["srow"][:, E + 1:E + 2], cap[:]).then_inc(s_rowst, 16)
            sp.wait_ge(s_rowst, 48)
            sp.dma_start(rowN[:], T["srow"][:, 2:E + 2].rearrange("a (t p) -> (a t) p", p=TP)).then_inc(s_rown, 16)
            sp.dma_start(rowP[:], T["srow"][:, 0:E].rearrange("a (t p) -> (a t) p", p=TP)).then_inc(s_rown, 16)
            sp.wait_ge(s_dinv, 1)
            for name, t in (("ssame", rowM), ("dinv", rowV)):
                sp.dma_start(T[name].rearrange("a (t p) -> (a t) p", p=TP), t[:]).then_inc(s_rowst, 16)
            sp.wait_ge(s_rowst, 80)

        @block.vector
        def _(dve):
            link = Chain(dve, s_dv)
            nc.vector.memset(cap[:], -1.0)
            rr.init()
            dve.wait_ge(s_s4, 16)
            nc.vector.tensor_copy(K["s_idxE"][:], s4[:, :, 2])
            nc.vector.tensor_copy(K["s_idxS"][:], s4[:, :, 1])
            dve.wait_ge(s_rowT, 1)
            nc.vector.tensor_copy(rowS[:], pR[0:NT, 0:TP])
            nc.vector.tensor_copy(rowH[:], pR[0:NT, TP:2 * TP]).then_inc(s_row, 1)
            dve.wait_ge(s_row, 1)
            dve.wait_ge(s_rown, 32)
            nc.vector.tensor_tensor(rowM[:], rowS[:], rowP[:], ALU.is_equal)
            link(nc.vector.tensor_tensor(rowE[:], rowS[:], rowN[:], ALU.is_equal))
            rr.rows(rowM, rowH)
            nc.vector.scalar_tensor_tensor(out=rowI[:], in0=rowE[:], scalar=float(FAR), in1=rowS[:],
                                           op0=ALU.mult, op1=ALU.add).then_inc(s_rowi, 1)
            dve.wait_ge(s_colT, 1)
            nc.vector.tensor_copy(K["src_end"][:], pR[0:TP, 256:256 + NT])
            rr.finish(dve, link)
            nc.vector.tensor_scalar(pref[:], run[:], 0.0, None, ALU.is_gt)
            link(nc.vector.tensor_scalar(rowV[:], run[:], 1.2e-38, None, ALU.max))
            nc.vector.tensor_scalar(rowE[:], rowE[:], -1.0, 1.0, ALU.mult, ALU.add)
            link(nc.vector.reciprocal(run[:], rowV[:]))
            link(nc.vector.tensor_tensor(pref[:], pref[:], rowE[:], ALU.mult))
            nc.vector.tensor_tensor(rowV[:], run[:], pref[:], ALU.mult).then_inc(s_dinv, 1)

        @block.tensor
        def _(pe):
            pe.wait_ge(s_s4, 16)
            nc.tensor.transpose(pR[0:NT, 0:TP], s4[:, :, 0], K["ident"][0:TP, 0:TP])
            nc.tensor.transpose(pR[0:NT, TP:2 * TP], s4[:, :, 3], K["ident"][0:TP, 0:TP]).then_inc(s_rowT, 1)
            pe.wait_ge(s_rowi, 1)
            nc.tensor.transpose(pR[0:TP, 256:256 + NT], rowI[:], K["ident"][0:NT, 0:NT]).then_inc(s_colT, 1)
            rr.tensor(pe, K["ident"])


def gathers(pool, s_go, s_ring, s_full, ring, index, c, n, table, buf):
    nc = pool.bass
    nc.gpsimd.tensor_copy(ring[:], index[:, bass.ds(CT * c, CT)]).then_inc(s_ring, 1)
    pool.wait_ge(s_ring, n)
    pool.sem_inc(s_go, 1)
    for k in range(CT):
        nc.gpsimd.indirect_dma_start(out=buf[:, k, :], out_offset=None, in_=table,
                                     in_offset=bass.IndirectOffsetOnAxis(ap=ring[:, k:k + 1], axis=0)).then_inc(s_full, 16)


def row_stats(nc, z, rows, st, mv, s_stats):
    for r in range(rows):
        last = nc.vector.bn_stats(st[:, r, :], z[:, r, :])
    last.then_inc(s_stats, 1)


def row_aggr(nc, rows, st, mv):
    for r in range(rows):
        last = nc.vector.bn_aggr(mv[:, r, :], st[:, r, :])
    return last


def normalize(nc, out, z, rows, mv, rs):
    for r in range(rows):
        last = nc.vector.tensor_scalar(out[:, r, :], z[:, r, :], mv[:, r, 0:1], rs[:, r:r + 1], ALU.subtract, ALU.mult)
    return last


def bc(vec, rows):
    p = vec.shape[0]
    return vec[:, :].rearrange("p (o f) -> p o f", o=1).broadcast_to([p, rows, D])


def attention_phase(nc, g, K, T, dn, off):
    with ExitStack() as ctx:
        a = Place(nc, ctx, "at")
        W = {n: a.sb(n, [D, D]) for n in ("Wq", "Wk", "Wv", "Wo")}
        cols = K["cols"]
        bo, sel = a.sb("bo", [TP, D]), a.sb("sel", [D, 8])
        eps = a.sb("eps", [128, 1])
        ringS, ringD = ([a.sb(f"{n}{p}", [TP, CT], I32) for p in range(2)] for n in ("ringS", "ringD"))
        srcI, dstI = a.sb("srcI", [TP, NT], I32), a.sb("dstI", [TP, NT], I32)
        ga, gb = ([a.sb(f"{n}{p}", [TP, CT, D]) for p in range(2)] for n in ("ga", "gb"))
        xs, xd, q, prod, f, p, pv, dif, o, oF = (a.sb(n, [D, CE]) for n in ("xs", "xd", "q", "prod", "f", "p", "pv", "dif", "o", "oF"))
        t1, t2, pen = (a.sb(n, [D, CE]) for n in ("t1", "t2", "pen"))
        eb = a.sb("eb", [8, CE])
        M, Nu, De = (a.sb(n, [D, CE + 1]) for n in ("M", "Nu", "De"))
        den, rec, wide = a.sb("den", [TP, CT * 8]), a.sb("rec", [TP, CT * 8]), a.sb("wide", [TP, CT * D])
        z, y = a.sb("z", [TP, 2 * CT, D]), a.sb("y", [TP, 2 * CT, D])
        st, mv = a.sb("st", [TP, 2 * CT, 6]), a.sb("mv", [TP, 2 * CT, 2])
        sd, rs, nb = (a.sb(n, [TP, 2 * CT]) for n in ("sd", "rs", "nb"))
        pA, pB, pQ, pK, pV, pAt, pO, pR = (a.ps(n, [128, 512]) for n in ("pA", "pB", "pQ", "pK", "pV", "pAt", "pO", "pR"))
        (s_w, s_go, s_ringS, s_ringD, s_tA, s_tB, s_xs, s_xd, s_psQ, s_psK, s_psV, s_q, s_prod, s_att, s_args, s_exp, s_pv, s_sum,
         s_carry, s_M, s_psD, s_den, s_rec, s_psRc, s_o, s_psO, s_oF, s_psR, s_z, s_z2, s_gbc, s_pen, s_sd, s_mv, s_rs, s_r, s_y, s_eb,
         s_st, s_dgo, s_d, s_eps, s_init) = (
            a.sem(n) for n in ("weights", "go", "ringS", "ringD", "tA", "tB", "xs", "xd", "psQ", "psK", "psV", "q", "prod", "att",
                               "args", "exp", "pv", "sum", "carry", "max", "psD", "den", "rec", "psRc", "o", "psO", "oF", "psR", "z",
                               "z_source", "gb_copied", "pen", "sd", "mv", "rs", "scale", "y", "eb", "stored", "dve_go", "stats", "eps", "init"))
        s_ga, s_gb = ([a.sem(f"{n}{p}") for p in range(2)] for n in ("ga", "gb"))
        block = ctx.enter_context(nc.Block())
        DONE = 16 * 8

        @block.sync
        def _(sp):
            for n in W:
                sp.dma_start(W[n][:], g[n]).then_inc(s_w, 16)
            sp.dma_start(bo[:], g["rowv"][0:1, :].broadcast_to([TP, D])).then_inc(s_w, 16)
            sp.dma_start(sel[:], g["sel"]).then_inc(s_w, 16)
            sp.dma_start(srcI[:], g["src_col"]).then_inc(s_w, 16)
            sp.dma_start(dstI[:], g["dst_col"]).then_inc(s_w, 16)

            def load_pen(c):
                sp.dma_start(pen[:], T["dpen"][:, bass.ds(CE * c, CE)].broadcast_to([D, CE])).then_inc(s_pen, 16)

            def load_bias(c):
                sp.dma_start(eb[:], g["ea8T"][:, bass.ds(CE * c, CE)]).then_inc(s_eb, 16)

            def store(c):
                sp.wait_ge(s_y, c + 1)
                sp.dma_start(rows_of(T["T1"], CE * c, CT), y[:, 0:CT, :]).then_inc(s_st, 16)
                sp.dma_start(rows_of(T["T1"], CE * c + E, CT), y[:, CT:2 * CT, :]).then_inc(s_st, 16)

            load_pen(0)
            load_bias(0)

            def chunk(u, a):
                c = 2 * u + a
                dn.load(sp, u, a + off + 1)
                if not last_of(c, 1):
                    sp.wait_ge(s_att, c + 1)
                    load_bias(c + 1)
                    sp.wait_ge(s_args, c + 1)
                    load_pen(c + 1)
                if not first_of(c):
                    store(c - 1)
                dn.store(sp, u, a + off - LAG_W)

            chunks(sp, NC - 1)(chunk)
            chunk(0, NC - 1)
            store(NC - 1)
            sp.wait_ge(s_st, 32 * NC)

        @block.gpsimd
        def _(pool):
            pool.wait_ge(s_w, DONE)
            nc.gpsimd.memset(eps[:], EPS).then_inc(s_eps, 1)
            gathers(pool, s_go, s_ringS, s_ga[0], ringS[0], srcI, 0, 1, g["x"], ga[0])
            gathers(pool, s_go, s_ringD, s_gb[0], ringD[0], dstI, 0, 1, g["x"], gb[0])

            @chunks(pool)
            def _(u, a):
                c, p1 = 2 * u + a, (a + 1) % 2
                if not last_of(c, 1):
                    if not first_of(c):
                        pool.wait_ge(s_z2, c)
                        pool.wait_ge(s_tA, c)
                        pool.sem_inc(s_go, 1)
                    gathers(pool, s_go, s_ringS, s_ga[p1], ringS[p1], srcI, c + 1, c + 2, g["x"], ga[p1])
                    if not first_of(c):
                        pool.wait_ge(s_gbc, c)
                        pool.wait_ge(s_tB, c)
                        pool.sem_inc(s_go, 1)
                    gathers(pool, s_go, s_ringD, s_gb[p1], ringD[p1], dstI, c + 1, c + 2, g["x"], gb[p1])
                dn.pool_z(pool, u, a + off)
                dn.pool_q(pool, u, a + off - LAG_Q)
                dn.pool_w(pool, u, a + off - LAG_V)
                pool.wait_ge(s_ga[a % 2], 64 * (u + a // 2 + 1))
                need(pool, s_y, c)
                nc.gpsimd.tensor_tensor(z[:, CT:2 * CT, :], ga[a % 2][:], bc(bo, CT), ALU.add).then_inc(s_z2, 1)

        @block.tensor
        def _(pe):
            pe.wait_ge(s_w, DONE)

            def turn(u, a):
                c, k2 = 2 * u + a, a % 2
                pe.wait_ge(s_ga[k2], 64 * (u + a // 2 + 1))
                need(pe, s_xs, c)
                for k in range(CT):
                    last = nc.tensor.transpose(pA[:, k * TP:(k + 1) * TP], ga[k2][:, k, :], K["ident"][0:TP, 0:TP])
                last.then_inc(s_tA, 1)
                pe.wait_ge(s_gb[k2], 64 * (u + a // 2 + 1))
                need(pe, s_xd, c)
                for k in range(CT):
                    last = nc.tensor.transpose(pB[:, k * TP:(k + 1) * TP], gb[k2][:, k, :], K["ident"][0:TP, 0:TP])
                last.then_inc(s_tB, 1)

            def project(c):
                pe.wait_ge(s_xd, c + 1)
                nc.tensor.matmul(pQ[:, 0:CE], W["Wq"][:], xd[:], start=True, stop=True).then_inc(s_psQ, 1)
                pe.wait_ge(s_xs, c + 1)
                nc.tensor.matmul(pK[:, 0:CE], W["Wk"][:], xs[:], start=True, stop=True).then_inc(s_psK, 1)

            def values(c):
                nc.tensor.matmul(pV[:, 0:CE], W["Wv"][:], xs[:], start=True, stop=True).then_inc(s_psV, 1)

            turn(0, 0)
            project(0)
            values(0)

            @chunks(pe)
            def _(u, a):
                c = 2 * u + a
                pe.wait_ge(s_prod, c + 1)
                pe.wait_ge(s_eb, 16 * (c + 1))
                need(pe, s_o, c)
                nc.tensor.matmul(pAt[:, 0:CE], K["heads"][:], prod[:], start=True, stop=False)
                nc.tensor.matmul(pAt[:, 0:CE], K["expand"][:], eb[:], start=False, stop=True).then_inc(s_att, 1)
                if not last_of(c, 1):
                    turn(u, a + 1)
                pe.wait_ge(s_sum, c + 1)
                need(pe, s_z, c)
                for k in range(CT):
                    last = nc.tensor.matmul(pR[0:TP, k * 8:(k + 1) * 8], De[:, 1 + k * TP:1 + (k + 1) * TP], sel[:], start=True, stop=True)
                last.then_inc(s_psD, 1)
                if not last_of(c, 1):
                    project(c + 1)
                pe.wait_ge(s_rec, c + 1)
                pe.wait_ge(s_args, c + 1)
                for k in range(CT):
                    last = nc.tensor.matmul(pAt[:, k * TP:(k + 1) * TP], wide[:, k * D:(k + 1) * D], K["ident"][0:TP, 0:TP], start=True, stop=True)
                last.then_inc(s_psRc, 1)
                if not last_of(c, 1):
                    values(c + 1)
                pe.wait_ge(s_o, c + 1)
                nc.tensor.matmul(pO[:, 0:CE], W["Wo"][:], o[:], start=True, stop=True).then_inc(s_psO, 1)
                pe.wait_ge(s_oF, c + 1)
                for k in range(CT):
                    last = nc.tensor.transpose(pR[0:TP, k * D:(k + 1) * D], oF[:, k * TP:(k + 1) * TP], K["ident"][:])
                last.then_inc(s_psR, 1)

        @block.scalar
        def _(act):
            act.wait_ge(s_eps, 1)
            act.wait_ge(s_w, DONE)

            def rows(c):
                act.wait_ge(s_tB, c + 1)
                need(act, s_psQ, c)
                nc.scalar.activation(xd[:], pB[:, 0:CE], ACT.Copy).then_inc(s_xd, 1)
                act.wait_ge(s_tA, c + 1)
                need(act, s_psV, c)
                nc.scalar.activation(xs[:], pA[:, 0:CE], ACT.Copy).then_inc(s_xs, 1)

            def query(c):
                act.wait_ge(s_psQ, c + 1)
                need(act, s_prod, c)
                nc.scalar.activation(q[:], pQ[:, 0:CE], ACT.Identity, bias=cols[:, 0:1]).then_inc(s_q, 1)

            def root(c):
                act.wait_ge(s_mv, c + 1)
                nc.scalar.activation(sd[:], mv[:, :, 1], ACT.Sqrt, bias=eps[0:TP, :]).then_inc(s_sd, 1)

            def norm(c):
                act.wait_ge(s_r, c + 1)
                need(act, s_st, 32 * c)
                for r in range(2 * CT):
                    last = nc.scalar.activation(y[:, r, :], z[:, r, :], ACT.Identity, bias=nb[:, r:r + 1], scale=rs[:, r:r + 1])
                last.then_inc(s_y, 1)

            rows(0)
            query(0)

            @chunks(act)
            def _(u, a):
                c = 2 * u + a
                dn.act_root3(act, u, a + off - LAG_Y)
                dn.act_root4(act, u, a + off - LAG_W)
                if not first_of(c):
                    root(c - 1)
                act.wait_ge(s_args, c + 1)
                need(act, s_sum, c)
                nc.scalar.activation(f[:], t2[:], ACT.Exp)
                nc.scalar.activation(p[:], dif[:], ACT.Exp).then_inc(s_exp, 1)
                if not last_of(c, 1):
                    rows(c + 1)
                dn.act_root1(act, u, a + off - 1)
                if not last_of(c, 1):
                    query(c + 1)
                if not first_of(c):
                    norm(c - 1)
                act.wait_ge(s_gb[a % 2], 64 * (u + a // 2 + 1))
                need(act, s_y, c)
                nc.scalar.activation(z[:, 0:CT, :], gb[a % 2][:], ACT.Copy).then_inc(s_gbc, 1)
                dn.act_root2(act, u, a + off - 1)
                dn.act_out(act, u, a + off - LAG_W)
                dn.act_x3(act, u, a + off - LAG_Y)
                act.wait_ge(s_psO, c + 1)
                need(act, s_psR, c)
                nc.scalar.activation(oF[:], pO[:, 0:CE], ACT.Identity, bias=cols[:, 3:4]).then_inc(s_oF, 1)
                dn.act_n(act, u, a + off - 1)
            root(NC - 1)
            norm(NC - 1)

        @block.vector
        def _(dve):
            nc.vector.memset(M[:], -NEG)
            nc.vector.memset(Nu[:], 0.0)
            nc.vector.memset(De[:], 0.0).then_inc(s_init, 1)
            dve.wait_ge(s_init, 1)
            dve.wait_ge(s_w, DONE)

            def residual(c):
                dve.wait_ge(s_gbc, c + 1)
                dve.wait_ge(s_z2, c + 1)
                dve.wait_ge(s_psR, c + 1)
                nc.vector.tensor_tensor(z[:, 0:CT, :], z[:, 0:CT, :], pR[0:TP, :].rearrange("p (k f) -> p k f", k=CT), ALU.add).then_inc(s_z, 1)
                dve.wait_ge(s_z, c + 1)
                row_stats(nc, z, 2 * CT, st, mv, s_d)
                need(dve, s_r, c)
                dve.wait_ge(s_d, c + 1)
                dve.sem_inc(s_dgo, 1)
                row_aggr(nc, 2 * CT, st, mv).then_inc(s_mv, 1)

            def scale(c):
                dve.wait_ge(s_sd, c + 1)
                need(dve, s_y, c)
                nc.vector.reciprocal(rs[:], sd[:]).then_inc(s_rs, 1)
                dve.wait_ge(s_rs, c + 1)
                nc.vector.scalar_tensor_tensor(out=nb[:], in0=mv[:, :, 0], scalar=-1.0, in1=rs[:], op0=ALU.mult, op1=ALU.mult).then_inc(s_r, 1)

            @chunks(dve)
            def _(u, a):
                c = 2 * u + a
                dve.wait_ge(s_psK, c + 1)
                dve.wait_ge(s_q, c + 1)
                nc.vector.scalar_tensor_tensor(out=prod[:], in0=pK[:, 0:CE], scalar=cols[:, 1:2], in1=q[:],
                                               op0=ALU.add, op1=ALU.mult).then_inc(s_prod, 1)
                nc.vector.tensor_copy(M[:, 0:1], M[:, CE:CE + 1])
                nc.vector.tensor_copy(Nu[:, 0:1], Nu[:, CE:CE + 1])
                nc.vector.tensor_copy(De[:, 0:1], De[:, CE:CE + 1]).then_inc(s_carry, 1)
                dn.dve_y(dve, u, a + off - LAG_Y)
                dn.dve_w(dve, u, a + off - LAG_W)
                if not first_of(c):
                    residual(c - 1)
                dve.wait_ge(s_carry, c + 1)
                dve.wait_ge(s_pen, 16 * (c + 1))
                dve.wait_ge(s_att, c + 1)
                need(dve, s_exp, c)
                nc.vector.tensor_tensor_scan(M[:, 1:CE + 1], pen[:], pAt[:, 0:CE], M[:, 0:1], ALU.add, ALU.max).then_inc(s_M, 1)
                dn.dve_z(dve, u, a + off - 1)
                dve.wait_ge(s_M, 2 * c + 1)
                nc.vector.tensor_tensor(t1[:], M[:, 0:CE], M[:, 1:CE + 1], ALU.subtract).then_inc(s_M, 1)
                nc.vector.tensor_tensor(dif[:], pAt[:, 0:CE], M[:, 1:CE + 1], ALU.subtract)
                dve.wait_ge(s_M, 2 * c + 2)
                nc.vector.scalar_tensor_tensor(out=t2[:], in0=t1[:], scalar=0.0, in1=pen[:], op0=ALU.min, op1=ALU.add).then_inc(s_args, 1)
                if not first_of(c):
                    scale(c - 1)
                dve.wait_ge(s_exp, c + 1)
                dve.wait_ge(s_psV, c + 1)
                nc.vector.scalar_tensor_tensor(out=pv[:], in0=pV[:, 0:CE], scalar=cols[:, 2:3], in1=p[:], op0=ALU.add, op1=ALU.mult).then_inc(s_pv, 1)
                need(dve, s_psD, c)
                nc.vector.tensor_tensor_scan(De[:, 1:CE + 1], f[:], p[:], De[:, 0:1], ALU.mult, ALU.add)
                dve.wait_ge(s_pv, c + 1)
                nc.vector.tensor_tensor_scan(Nu[:, 1:CE + 1], f[:], pv[:], Nu[:, 0:1], ALU.mult, ALU.add).then_inc(s_sum, 1)
                dn.dve_x3(dve, u, a + off - LAG_Y)
                dn.dve_o(dve, u, a + off - LAG_W)
                dve.wait_ge(s_psD, c + 1)
                nc.vector.tensor_scalar(den[:], pR[0:TP, 0:CT * 8], 1e-16, None, ALU.add).then_inc(s_den, 1)
                dve.wait_ge(s_den, 2 * c + 1)
                nc.vector.reciprocal(rec[:], den[:]).then_inc(s_den, 1)
                dve.wait_ge(s_den, 2 * c + 2)
                nc.vector.tensor_scalar(wide[:].rearrange("p (h o) -> p h o", o=16), rec[:].rearrange("p (h o) -> p h o", o=1).broadcast_to([TP, CT * 8, 16]),
                                        1.0, None, ALU.mult).then_inc(s_rec, 1)
                dn.dve_h(dve, u, a + off - 1)
                dn.dve_n(dve, u, a + off - 1)
                dve.wait_ge(s_psRc, c + 1)
                dve.wait_ge(s_sum, c + 1)
                need(dve, s_psO, c)
                nc.vector.tensor_tensor(o[:], Nu[:, 1:CE + 1], pAt[:, 0:CE], ALU.mult).then_inc(s_o, 1)
            residual(NC - 1)
            scale(NC - 1)


DR = 5
DP = N // 128
DS = DP // DR
DL = N - 128 * DP
LAG_Q, LAG_Y, LAG_V, LAG_W = 2, 3, 4, 5
assert DP == DS * DR and DL > 0 and LAG_W + 3 * NC == DS + 2


def outside(t):
    return isinstance(t, int) and not 0 <= t <= DS


def first_of(c):
    return isinstance(c, int) and c == 0


def last_of(c, n):
    return isinstance(c, int) and c + n >= NC


def need(eng, sem, n):
    if not isinstance(n, int) or n > 0:
        eng.wait_ge(sem, n)


class Dense:

    def __init__(self, nc, ctx, g, T):
        self.nc, self.g, self.T = nc, g, T
        a = self.place = Place(nc, ctx, "dn")
        self.bo, self.ub, self.lg, self.lb, self.b2, self.cb = (a.sb(n, [128, D]) for n in ("bo", "ub", "lg", "lb", "b2", "cb"))
        self.eps = a.sb("eps", [128, 1])
        self.x, self.z, self.h, self.n, self.q, self.y, self.x3, self.w, self.o = (
            a.sb(n, [128, 2, DR, D]) for n in ("x", "z", "h", "n", "q", "y", "x3", "w", "o"))
        self.ng = a.sb("ng", [128, DR, D])
        self.st = a.sb("st", [128, 4, DR, 6])
        self.mv = a.sb("mv", [128, 4, DR, 2])
        self.sd, self.rs, self.nb = (a.sb(n, [128, 4, DR]) for n in ("sd", "rs", "nb"))
        self.t3, self.v3 = a.sb("t3", [128, DR]), a.sb("v3", [128, DR])
        self.s_w = a.sem("weights")
        self.s_c = a.sem("consts")
        self.s_x = [a.sem(f"x{k}") for k in range(2)]
        self.s_st = [a.sem(f"stored{k}") for k in range(2)]
        (self.s_z, self.s_m1, self.s_sd1, self.s_h, self.s_m2, self.s_sd2, self.s_r2, self.s_n, self.s_ng, self.s_q, self.s_y,
         self.s_m3, self.s_sd3, self.s_r3, self.s_x3, self.s_w4, self.s_m4, self.s_sd4, self.s_r4, self.s_o, self.s_go) = (
            a.sem(n) for n in ("z", "stats1", "sd1", "h", "stats2", "sd2", "scale2", "n", "ng", "q", "y", "stats3", "sd3", "scale3",
                               "x3", "w", "stats4", "sd4", "scale4", "out", "dve_go"))
        self.s_l = [a.sem(f"chain{j}") for j in range(4)]
        self.xv = g["x"][0:128 * DP, :].rearrange("(p r) f -> p r f", p=128)
        self.ov = T["out"][0:128 * DP, :].rearrange("(p r) f -> p r f", p=128)

    def rows(self, t):
        return (DL, 1) if isinstance(t, int) and t == DS else (128, DR)

    def cut(self, buf, t, k):
        p, r = self.rows(t)
        return buf[0:p, k, 0:r]

    def vec(self, v, t):
        p, r = self.rows(t)
        return bc(v[0:p], r)

    def weights(self, sp):
        for v, r in ((self.bo, 0), (self.ub, 1), (self.lg, 2), (self.lb, 3), (self.b2, 4)):
            sp.dma_start(v[:], self.g["rowv"][r:r + 1, :].broadcast_to([128, D])).then_inc(self.s_w, 16)

    def side(self, view, tensor, t):
        if isinstance(t, int) and t == DS:
            return tensor[128 * DP:N, :].rearrange("p (r f) -> p r f", r=1)
        return view[:, bass.ds(t * DR, DR), :]

    def load(self, sp, u, a):
        t, k = 2 * u + a, a % 2
        if outside(t):
            return
        need(sp, self.s_z, t - 1)
        sp.dma_start(self.cut(self.x, t, k), self.side(self.xv, self.g["x"], t)).then_inc(self.s_x[k], 16)

    def store(self, sp, u, a):
        t, k = 2 * u + a, a % 2
        if outside(t):
            return
        sp.wait_ge(self.s_o, t + 1)
        sp.dma_start(self.side(self.ov, self.T["out"], t), self.cut(self.o, t, k)).then_inc(self.s_st[k], 16)

    def pool_z(self, pool, u, a):
        t, k = 2 * u + a, a % 2
        if outside(t):
            return
        pool.wait_ge(self.s_x[k], 16 * (u + a // 2 + 1))
        need(pool, self.s_h, t - 1)
        self.nc.gpsimd.tensor_tensor(self.cut(self.z, t, k), self.cut(self.x, t, k), self.vec(self.bo, t), ALU.add).then_inc(self.s_z, 1)

    def pool_q(self, pool, u, a):
        t, k = 2 * u + a, a % 2
        if outside(t):
            return
        p, r = self.rows(t)
        pool.wait_ge(self.s_n, t + 1)
        need(pool, self.s_q, t)
        self.nc.gpsimd.tensor_tensor(self.ng[0:p, 0:r], self.cut(self.n, t, k), self.vec(self.lg, t), ALU.mult).then_inc(self.s_ng, 1)
        need(pool, self.s_y, t - 1)
        pool.wait_ge(self.s_ng, t + 1)
        self.nc.gpsimd.tensor_tensor(self.cut(self.q, t, k), self.ng[0:p, 0:r], self.vec(self.cb, t), ALU.add).then_inc(self.s_q, 1)

    def pool_w(self, pool, u, a):
        t, k = 2 * u + a, a % 2
        if outside(t):
            return
        pool.wait_ge(self.s_x3, t + 1)
        need(pool, self.s_o, t - 1)
        self.nc.gpsimd.tensor_tensor(self.cut(self.w, t, k), self.cut(self.x3, t, k), self.vec(self.b2, t), ALU.add).then_inc(self.s_w4, 1)

    def consts(self, dve):
        nc = self.nc
        nc.vector.memset(self.eps[:], EPS)
        dve.wait_ge(self.s_w, 80)
        nc.vector.tensor_tensor(self.cb[:], self.lb[:], self.ub[:], ALU.subtract).then_inc(self.s_c, 1)

    def stats(self, dve, buf, t, k, j, s_chain, n):
        nc = self.nc
        p, r = self.rows(t)
        for i in range(r):
            last = nc.vector.bn_stats(self.st[0:p, j, i, :], buf[0:p, k, i, :])
        last.then_inc(s_chain, 1)
        dve.wait_ge(s_chain, n)
        dve.sem_inc(self.s_go, 1)
        for i in range(r):
            last = nc.vector.bn_aggr(self.mv[0:p, j, i, :], self.st[0:p, j, i, :])
        return last

    def scale(self, dve, t, j, s_chain, n, s_done):
        nc = self.nc
        p, r = self.rows(t)
        nc.vector.reciprocal(self.rs[0:p, j, 0:r], self.sd[0:p, j, 0:r]).then_inc(s_chain, 1)
        dve.wait_ge(s_chain, n)
        nc.vector.scalar_tensor_tensor(out=self.nb[0:p, j, 0:r], in0=self.mv[0:p, j, 0:r, 0], scalar=-1.0, in1=self.rs[0:p, j, 0:r],
                                       op0=ALU.mult, op1=ALU.mult).then_inc(s_done, 1)

    def dve_z(self, dve, u, a):
        t, k = 2 * u + a, a % 2
        if outside(t):
            return
        dve.wait_ge(self.s_z, t + 1)
        self.stats(dve, self.z, t, k, 0, self.s_l[0], 2 * t + 1).then_inc(self.s_m1, 1)

    def dve_h(self, dve, u, a):
        nc = self.nc
        t, k = 2 * u + a, a % 2
        if outside(t):
            return
        p, r = self.rows(t)
        dve.wait_ge(self.s_sd1, t + 1)
        nc.vector.reciprocal(self.rs[0:p, 0, 0:r], self.sd[0:p, 0, 0:r]).then_inc(self.s_l[0], 1)
        need(dve, self.s_n, t - 1)
        need(dve, self.s_y, t - 1)
        dve.wait_ge(self.s_l[0], 2 * t + 2)
        for i in range(r):
            last = nc.vector.scalar_tensor_tensor(out=self.h[0:p, k, i, :], in0=self.z[0:p, k, i, :], scalar=self.rs[0:p, 0, i:i + 1],
                                                  in1=self.ub[0:p, :], op0=ALU.mult, op1=ALU.add)
        last.then_inc(self.s_h, 1)
        dve.wait_ge(self.s_h, t + 1)
        self.stats(dve, self.h, t, k, 1, self.s_l[1], 2 * t + 1).then_inc(self.s_m2, 1)

    def dve_n(self, dve, u, a):
        t = 2 * u + a
        if outside(t):
            return
        dve.wait_ge(self.s_sd2, t + 1)
        need(dve, self.s_n, t)
        self.scale(dve, t, 1, self.s_l[1], 2 * t + 2, self.s_r2)

    def dve_y(self, dve, u, a):
        nc = self.nc
        t, k = 2 * u + a, a % 2
        if outside(t):
            return
        p, r = self.rows(t)
        dve.wait_ge(self.s_q, t + 1)
        need(dve, self.s_x3, t - 1)
        nc.vector.tensor_tensor(self.cut(self.y, t, k), self.cut(self.h, t, k), self.cut(self.q, t, k), ALU.add).then_inc(self.s_y, 1)
        dve.wait_ge(self.s_y, t + 1)
        self.stats(dve, self.y, t, k, 2, self.s_l[2], 4 * t + 1).then_inc(self.s_l[2], 1)
        dve.wait_ge(self.s_l[2], 4 * t + 2)
        var = self.mv[0:p, 2, 0:r, 1]
        nc.vector.tensor_scalar(self.t3[0:p, 0:r], var, EPS, EPS, ALU.add, ALU.mult).then_inc(self.s_l[2], 1)
        dve.wait_ge(self.s_l[2], 4 * t + 3)
        nc.vector.tensor_tensor(self.v3[0:p, 0:r], self.t3[0:p, 0:r], var, ALU.add).then_inc(self.s_m3, 1)

    def dve_x3(self, dve, u, a):
        t = 2 * u + a
        if outside(t):
            return
        dve.wait_ge(self.s_sd3, t + 1)
        need(dve, self.s_x3, t)
        self.scale(dve, t, 2, self.s_l[2], 4 * t + 4, self.s_r3)

    def dve_w(self, dve, u, a):
        t, k = 2 * u + a, a % 2
        if outside(t):
            return
        dve.wait_ge(self.s_w4, t + 1)
        self.stats(dve, self.w, t, k, 3, self.s_l[3], 2 * t + 1).then_inc(self.s_m4, 1)

    def dve_o(self, dve, u, a):
        t = 2 * u + a
        if outside(t):
            return
        dve.wait_ge(self.s_sd4, t + 1)
        need(dve, self.s_o, t)
        self.scale(dve, t, 3, self.s_l[3], 2 * t + 2, self.s_r4)

    def root(self, act, u, a, j, s_from, s_to):
        t = 2 * u + a
        if outside(t):
            return
        p, r = self.rows(t)
        act.wait_ge(s_from, t + 1)
        if j == 2:
            last = self.nc.scalar.activation(self.sd[0:p, j, 0:r], self.v3[0:p, 0:r], ACT.Sqrt)
        else:
            last = self.nc.scalar.activation(self.sd[0:p, j, 0:r], self.mv[0:p, j, 0:r, 1], ACT.Sqrt, bias=self.eps[0:p, :])
        last.then_inc(s_to, 1)

    def act_root1(self, act, u, a):
        self.root(act, u, a, 0, self.s_m1, self.s_sd1)

    def act_root2(self, act, u, a):
        self.root(act, u, a, 1, self.s_m2, self.s_sd2)

    def act_root3(self, act, u, a):
        self.root(act, u, a, 2, self.s_m3, self.s_sd3)

    def act_root4(self, act, u, a):
        self.root(act, u, a, 3, self.s_m4, self.s_sd4)

    def norm(self, act, t, k, j, out, src, s_done):
        p, r = self.rows(t)
        for i in range(r):
            last = self.nc.scalar.activation(out[0:p, k, i, :], src[0:p, k, i, :], ACT.Identity,
                                             bias=self.nb[0:p, j, i:i + 1], scale=self.rs[0:p, j, i:i + 1])
        last.then_inc(s_done, 1)

    def act_n(self, act, u, a):
        t, k = 2 * u + a, a % 2
        if outside(t):
            return
        act.wait_ge(self.s_r2, t + 1)
        need(act, self.s_q, t - 1)
        self.norm(act, t, k, 1, self.n, self.h, self.s_n)

    def act_x3(self, act, u, a):
        t, k = 2 * u + a, a % 2
        if outside(t):
            return
        act.wait_ge(self.s_r3, t + 1)
        need(act, self.s_w4, t - 1)
        self.norm(act, t, k, 2, self.x3, self.y, self.s_x3)

    def act_out(self, act, u, a):
        t, k = 2 * u + a, a % 2
        if outside(t):
            return
        act.wait_ge(self.s_r4, t + 1)
        need(act, self.s_st[k], 16 * (u + a // 2))
        self.norm(act, t, k, 3, self.o, self.w, self.s_o)


def dense_alone(nc, dn, first, last):
    with nc.Block() as block:
        def each(eng, *stages):
            for j in range(first, last):
                for stage, lag in stages:
                    stage(eng, 0, j - lag)

        @block.sync
        def _(sp):
            if first == 0:
                dn.weights(sp)
                dn.load(sp, 0, 0)
            each(sp, (dn.load, -1), (dn.store, LAG_W))
            if last > DS:
                for k in range(2):
                    sp.wait_ge(dn.s_st[k], 16 * ((DS + 2 - k) // 2))

        @block.gpsimd
        def _(pool):
            if first == 0:
                pool.wait_ge(dn.s_c, 1)
            each(pool, (dn.pool_z, 0), (dn.pool_q, LAG_Q), (dn.pool_w, LAG_V))

        @block.vector
        def _(dve):
            if first == 0:
                dn.consts(dve)
                dve.wait_ge(dn.s_c, 1)
            each(dve, (dn.dve_y, LAG_Y), (dn.dve_w, LAG_W), (dn.dve_z, 1), (dn.dve_h, 1), (dn.dve_x3, LAG_Y), (dn.dve_o, LAG_W), (dn.dve_n, 1))

        @block.scalar
        def _(act):
            each(act, (dn.act_root3, LAG_Y), (dn.act_root4, LAG_W), (dn.act_root1, 1), (dn.act_root2, 1), (dn.act_out, LAG_W), (dn.act_x3, LAG_Y), (dn.act_n, 1))


def message_phase(nc, g, K, T, dn, off):
    with ExitStack() as ctx:
        a = Place(nc, ctx, "ms")
        Wx, Wu = a.sb("Wx", [D, D]), a.sb("Wu", [D, D])
        We, emb = a.sb("We", [32, D]), a.sb("emb", [32, 16])
        typeW = a.sb("typeW", [16, D])
        ub, lg, lb = a.sb("ub", [TP, D]), a.sb("lg", [TP, D]), a.sb("lb", [TP, D])
        eps = a.sb("eps", [128, 1])
        kind, kindf = a.sb("kind", [16, 1], I32), a.sb("kindf", [16, 1])
        ring, ringE = ([a.sb(f"{n}{p}", [TP, CT], I32) for p in range(2)] for n in ("ring", "ringE"))
        ga, xt, pg = ([a.sb(f"{n}{p}", s) for p in range(2)] for n, s in (("ga", [TP, CT, D]), ("xt", [TP, CT, D]), ("pg", [TP, CT, 2])))
        xu, xb = ([a.sb(f"{n}{p}", [TP, 2 * CT, D]) for p in range(2)] for n in ("xu", "xb"))
        xs, m, S, oF = (a.sb(n, [D, CE]) for n in ("xs", "m", "S", "oF"))
        carry = a.sb("carry", [D, 1])
        same = a.sb("same", [D, CE])
        typ, oneh = a.sb("typ", [16, CE], I32), a.sb("oneh", [16, CE])
        n1, hg, h2, y = (a.sb(n, [TP, 2 * CT, D]) for n in ("n1", "hg", "h2", "y"))
        st, mv = a.sb("st", [TP, 2 * CT, 6]), a.sb("mv", [TP, 2 * CT, 2])
        sd, rs, nb = (a.sb(n, [TP, 2 * CT]) for n in ("sd", "rs", "nb"))
        pA, pM, pO, pR = (a.ps(n, [128, 512]) for n in ("pA", "pM", "pO", "pR"))
        (s_w, s_go, s_ring, s_ringE, s_pay, s_same, s_typ, s_st, s_eps, s_kind, s_init, s_tw, s_tA, s_xs, s_oneh, s_psM, s_m, s_S, s_psO,
         s_oF, s_psR, s_xu, s_xb, s_h1, s_d, s_dgo, s_mv, s_sd, s_rs, s_r, s_n1, s_hg, s_h2, s_y, s_twc) = (
            a.sem(n) for n in ("weights", "go", "ring", "ringE", "pay", "same", "type", "stored", "eps", "kind", "init", "typeW",
                               "tA", "xs", "onehot", "psM", "m", "S", "psO", "oF", "psR", "xu", "xb", "h1", "stats", "dve_go",
                               "mv", "sd", "rs", "scale", "n1", "hg", "h2", "y", "typeW_copied"))
        s_ga, s_xt, s_pg = ([a.sem(f"{n}{p}") for p in range(2)] for n in ("ga", "xt", "pg"))
        block = ctx.enter_context(nc.Block())

        @block.sync
        def _(sp):
            for t, n in ((Wx, "Wmx"), (Wu, "Wu"), (We, "Wme"), (emb, "embT")):
                sp.dma_start(t[:], g[n]).then_inc(s_w, 16)
            for t, r in ((ub, 1), (lg, 2), (lb, 3)):
                sp.dma_start(t[:], g["rowv"][r:r + 1, :].broadcast_to([TP, D])).then_inc(s_w, 16)

            def load_mask(c):
                sp.dma_start(same[:], T["dsame"][:, bass.ds(CE * c, CE)].broadcast_to([D, CE])).then_inc(s_same, 16)

            def load_types(c):
                sp.dma_start(typ[:], g["type_row"][:, bass.ds(CE * c, CE)].broadcast_to([16, CE])).then_inc(s_typ, 16)

            def load_targets(c, p):
                sp.dma_start(xt[p][:], rows_of(T["T1"], CE * c, CT)).then_inc(s_xt[p], 16)

            def store(c):
                sp.wait_ge(s_y, c + 1)
                sp.dma_start(rows_of(T["T2"], CE * c, CT), y[:, 0:CT, :]).then_inc(s_st, 16)
                sp.dma_start(rows_of(T["T2"], CE * c + E, CT), y[:, CT:2 * CT, :]).then_inc(s_st, 16)

            load_types(0)
            load_mask(0)
            load_targets(0, 0)
            sp.wait_ge(s_oneh, 1)
            load_types(1)

            def chunk(u, a):
                c = 2 * u + a
                dn.load(sp, u, a + off + 1)
                if not last_of(c, 2):
                    sp.wait_ge(s_oneh, c + 2)
                    load_types(c + 2)
                if not last_of(c, 1):
                    sp.wait_ge(s_S, c + 1)
                    load_mask(c + 1)
                if not last_of(c, 1):
                    need(sp, s_xb, c)
                    load_targets(c + 1, (a + 1) % 2)
                if not first_of(c):
                    store(c - 1)
                dn.store(sp, u, a + off - LAG_W)

            chunks(sp, NC - 1)(chunk)
            chunk(0, NC - 1)
            store(NC - 1)
            sp.wait_ge(s_st, 32 * NC)

        @block.gpsimd
        def _(pool):
            nc.gpsimd.iota(kind[:], pattern=[[0, 1]], base=0, channel_multiplier=1).then_inc(s_kind, 1)
            pool.wait_ge(s_kind, 1)
            nc.gpsimd.tensor_copy(kindf[:], kind[:])
            nc.gpsimd.memset(eps[:], EPS).then_inc(s_eps, 1)
            pool.wait_ge(s_w, 16 * 7)
            gathers(pool, s_go, s_ring, s_ga[0], ring[0], K["idxS"], 0, 1, T["T1"], ga[0])

            def keep(u, a):
                c, p = 2 * u + a, a % 2
                pool.wait_ge(s_pg[p], 64 * (u + a // 2 + 1))
                pool.sem_inc(s_go, 1)
                nc.gpsimd.tensor_copy(K["pay"][:, bass.ds(CT * c, CT), 2:4], pg[p][:]).then_inc(s_pay, 1)

            @chunks(pool)
            def _(u, a):
                c, p, p1 = 2 * u + a, a % 2, (a + 1) % 2
                if not last_of(c, 1):
                    if not first_of(c):
                        pool.wait_ge(s_xb, c)
                        pool.wait_ge(s_tA, c)
                        pool.sem_inc(s_go, 1)
                    gathers(pool, s_go, s_ring, s_ga[p1], ring[p1], K["idxS"], c + 1, c + 2, T["T1"], ga[p1])
                need(pool, s_pay, c - 1)
                pool.sem_inc(s_go, 1)
                gathers(pool, s_go, s_ringE, s_pg[p], ringE[p], K["clip"], c, c + 1, T["ptab"], pg[p])
                if not first_of(c):
                    keep(u, a - 1)
                pool.wait_ge(s_ga[p], 64 * (u + a // 2 + 1))
                pool.wait_ge(s_xt[p], 16 * (u + a // 2 + 1))
                need(pool, s_n1, c - 1)
                nc.gpsimd.tensor_tensor(xu[p][:, 0:CT, :], xt[p][:], bc(ub, CT), ALU.add)
                nc.gpsimd.tensor_tensor(xu[p][:, CT:2 * CT, :], ga[p][:], bc(ub, CT), ALU.add).then_inc(s_xu, 1)
                dn.pool_z(pool, u, a + off)
                dn.pool_q(pool, u, a + off - LAG_Q)
                dn.pool_w(pool, u, a + off - LAG_V)
                need(pool, s_h2, c - 1)
                nc.gpsimd.tensor_tensor(xb[p][:, 0:CT, :], xt[p][:], bc(lb, CT), ALU.add)
                nc.gpsimd.tensor_tensor(xb[p][:, CT:2 * CT, :], ga[p][:], bc(lb, CT), ALU.add).then_inc(s_xb, 1)
            keep(0, NC - 1)

        @block.tensor
        def _(pe):
            pe.wait_ge(s_w, 16 * 7)
            nc.tensor.matmul(pM[0:16, 0:D], emb[:], We[:], start=True, stop=True).then_inc(s_tw, 1)
            pe.wait_ge(s_twc, 1)

            def turn(u, a):
                c, p = 2 * u + a, a % 2
                pe.wait_ge(s_ga[p], 64 * (u + a // 2 + 1))
                need(pe, s_xs, c)
                for k in range(CT):
                    last = nc.tensor.transpose(pA[:, k * TP:(k + 1) * TP], ga[p][:, k, :], K["ident"][0:TP, 0:TP])
                last.then_inc(s_tA, 1)

            def message(c):
                pe.wait_ge(s_xs, c + 1)
                pe.wait_ge(s_oneh, c + 1)
                need(pe, s_m, c)
                nc.tensor.matmul(pM[:, 0:CE], Wx[:], xs[:], start=True, stop=False)
                nc.tensor.matmul(pM[:, 0:CE], typeW[:], oneh[:], start=False, stop=True).then_inc(s_psM, 1)

            turn(0, 0)
            message(0)

            @chunks(pe)
            def _(u, a):
                c = 2 * u + a
                if not last_of(c, 1):
                    turn(u, a + 1)
                pe.wait_ge(s_S, c + 1)
                nc.tensor.matmul(pO[:, 0:CE], Wu[:], S[:], start=True, stop=True).then_inc(s_psO, 1)
                if not last_of(c, 1):
                    message(c + 1)
                pe.wait_ge(s_oF, c + 1)
                need(pe, s_h1, c)
                for k in range(CT):
                    last = nc.tensor.transpose(pR[0:TP, k * D:(k + 1) * D], oF[:, k * TP:(k + 1) * TP], K["ident"][:])
                last.then_inc(s_psR, 1)

        @block.scalar
        def _(act):
            act.wait_ge(s_tw, 1)
            nc.scalar.activation(typeW[:], pM[0:16, 0:D], ACT.Copy).then_inc(s_twc, 1)
            act.wait_ge(s_eps, 1)
            act.wait_ge(s_w, 16 * 7)

            def source(c):
                act.wait_ge(s_tA, c + 1)
                need(act, s_psM, c)
                nc.scalar.activation(xs[:], pA[:, 0:CE], ACT.Copy).then_inc(s_xs, 1)

            def message(c):
                act.wait_ge(s_psM, c + 1)
                need(act, s_S, c)
                nc.scalar.activation(m[:], pM[:, 0:CE], ACT.Relu, bias=K["cols"][:, 4:5]).then_inc(s_m, 1)

            def root(n):
                act.wait_ge(s_mv, n)
                nc.scalar.activation(sd[:], mv[:, :, 1], ACT.Sqrt, bias=eps[0:TP, :]).then_inc(s_sd, 1)

            def norm(n, out, rows, s_done):
                act.wait_ge(s_r, n)
                for r in range(2 * CT):
                    last = nc.scalar.activation(out[:, r, :], rows[:, r, :], ACT.Identity, bias=nb[:, r:r + 1], scale=rs[:, r:r + 1])
                last.then_inc(s_done, 1)

            def norm1(u, a):
                c = 2 * u + a
                need(act, s_hg, c)
                norm(2 * c + 1, n1, xu[a % 2], s_n1)

            def norm2(c):
                need(act, s_st, 32 * c)
                norm(2 * c + 2, y, h2, s_y)

            source(0)
            message(0)

            @chunks(act)
            def _(u, a):
                c = 2 * u + a
                if not last_of(c, 1):
                    source(c + 1)
                if not first_of(c):
                    root(2 * c - 1)
                dn.act_root3(act, u, a + off - LAG_Y)
                if not first_of(c):
                    norm1(u, a - 1)
                dn.act_root4(act, u, a + off - LAG_W)
                dn.act_root1(act, u, a + off - 1)
                act.wait_ge(s_psO, c + 1)
                need(act, s_psR, c)
                nc.scalar.activation(oF[:], pO[:, 0:CE], ACT.Copy).then_inc(s_oF, 1)
                if not last_of(c, 1):
                    message(c + 1)
                dn.act_out(act, u, a + off - LAG_W)
                if not first_of(c):
                    root(2 * c)
                dn.act_root2(act, u, a + off - 1)
                if not first_of(c):
                    norm2(c - 1)
                dn.act_x3(act, u, a + off - LAG_Y)
                dn.act_n(act, u, a + off - 1)
            root(2 * NC - 1)
            norm1(0, NC - 1)
            root(2 * NC)
            norm2(NC - 1)

        @block.vector
        def _(dve):
            nc.vector.memset(carry[:], 0.0).then_inc(s_init, 1)
            dve.wait_ge(s_init, 1)
            dve.wait_ge(s_eps, 1)
            dve.wait_ge(s_w, 16 * 7)

            def one_hot(c):
                dve.wait_ge(s_typ, 16 * (c + 1))
                need(dve, s_psM, c)
                nc.vector.tensor_scalar(oneh[:], typ[:], kindf[:, 0:1], None, ALU.is_equal).then_inc(s_oneh, 1)

            def stats(rows, n):
                row_stats(nc, rows, 2 * CT, st, mv, s_d)
                need(dve, s_r, n - 1)
                dve.wait_ge(s_d, n)
                dve.sem_inc(s_dgo, 1)
                row_aggr(nc, 2 * CT, st, mv).then_inc(s_mv, 1)

            def scale(n):
                dve.wait_ge(s_sd, n)
                nc.vector.reciprocal(rs[:], sd[:]).then_inc(s_rs, 1)
                dve.wait_ge(s_rs, n)
                nc.vector.scalar_tensor_tensor(out=nb[:], in0=mv[:, :, 0], scalar=-1.0, in1=rs[:], op0=ALU.mult, op1=ALU.mult).then_inc(s_r, 1)

            def residual(u, a):
                c, p = 2 * u + a, a % 2
                dve.wait_ge(s_xu, c + 1)
                dve.wait_ge(s_psR, c + 1)
                for k in range(CT):
                    last = nc.vector.scalar_tensor_tensor(out=xu[p][:, k, :], in0=pR[0:TP, k * D:(k + 1) * D],
                                                          scalar=K["rdeg"][:, bass.ds(CT * c + k, 1)],
                                                          in1=xu[p][:, k, :], op0=ALU.mult, op1=ALU.add)
                last.then_inc(s_h1, 1)
                dve.wait_ge(s_h1, c + 1)
                stats(xu[p], 2 * c + 1)

            def second(u, a):
                c, p = 2 * u + a, a % 2
                dve.wait_ge(s_n1, c + 1)
                nc.vector.tensor_tensor(hg[:], n1[:], bc(lg, 2 * CT), ALU.mult).then_inc(s_hg, 1)
                dve.wait_ge(s_hg, c + 1)
                dve.wait_ge(s_xb, c + 1)
                need(dve, s_y, c)
                nc.vector.tensor_tensor(h2[:], hg[:], xb[p][:], ALU.add).then_inc(s_h2, 1)
                dve.wait_ge(s_h2, c + 1)
                stats(h2, 2 * c + 2)

            one_hot(0)

            @chunks(dve)
            def _(u, a):
                c = 2 * u + a
                dve.wait_ge(s_m, c + 1)
                dve.wait_ge(s_same, 16 * (c + 1))
                need(dve, s_psO, c)
                nc.vector.tensor_tensor_scan(S[:], same[:], m[:], carry[:], ALU.mult, ALU.add).then_inc(s_S, 1)
                if not last_of(c, 1):
                    one_hot(c + 1)
                if not first_of(c):
                    residual(u, a - 1)
                dve.wait_ge(s_S, c + 1)
                nc.vector.tensor_copy(carry[:], S[:, CE - 1:CE])
                dn.dve_y(dve, u, a + off - LAG_Y)
                if not first_of(c):
                    need(dve, s_y, c - 1)
                    scale(2 * c - 1)
                dn.dve_w(dve, u, a + off - LAG_W)
                dn.dve_z(dve, u, a + off - 1)
                dn.dve_o(dve, u, a + off - LAG_W)
                if not first_of(c):
                    second(u, a - 1)
                dn.dve_x3(dve, u, a + off - LAG_Y)
                dn.dve_h(dve, u, a + off - 1)
                if not first_of(c):
                    scale(2 * c)
                dn.dve_n(dve, u, a + off - 1)
            residual(0, NC - 1)
            dve.wait_ge(s_y, NC - 1)
            scale(2 * NC - 1)
            second(0, NC - 1)
            scale(2 * NC)


def equivariant_phase(nc, g, K, T, dn, off):
    with ExitStack() as ctx:
        a = Place(nc, ctx, "eq")
        A1, B1 = a.sb("A1", [D, D]), a.sb("B1", [D, D])
        fc1 = a.sb("fc1", [8, 64])
        fA, fB, fC = (a.sb(n, [64, D]) for n in ("fA", "fB", "fC"))
        oA, oB, oC = (a.sb(n, [D, D]) for n in ("oA", "oB", "oC"))
        eps = a.sb("eps", [128, 1])
        ring = [a.sb(f"ring{p}", [TP, CT], I32) for p in range(2)]
        ga = [a.sb(f"ga{p}", [TP, CT, D]) for p in range(2)]
        z, y = a.sb("z", [TP, 2 * CT, D]), a.sb("y", [TP, 2 * CT, D])
        xs, sv, se = (a.sb(n, [D, CE]) for n in ("xs", "sv", "se"))
        u1, u2, u3, u4, u5, u6 = (a.sb(f"u{i}", [D, CE]) for i in range(1, 7))
        S = a.sb("S", [D, CE])
        carry = a.sb("carry", [D, 1])
        same = a.sb("same", [D, CE])
        ea8 = a.sb("ea8", [8, CE])
        es, ev = a.sb("es", [D, CE]), a.sb("ev", [D, CE])
        hid, sg = a.sb("hid", [64, CE]), a.sb("sg", [64, CE])
        st, mv = a.sb("st", [TP, 2 * CT, 6]), a.sb("mv", [TP, 2 * CT, 2])
        sd, rs, nb = (a.sb(n, [TP, 2 * CT]) for n in ("sd", "rs", "nb"))
        pX, pP, pQ, pA, pB, pC, pH, pR = (a.ps(n, [128, 512]) for n in ("pX", "pP", "pQ", "pA", "pB", "pC", "pH", "pR"))
        (s_w, s_go, s_ring, s_zd, s_same, s_ea8, s_es, s_st, s_eps, s_init, s_tA, s_xs, s_gac, s_psH, s_sg, s_hid, s_psW,
         s_psX, s_sv, s_v, s_u, s_psO, s_S, s_psR, s_mv, s_sd, s_y, s_d, s_dgo, s_z, s_rs, s_r) = (
            a.sem(n) for n in ("weights", "go", "ring", "zd", "same", "ea8", "es", "stored", "eps", "init", "tA", "xs",
                               "ga_copied", "psH", "sg", "hid", "psW", "psX", "sv", "v", "u", "psO", "S", "psR", "mv", "sd",
                               "y", "stats", "dve_go", "z", "rs", "scale"))
        s_ga = [a.sem(f"ga{p}") for p in range(2)]
        rslot, rpay = a.sb("rslot", [TP, CT], I32), a.sb("rpay", [TP, CT, 4])
        s_ringP, s_pay = a.sem("ringP"), a.sem("pay")
        block = ctx.enter_context(nc.Block())
        by_lin1 = 1.0 / 32.0 ** 0.5
        by_rest = SILU / (64.0 ** 0.5) / (16.0 ** 0.5) / (64.0 ** 0.5)

        @block.sync
        def _(sp):
            for t, n in ((A1, "L1A"), (B1, "L1B"), (fc1, "fc1"), (fA, "fcA"), (fB, "fcB"), (fC, "fcC"), (oA, "oA"), (oB, "oB"), (oC, "oC")):
                sp.dma_start(t[:], g[n]).then_inc(s_w, 16)

            def load_mask(c):
                sp.dma_start(same[:], T["dsame"][:, bass.ds(CE * c, CE)].broadcast_to([D, CE])).then_inc(s_same, 16)

            def load_scalars(c):
                sp.dma_start(ea8[:], g["ea8T"][:, bass.ds(CE * c, CE)]).then_inc(s_ea8, 16)

            def load_attr(c):
                sp.dma_start(es[:], g["ea4T"][0:1, bass.ds(CE * c, CE)].broadcast_to([D, CE])).then_inc(s_es, 16)
                for j in range(4):
                    sp.dma_start(ev[32 * j:32 * j + 32, :], g["ea4T"][j:j + 1, bass.ds(CE * c, CE)].broadcast_to([32, CE])).then_inc(s_es, 16)

            def store(c):
                sp.wait_ge(s_y, c + 1)
                sp.dma_start(rows_of(T["T3"], CE * c, CT), y[:, 0:CT, :]).then_inc(s_st, 16)
                sp.dma_start(rows_of(T["T3"], CE * c + E, CT), y[:, CT:2 * CT, :]).then_inc(s_st, 16)

            load_mask(0)
            load_scalars(0)
            load_attr(0)
            sp.wait_ge(s_psH, 1)
            load_scalars(1)

            def chunk(u, a):
                c = 2 * u + a
                dn.load(sp, u, a + off + 1)
                if not last_of(c, 2):
                    sp.wait_ge(s_psH, c + 2)
                    load_scalars(c + 2)
                if not last_of(c, 1):
                    sp.wait_ge(s_v, c + 1)
                    load_attr(c + 1)
                need(sp, s_y, c)
                sp.dma_start(z[:, 0:CT, :], rows_of(T["T2"], CE * c, CT)).then_inc(s_zd, 16)
                if not first_of(c):
                    store(c - 1)
                dn.store(sp, u, a + off - LAG_W)
                if not last_of(c, 1):
                    sp.wait_ge(s_S, c + 1)
                    load_mask(c + 1)

            chunks(sp, NC - 1)(chunk)
            chunk(0, NC - 1)
            store(NC - 1)
            sp.wait_ge(s_st, 32 * NC)

        @block.gpsimd
        def _(pool):
            nc.gpsimd.memset(eps[:], EPS).then_inc(s_eps, 1)
            gathers(pool, s_go, s_ring, s_ga[0], ring[0], K["idxS"], 0, 1, T["T2"], ga[0])

            @chunks(pool)
            def _(u, a):
                c, p = 2 * u + a, (a + 1) % 2
                if not last_of(c, 1):
                    if not first_of(c):
                        pool.wait_ge(s_gac, c)
                        pool.wait_ge(s_tA, c)
                        pool.sem_inc(s_go, 1)
                    gathers(pool, s_go, s_ring, s_ga[p], ring[p], K["idxS"], c + 1, c + 2, T["T2"], ga[p])
                need(pool, s_pay, 64 * c)
                pool.sem_inc(s_go, 1)
                nc.gpsimd.tensor_copy(rpay[:], K["pay"][:, bass.ds(CT * c, CT), :])
                nc.gpsimd.tensor_copy(rslot[:], K["slot"][:, bass.ds(CT * c, CT)]).then_inc(s_ringP, 1)
                pool.wait_ge(s_ringP, c + 1)
                pool.sem_inc(s_go, 1)
                for k in range(CT):
                    nc.gpsimd.indirect_dma_start(out=T["S4"], out_offset=bass.IndirectOffsetOnAxis(ap=rslot[:, k:k + 1], axis=0),
                                                 in_=rpay[:, k, :], in_offset=None).then_inc(s_pay, 16)
                dn.pool_z(pool, u, a + off)
                dn.pool_q(pool, u, a + off - LAG_Q)
                dn.pool_w(pool, u, a + off - LAG_V)
            pool.wait_ge(s_pay, 16 * NT)

        @block.tensor
        def _(pe):
            pe.wait_ge(s_w, 16 * 9)

            def net(c):
                pe.wait_ge(s_ea8, 16 * (c + 1))
                nc.tensor.matmul(pH[0:64, 0:CE], fc1[:], ea8[:], start=True, stop=True).then_inc(s_psH, 1)

            def turn(u, a):
                pe.wait_ge(s_ga[a % 2], 64 * (u + a // 2 + 1))
                for k in range(CT):
                    last = nc.tensor.transpose(pX[:, k * TP:(k + 1) * TP], ga[a % 2][:, k, :], K["ident"][0:TP, 0:TP])
                last.then_inc(s_tA, 1)

            def features(c):
                pe.wait_ge(s_xs, c + 1)
                nc.tensor.matmul(pP[:, 0:CE], A1[:], xs[:], start=True, stop=True)
                nc.tensor.matmul(pQ[:, 0:CE], B1[:], xs[:], start=True, stop=True).then_inc(s_psX, 1)

            def weights(c):
                pe.wait_ge(s_hid, c + 1)
                for w, p in ((fA, pA), (fB, pB), (fC, pC)):
                    last = nc.tensor.matmul(p[:, 0:CE], w[:], hid[:], start=True, stop=True)
                last.then_inc(s_psW, 1)

            net(0)
            turn(0, 0)
            features(0)
            weights(0)

            @chunks(pe)
            def _(u, a):
                c = 2 * u + a
                if not last_of(c, 1):
                    need(pe, s_S, c)
                    net(c + 1)
                    turn(u, a + 1)
                pe.wait_ge(s_u, c + 1)
                if not last_of(c, 1):
                    pe.wait_ge(s_xs, c + 2)
                nc.tensor.matmul(pX[:, 0:CE], oA[:], u2[:], start=True, stop=False)
                nc.tensor.matmul(pX[:, 0:CE], oB[:], u4[:], start=False, stop=False)
                nc.tensor.matmul(pX[:, 0:CE], oC[:], u6[:], start=False, stop=True).then_inc(s_psO, 1)
                if not last_of(c, 1):
                    features(c + 1)
                    weights(c + 1)
                pe.wait_ge(s_S, c + 1)
                need(pe, s_z, c)
                for k in range(CT):
                    last = nc.tensor.transpose(pR[0:TP, k * D:(k + 1) * D], S[:, k * TP:(k + 1) * TP], K["ident"][:])
                last.then_inc(s_psR, 1)

        @block.scalar
        def _(act):
            act.wait_ge(s_eps, 1)

            def gate(c):
                act.wait_ge(s_psH, c + 1)
                nc.scalar.activation(sg[:], pH[0:64, 0:CE], ACT.Sigmoid, scale=1.0 / 8.0 ** 0.5).then_inc(s_sg, 1)

            def source(c):
                act.wait_ge(s_tA, c + 1)
                nc.scalar.activation(xs[:], pX[:, 0:CE], ACT.Copy).then_inc(s_xs, 1)

            def features(c):
                act.wait_ge(s_psX, c + 1)
                nc.scalar.activation(sv[:], pP[:, 0:CE], ACT.Copy, scale=by_lin1)
                nc.scalar.activation(se[:], pQ[:, 0:CE], ACT.Copy, scale=by_lin1).then_inc(s_sv, 1)

            def root(c):
                act.wait_ge(s_mv, c + 1)
                nc.scalar.activation(sd[:], mv[:, :, 1], ACT.Sqrt, bias=eps[0:TP, :]).then_inc(s_sd, 1)

            def norm(c):
                act.wait_ge(s_r, c + 1)
                need(act, s_st, 32 * c)
                for r in range(2 * CT):
                    last = nc.scalar.activation(y[:, r, :], z[:, r, :], ACT.Identity, bias=nb[:, r:r + 1], scale=rs[:, r:r + 1])
                last.then_inc(s_y, 1)

            gate(0)
            source(0)
            features(0)

            @chunks(act)
            def _(u, a):
                c = 2 * u + a
                if not last_of(c, 1):
                    act.wait_ge(s_hid, c + 1)
                    gate(c + 1)
                    act.wait_ge(s_psX, c + 1)
                    source(c + 1)
                dn.act_root3(act, u, a + off - LAG_Y)
                if not first_of(c):
                    root(c - 1)
                dn.act_root4(act, u, a + off - LAG_W)
                dn.act_root1(act, u, a + off - 1)
                if not first_of(c):
                    norm(c - 1)
                if not last_of(c, 1):
                    act.wait_ge(s_u, c + 1)
                    features(c + 1)
                need(act, s_y, c)
                nc.scalar.activation(z[:, CT:2 * CT, :], ga[a % 2][:], ACT.Copy).then_inc(s_gac, 1)
                dn.act_root2(act, u, a + off - 1)
                dn.act_out(act, u, a + off - LAG_W)
                dn.act_x3(act, u, a + off - LAG_Y)
                dn.act_n(act, u, a + off - 1)
            root(NC - 1)
            norm(NC - 1)

        @block.vector
        def _(dve):
            nc.vector.memset(carry[:], 0.0).then_inc(s_init, 1)
            dve.wait_ge(s_init, 1)
            dve.wait_ge(s_eps, 1)

            def hidden(c):
                dve.wait_ge(s_sg, c + 1)
                nc.vector.scalar_tensor_tensor(out=hid[:], in0=pH[0:64, 0:CE], scalar=1.0 / 8.0 ** 0.5, in1=sg[:],
                                               op0=ALU.mult, op1=ALU.mult).then_inc(s_hid, 1)

            def residual(c):
                dve.wait_ge(s_zd, 16 * (c + 1))
                dve.wait_ge(s_gac, c + 1)
                dve.wait_ge(s_psR, c + 1)
                nc.vector.tensor_tensor(z[:, 0:CT, :], z[:, 0:CT, :], pR[0:TP, :].rearrange("p (k f) -> p k f", k=CT), ALU.add).then_inc(s_z, 1)
                dve.wait_ge(s_z, c + 1)
                row_stats(nc, z, 2 * CT, st, mv, s_d)
                need(dve, s_r, c)
                dve.wait_ge(s_d, c + 1)
                dve.sem_inc(s_dgo, 1)
                row_aggr(nc, 2 * CT, st, mv).then_inc(s_mv, 1)

            def scale(c):
                dve.wait_ge(s_sd, c + 1)
                need(dve, s_y, c)
                nc.vector.reciprocal(rs[:], sd[:]).then_inc(s_rs, 1)
                dve.wait_ge(s_rs, c + 1)
                nc.vector.scalar_tensor_tensor(out=nb[:], in0=mv[:, :, 0], scalar=-1.0, in1=rs[:], op0=ALU.mult, op1=ALU.mult).then_inc(s_r, 1)

            hidden(0)

            @chunks(dve)
            def _(u, a):
                c = 2 * u + a
                dve.wait_ge(s_es, 80 * (c + 1))
                dve.wait_ge(s_psW, c + 1)
                need(dve, s_u, c)
                nc.vector.scalar_tensor_tensor(out=u1[:], in0=pA[:, 0:CE], scalar=by_rest, in1=es[:], op0=ALU.mult, op1=ALU.mult)
                nc.vector.scalar_tensor_tensor(out=u3[:], in0=pB[:, 0:CE], scalar=by_rest, in1=ev[:], op0=ALU.mult, op1=ALU.mult)
                nc.vector.scalar_tensor_tensor(out=u5[:], in0=pC[:, 0:CE], scalar=by_rest / 3.0 ** 0.5, in1=ev[:],
                                               op0=ALU.mult, op1=ALU.mult).then_inc(s_v, 1)
                dve.wait_ge(s_v, c + 1)
                dve.wait_ge(s_sv, c + 1)
                need(dve, s_psO, c)
                nc.vector.tensor_tensor(u2[:], u1[:], sv[:], ALU.mult)
                nc.vector.tensor_tensor(u4[:], u3[:], se[:], ALU.mult)
                nc.vector.tensor_tensor(u6[:], u5[:], sv[:], ALU.mult).then_inc(s_u, 1)
                if not first_of(c):
                    residual(c - 1)
                if not last_of(c, 1):
                    hidden(c + 1)
                dn.dve_y(dve, u, a + off - LAG_Y)
                if not first_of(c):
                    scale(c - 1)
                dn.dve_w(dve, u, a + off - LAG_W)
                dve.wait_ge(s_same, 16 * (c + 1))
                dve.wait_ge(s_psO, c + 1)
                nc.vector.tensor_tensor_scan(S[:], same[:], pX[:, 0:CE], carry[:], ALU.mult, ALU.add).then_inc(s_S, 1)
                dn.dve_z(dve, u, a + off - 1)
                dve.wait_ge(s_S, c + 1)
                nc.vector.tensor_copy(carry[:], S[:, CE - 1:CE])
                dn.dve_x3(dve, u, a + off - LAG_Y)
                dn.dve_o(dve, u, a + off - LAG_W)
                dn.dve_h(dve, u, a + off - 1)
                dn.dve_n(dve, u, a + off - 1)
            residual(NC - 1)
            scale(NC - 1)


def hyperedge_phase(nc, g, K, T, tag, table, index, weight, out):
    with ExitStack() as ctx:
        a = Place(nc, ctx, tag)
        W = a.sb("W", [D, D])
        ring = [a.sb(f"ring{p}", [TP, CT], I32) for p in range(2)]
        ga = [a.sb(f"ga{p}", [TP, CT, D]) for p in range(2)]
        y = [a.sb(f"y{p}", [TP, CT, D]) for p in range(2)]
        same = [a.sb(f"same{p}", [D, CE]) for p in range(2)]
        xs, S = a.sb("xs", [D, CE]), a.sb("S", [D, CE])
        carry, zrow = a.sb("carry", [D, 1]), a.sb("zrow", [1, D])
        pX = [a.ps(f"pX{p}", [128, 512]) for p in range(2)]
        pM = [a.ps(f"pM{p}", [128, 512]) for p in range(2)]
        pR = [a.ps(f"pR{p}", [128, 512]) for p in range(2)]
        s_w, s_go, s_ring, s_init, s_tA, s_xs, s_psM, s_S, s_psR, s_y = (
            a.sem(n) for n in ("weights", "go", "ring", "init", "tA", "xs", "psM", "S", "psR", "y"))
        s_ga, s_same, s_st = ([a.sem(f"{n}{p}") for p in range(2)] for n in ("ga", "same", "stored"))
        block = ctx.enter_context(nc.Block())

        @block.sync
        def _(sp):
            if weight:
                sp.dma_start(W[:], g[weight]).then_inc(s_w, 16)

            def load_mask(c, p):
                sp.dma_start(same[p][:], T["dsame"][:, bass.ds(CE * c, CE)].broadcast_to([D, CE])).then_inc(s_same[p], 16)

            load_mask(0, 0)
            load_mask(1, 1)
            @chunks(sp)
            def _(u, a):
                c, p = 2 * u + a, a % 2
                if not (isinstance(c, int) and c + 2 >= NC):
                    sp.wait_ge(s_S, c + 1)
                    load_mask(c + 2, p)
                sp.wait_ge(s_y, c + 1)
                sp.dma_start(rows_of(out, CE * c, CT), y[p][:]).then_inc(s_st[p], 16)
            sp.dma_start(out[E:E + 1, :], zrow[:]).then_inc(s_w, 16)
            sp.wait_ge(s_st[0], 16 * (NC // 2 + 1))
            sp.wait_ge(s_st[1], 16 * (NC // 2))
            sp.wait_ge(s_w, 32 if weight else 16)

        @block.gpsimd
        def _(pool):
            @chunks(pool)
            def _(u, a):
                c, p = 2 * u + a, a % 2
                need(pool, s_tA, c - 1)
                pool.sem_inc(s_go, 1)
                gathers(pool, s_go, s_ring, s_ga[p], ring[p], index, c, c + 1, table, ga[p])

        @block.tensor
        def _(pe):
            if weight:
                pe.wait_ge(s_w, 16)

            def back(u, a):
                c, p = 2 * u + a, a % 2
                pe.wait_ge(s_S, c + 1)
                need(pe, s_y, c)
                for k in range(CT):
                    last = nc.tensor.transpose(pR[p][0:TP, k * D:(k + 1) * D], S[:, k * TP:(k + 1) * TP], K["ident"][:])
                last.then_inc(s_psR, 1)

            @chunks(pe)
            def _(u, a):
                c, p = 2 * u + a, a % 2
                pe.wait_ge(s_ga[p], 64 * (u + a // 2 + 1))
                if weight:
                    need(pe, s_xs, c - 1)
                else:
                    need(pe, s_S, c - 1)
                for k in range(CT):
                    last = nc.tensor.transpose(pX[p][:, k * TP:(k + 1) * TP], ga[p][:, k, :], K["ident"][0:TP, 0:TP])
                last.then_inc(s_tA, 1)
                if not (isinstance(c, int) and c == 0):
                    back(u, a - 1)
                if weight:
                    pe.wait_ge(s_xs, c + 1)
                    need(pe, s_S, c - 1)
                    nc.tensor.matmul(pM[p][:, 0:CE], W[:], xs[:], start=True, stop=True).then_inc(s_psM, 1)
            back(0, NC - 1)

        @block.scalar
        def _(act):
            if weight:
                @chunks(act)
                def _(u, a):
                    c, p = 2 * u + a, a % 2
                    act.wait_ge(s_tA, c + 1)
                    need(act, s_psM, c)
                    nc.scalar.activation(xs[:], pX[p][:, 0:CE], ACT.Copy).then_inc(s_xs, 1)

        @block.vector
        def _(dve):
            nc.vector.memset(carry[:], 0.0)
            nc.vector.memset(zrow[:], 0.0).then_inc(s_init, 1)
            dve.wait_ge(s_init, 1)
            @chunks(dve)
            def _(u, a):
                c, p = 2 * u + a, a % 2
                dve.wait_ge(s_same[p], 16 * (u + a // 2 + 1))
                need(dve, s_psR, c)
                if weight:
                    dve.wait_ge(s_psM, c + 1)
                else:
                    dve.wait_ge(s_tA, c + 1)
                nc.vector.tensor_tensor_scan(S[:], same[p][:], (pM if weight else pX)[p][:, 0:CE], carry[:], ALU.mult, ALU.add).then_inc(s_S, 1)
                dve.wait_ge(s_S, c + 1)
                nc.vector.tensor_copy(carry[:], S[:, CE - 1:CE])
                dve.wait_ge(s_psR, c + 1)
                need(dve, s_st[p], 16 * (u + a // 2))
                for k in range(CT):
                    last = nc.vector.tensor_scalar(y[p][:, k, :], pR[p][0:TP, k * D:(k + 1) * D], K["rdegH"][:, bass.ds(CT * c + k, 1)], None, ALU.mult)
                last.then_inc(s_y, 1)
                dve.wait_ge(s_y, c + 1)


def node_phase(nc, g, K, T, H):
    with ExitStack() as ctx:
        a = Place(nc, ctx, "nd")
        ring, rinx = ([a.sb(f"{n}{p}", [TP, CT], I32) for p in range(2)] for n in ("ring", "rinx"))
        ga, gb = ([a.sb(f"{n}{p}", [TP, CT, D]) for p in range(2)] for n in ("ga", "gb"))
        same, dinv = ([a.sb(f"{n}{p}", [D, CE]) for p in range(2)] for n in ("same", "dinv"))
        S, sq, h = a.sb("S", [D, CE]), a.sb("sq", [D, CE]), [a.sb(f"h{p}", [D, CE]) for p in range(2)]
        cS = a.sb("cS", [D, 1])
        acc = [a.sb(f"acc{p}", [D, 2]) for p in range(2)]
        pX = [a.ps(f"pX{p}", [128, 512]) for p in range(2)]
        s_go, s_ringA, s_ringB, s_init, s_tA, s_S, s_h, s_sq, s_sum = (
            a.sem(n) for n in ("go", "ringA", "ringB", "init", "tA", "S", "h", "sq", "sum"))
        s_ga, s_gb, s_rows, s_st, s_hst = ([a.sem(f"{n}{p}") for p in range(2)] for n in ("ga", "gb", "rows", "stored", "h_stored"))
        block = ctx.enter_context(nc.Block())

        @block.sync
        def _(sp):
            def load_rows(c, p):
                sp.dma_start(same[p][:], T["ssame"][:, bass.ds(CE * c, CE)].broadcast_to([D, CE])).then_inc(s_rows[p], 16)
                sp.dma_start(dinv[p][:], T["dinv"][:, bass.ds(CE * c, CE)].broadcast_to([D, CE])).then_inc(s_rows[p], 16)

            load_rows(0, 0)
            load_rows(1, 1)
            @chunks(sp)
            def _(u, a):
                c, p = 2 * u + a, a % 2
                sp.wait_ge(s_gb[p], 64 * (u + a // 2 + 1))
                sp.dma_start(rows_of(T["TS"], CE * c, CT), gb[p][:]).then_inc(s_st[p], 16)
                if not (isinstance(c, int) and c + 2 >= NC):
                    sp.wait_ge(s_h, c + 1)
                    load_rows(c + 2, p)
            for s in s_st:
                sp.wait_ge(s, 16 * (NC // 2 + (s is s_st[0])))

        @block.gpsimd
        def _(pool):
            @chunks(pool)
            def _(u, a):
                c, p = 2 * u + a, a % 2
                need(pool, s_tA, c - 1)
                pool.sem_inc(s_go, 1)
                gathers(pool, s_go, s_ringA, s_ga[p], ring[p], K["s_idxE"], c, c + 1, T["TE"], ga[p])
                need(pool, s_st[p], 16 * (u + a // 2))
                pool.sem_inc(s_go, 1)
                gathers(pool, s_go, s_ringB, s_gb[p], rinx[p], K["s_idxS"], c, c + 1, T["T3"], gb[p])

        @block.tensor
        def _(pe):
            @chunks(pe)
            def _(u, a):
                c, p = 2 * u + a, a % 2
                pe.wait_ge(s_ga[p], 64 * (u + a // 2 + 1))
                need(pe, s_S, c - 1)
                for k in range(CT):
                    last = nc.tensor.transpose(pX[p][:, k * TP:(k + 1) * TP], ga[p][:, k, :], K["ident"][0:TP, 0:TP])
                last.then_inc(s_tA, 1)

        @block.scalar
        def _(act):
            @chunks(act)
            def _(u, a):
                c, p = 2 * u + a, a % 2
                act.wait_ge(s_h, c + 1)
                need(act, s_sum, c - 1)
                need(act, s_sq, c)
                nc.scalar.activation(sq[:], h[p][:], ACT.Square, accum_out=acc[p][:, 1:2])
                nc.scalar.activation(H["h"][:, bass.ds(CE * c, CE)], h[p][:], ACT.Copy).then_inc(s_sq, 1)

        @block.vector
        def _(dve):
            nc.vector.memset(H["sum"][:], 0.0)
            nc.vector.memset(cS[:], 0.0).then_inc(s_init, 1)
            dve.wait_ge(s_init, 1)

            def total(u, a):
                c, p = 2 * u + a, a % 2
                dve.wait_ge(s_sq, c + 1)
                need(dve, s_sum, c)
                nc.vector.tensor_tensor(H["sum"][:], H["sum"][:], acc[p][:], ALU.add).then_inc(s_sum, 1)

            @chunks(dve)
            def _(u, a):
                c, p = 2 * u + a, a % 2
                dve.wait_ge(s_rows[p], 32 * (u + a // 2 + 1))
                dve.wait_ge(s_tA, c + 1)
                need(dve, s_h, c)
                nc.vector.tensor_tensor_scan(S[:], same[p][:], pX[p][:, 0:CE], cS[:], ALU.mult, ALU.add).then_inc(s_S, 1)
                if not (isinstance(c, int) and c == 0):
                    total(u, a - 1)
                dve.wait_ge(s_S, c + 1)
                nc.vector.tensor_copy(cS[:], S[:, CE - 1:CE])
                nc.vector.scalar_tensor_tensor(out=h[p][:], in0=S[:], scalar=1.0, in1=dinv[p][:],
                                               op0=ALU.mult, op1=ALU.mult, accum_out=acc[p][:, 0:1]).then_inc(s_h, 1)
            total(0, NC - 1)


def batchnorm_phase(nc, g, K, T, H):
    with ExitStack() as ctx:
        a = Place(nc, ctx, "bn")
        W = a.sb("W", [D, D])
        v = a.sb("v", [D, 12])
        eps, b2 = a.sb("eps", [128, 1]), a.sb("b2", [TP, D])
        hp, oF = a.sb("hp", [D, CE]), a.sb("oF", [D, CE])
        y, x, z, o = ([a.sb(f"{n}{p}", [TP, CT, D]) for p in range(2)] for n in ("y", "x", "z", "o"))
        rout = [a.sb(f"rout{p}", [TP, CT], I32) for p in range(2)]
        st, mv, tsd, trs = a.sb("st", [TP, CT, 6]), a.sb("mv", [TP, CT, 2]), a.sb("tsd", [TP, CT]), a.sb("trs", [TP, CT])
        pM, pR = (([a.ps(f"{n}{p}", [128, 512]) for p in range(2)]) for n in ("pM", "pR"))
        s_w, s_ch, s_a, s_sd, s_hp, s_psM, s_oF, s_psR, s_y, s_go, s_ring, s_z, s_d, s_dgo, s_mv, s_tsd, s_rs, s_o = (
            a.sem(n) for n in ("weights", "chain", "affine", "sd", "hp", "psM", "oF", "psR", "y", "go", "ring", "z", "stats", "dve_go",
                               "mv", "target_sd", "rs", "o"))
        s_st, s_x, s_out = ([a.sem(f"{n}{p}") for p in range(2)] for n in ("stored", "x", "out"))
        block = ctx.enter_context(nc.Block())
        b1, gam, bet = K["cols"][:, 5:6], K["cols"][:, 6:7], K["cols"][:, 7:8]
        m, m2, var, sd, rs, scale, t, bias = (v[:, i:i + 1] for i in range(8))

        @block.sync
        def _(sp):
            sp.dma_start(W[:], g["W2"]).then_inc(s_w, 16)
            sp.dma_start(b2[:], g["rowv"][4:5, :].broadcast_to([TP, D])).then_inc(s_w, 16)
            for p in range(2):
                sp.dma_start(x[p][:], rows_of(T["T3"], CE * p, CT)).then_inc(s_x[p], 16)
            @chunks(sp)
            def _(u, a):
                c, p = 2 * u + a, a % 2
                sp.wait_ge(s_y, c + 1)
                sp.dma_start(rows_of(T["TH"], CE * c, CT), y[p][:]).then_inc(s_st[p], 16)
                if not (isinstance(c, int) and c + 2 >= NC):
                    sp.wait_ge(s_z, c + 1)
                    sp.dma_start(x[p][:], rows_of(T["T3"], CE * c + 2 * CE, CT)).then_inc(s_x[p], 16)
            for s in s_st:
                sp.wait_ge(s, 16 * (NC // 2 + (s is s_st[0])))

        @block.gpsimd
        def _(pool):
            @chunks(pool)
            def _(u, a):
                c, p = 2 * u + a, a % 2
                need(pool, s_out[p], 64 * (u + a // 2))
                pool.sem_inc(s_go, 1)
                nc.gpsimd.tensor_copy(rout[p][:], K["dst_end"][:, bass.ds(CT * c, CT)]).then_inc(s_ring, 1)
                pool.wait_ge(s_ring, c + 1)
                pool.wait_ge(s_o, c + 1)
                pool.sem_inc(s_go, 1)
                for k in range(CT):
                    nc.gpsimd.indirect_dma_start(out=T["out"], out_offset=bass.IndirectOffsetOnAxis(ap=rout[p][:, k:k + 1], axis=0),
                                                 in_=o[p][:, k, :], in_offset=None, bounds_check=N - 1, oob_is_err=False).then_inc(s_out[p], 16)
            for s in s_out:
                pool.wait_ge(s, 64 * (NC // 2 + (s is s_out[0])))

        @block.vector
        def _(dve):
            link = Chain(dve, s_ch)
            nc.vector.memset(eps[:], EPS)
            link(nc.vector.tensor_scalar(m, H["sum"][:, 0:1], 1.0 / N, None, ALU.mult))
            link(nc.vector.tensor_tensor(m2, m, m, ALU.mult))
            nc.vector.scalar_tensor_tensor(out=var, in0=H["sum"][:, 1:2], scalar=1.0 / N, in1=m2, op0=ALU.mult, op1=ALU.subtract).then_inc(s_a, 1)
            dve.wait_ge(s_sd, 1)
            link(nc.vector.reciprocal(rs, sd))
            link(nc.vector.tensor_tensor(scale, rs, gam, ALU.mult))
            link(nc.vector.tensor_tensor(t, m, scale, ALU.mult))
            nc.vector.tensor_tensor(bias, bet, t, ALU.subtract).then_inc(s_a, 1)
            dve.wait_ge(s_w, 32)
            @chunks(dve)
            def _(u, a):
                c, p = 2 * u + a, a % 2
                dve.wait_ge(s_x[p], 16 * (u + a // 2 + 1))
                need(dve, s_o, c - 1)
                nc.vector.tensor_tensor(z[p][:], x[p][:], bc(b2, CT), ALU.add).then_inc(s_z, 1)
                dve.wait_ge(s_z, c + 1)
                row_stats(nc, z[p], CT, st, mv, s_d)
                dve.wait_ge(s_d, c + 1)
                need(dve, s_o, c)
                dve.sem_inc(s_dgo, 1)
                row_aggr(nc, CT, st, mv).then_inc(s_mv, 1)
                dve.wait_ge(s_psR, c + 1)
                need(dve, s_st[p], 16 * (u + a // 2))
                nc.vector.tensor_copy(y[p][:], pR[p][0:TP, :].rearrange("p (k f) -> p k f", k=CT)).then_inc(s_y, 1)
                dve.wait_ge(s_tsd, c + 1)
                nc.vector.reciprocal(trs[:], tsd[:]).then_inc(s_rs, 1)
                dve.wait_ge(s_rs, c + 1)
                need(dve, s_out[p], 64 * (u + a // 2))
                normalize(nc, o[p], z[p], CT, mv, trs).then_inc(s_o, 1)
                dve.wait_ge(s_o, c + 1)

        @block.scalar
        def _(act):
            act.wait_ge(s_a, 1)
            nc.scalar.activation(sd, var, ACT.Sqrt, bias=eps[:]).then_inc(s_sd, 1)
            act.wait_ge(s_a, 2)
            @chunks(act)
            def _(u, a):
                c, p = 2 * u + a, a % 2
                need(act, s_psM, c)
                nc.scalar.activation(hp[:], H["h"][:, bass.ds(CE * c, CE)], ACT.Identity, bias=bias, scale=scale).then_inc(s_hp, 1)
                act.wait_ge(s_psM, c + 1)
                need(act, s_psR, c)
                nc.scalar.activation(oF[:], pM[p][:, 0:CE], ACT.Copy).then_inc(s_oF, 1)
                act.wait_ge(s_mv, c + 1)
                nc.scalar.activation(tsd[:], mv[:, :, 1], ACT.Sqrt, bias=eps[0:TP, :]).then_inc(s_tsd, 1)

        @block.tensor
        def _(pe):
            pe.wait_ge(s_w, 32)
            @chunks(pe)
            def _(u, a):
                c, p = 2 * u + a, a % 2
                pe.wait_ge(s_hp, c + 1)
                need(pe, s_oF, c - 1)
                nc.tensor.matmul(pM[p][:, 0:CE], W[:], hp[:], start=True, stop=True).then_inc(s_psM, 1)
                pe.wait_ge(s_oF, c + 1)
                need(pe, s_y, c - 1)
                for k in range(CT):
                    last = nc.tensor.transpose(pR[p][0:TP, k * D:(k + 1) * D], oF[:, k * TP:(k + 1) * TP], K["ident"][:])
                last.then_inc(s_psR, 1)


def result_phase(nc, g, K, T):
    with ExitStack() as ctx:
        a = Place(nc, ctx, "rs")
        eps = a.sb("eps", [128, 1])
        ring, rout = ([a.sb(f"{n}{p}", [TP, CT], I32) for p in range(2)] for n in ("ring", "rout"))
        ga, x, y = ([a.sb(f"{n}{p}", [TP, CT, D]) for p in range(2)] for n in ("ga", "x", "y"))
        same, dinv = ([a.sb(f"{n}{p}", [D, CE]) for p in range(2)] for n in ("same", "dinv"))
        z = a.sb("z", [TP, CT, D])
        S, o, oF = (a.sb(n, [D, CE]) for n in ("S", "o", "oF"))
        cS = a.sb("cS", [D, 1])
        st, mv, sd, rs = a.sb("st", [TP, CT, 6]), a.sb("mv", [TP, CT, 2]), a.sb("sd", [TP, CT]), a.sb("rs", [TP, CT])
        pX, pR = ([a.ps(f"{n}{p}", [128, 512]) for p in range(2)] for n in ("pX", "pR"))
        (s_go, s_ringA, s_ringO, s_init, s_eps, s_tA, s_S, s_o, s_oF, s_psR, s_z, s_d, s_dgo, s_mv, s_sd, s_y, s_rs) = (
            a.sem(n) for n in ("go", "ringA", "ringO", "init", "eps", "tA", "S", "o", "oF", "psR", "z", "stats", "dve_go", "mv", "sd", "y", "rs"))
        s_ga, s_x, s_rows, s_out = ([a.sem(f"{n}{p}") for p in range(2)] for n in ("ga", "x", "rows", "out"))
        block = ctx.enter_context(nc.Block())

        @block.sync
        def _(sp):
            def load_rows(c, p):
                sp.dma_start(same[p][:], T["ssame"][:, bass.ds(CE * c, CE)].broadcast_to([D, CE])).then_inc(s_rows[p], 16)
                sp.dma_start(dinv[p][:], T["dinv"][:, bass.ds(CE * c, CE)].broadcast_to([D, CE])).then_inc(s_rows[p], 16)

            def load_states(c, p):
                sp.dma_start(x[p][:], rows_of(T["TS"], CE * c, CT)).then_inc(s_x[p], 16)

            for p in range(2):
                load_rows(p, p)
                load_states(p, p)
            @chunks(sp, NC - 2)
            def _(u, a):
                c, p = 2 * u + a, a % 2
                sp.wait_ge(s_o, c + 1)
                load_rows(c + 2, p)
                sp.wait_ge(s_z, c + 1)
                load_states(c + 2, p)

        @block.gpsimd
        def _(pool):
            nc.gpsimd.memset(eps[:], EPS).then_inc(s_eps, 1)

            def scatter(u, a):
                c, p = 2 * u + a, a % 2
                need(pool, s_out[p], 64 * (u + a // 2))
                pool.sem_inc(s_go, 1)
                nc.gpsimd.tensor_copy(rout[p][:], K["src_end"][:, bass.ds(CT * c, CT)]).then_inc(s_ringO, 1)
                pool.wait_ge(s_ringO, c + 1)
                pool.wait_ge(s_y, c + 1)
                pool.sem_inc(s_go, 1)
                for k in range(CT):
                    nc.gpsimd.indirect_dma_start(out=T["out"], out_offset=bass.IndirectOffsetOnAxis(ap=rout[p][:, k:k + 1], axis=0),
                                                 in_=y[p][:, k, :], in_offset=None, bounds_check=N - 1, oob_is_err=False).then_inc(s_out[p], 16)

            @chunks(pool)
            def _(u, a):
                c, p = 2 * u + a, a % 2
                need(pool, s_tA, c - 1)
                pool.sem_inc(s_go, 1)
                gathers(pool, s_go, s_ringA, s_ga[p], ring[p], K["s_idxE"], c, c + 1, T["TE2"], ga[p])
                if not (isinstance(c, int) and c == 0):
                    scatter(u, a - 1)
            scatter(0, NC - 1)
            for s in s_out:
                pool.wait_ge(s, 64 * (NC // 2 + (s is s_out[0])))

        @block.tensor
        def _(pe):
            @chunks(pe)
            def _(u, a):
                c, p = 2 * u + a, a % 2
                pe.wait_ge(s_ga[p], 64 * (u + a // 2 + 1))
                need(pe, s_S, c - 1)
                for k in range(CT):
                    last = nc.tensor.transpose(pX[p][:, k * TP:(k + 1) * TP], ga[p][:, k, :], K["ident"][0:TP, 0:TP])
                last.then_inc(s_tA, 1)
                pe.wait_ge(s_oF, c + 1)
                need(pe, s_z, c - 1)
                for k in range(CT):
                    last = nc.tensor.transpose(pR[p][0:TP, k * D:(k + 1) * D], oF[:, k * TP:(k + 1) * TP], K["ident"][:])
                last.then_inc(s_psR, 1)

        @block.scalar
        def _(act):
            act.wait_ge(s_eps, 1)
            @chunks(act)
            def _(u, a):
                c = 2 * u + a
                act.wait_ge(s_o, c + 1)
                need(act, s_psR, c)
                nc.scalar.activation(oF[:], o[:], ACT.Identity, bias=K["cols"][:, 8:9]).then_inc(s_oF, 1)
                act.wait_ge(s_mv, c + 1)
                nc.scalar.activation(sd[:], mv[:, :, 1], ACT.Sqrt, bias=eps[0:TP, :]).then_inc(s_sd, 1)

        @block.vector
        def _(dve):
            nc.vector.memset(cS[:], 0.0).then_inc(s_init, 1)
            dve.wait_ge(s_init, 1)
            @chunks(dve)
            def _(u, a):
                c, p = 2 * u + a, a % 2
                dve.wait_ge(s_rows[p], 32 * (u + a // 2 + 1))
                dve.wait_ge(s_tA, c + 1)
                need(dve, s_o, c)
                nc.vector.tensor_tensor_scan(S[:], same[p][:], pX[p][:, 0:CE], cS[:], ALU.mult, ALU.add).then_inc(s_S, 1)
                dve.wait_ge(s_S, c + 1)
                need(dve, s_oF, c)
                nc.vector.tensor_copy(cS[:], S[:, CE - 1:CE])
                nc.vector.tensor_tensor(o[:], S[:], dinv[p][:], ALU.mult).then_inc(s_o, 1)
                dve.wait_ge(s_x[p], 16 * (u + a // 2 + 1))
                dve.wait_ge(s_psR, c + 1)
                need(dve, s_y, c)
                nc.vector.tensor_tensor(z[:], x[p][:], pR[p][0:TP, :].rearrange("p (k f) -> p k f", k=CT), ALU.add).then_inc(s_z, 1)
                dve.wait_ge(s_z, c + 1)
                row_stats(nc, z, CT, st, mv, s_d)
                dve.wait_ge(s_d, c + 1)
                dve.sem_inc(s_dgo, 1)
                row_aggr(nc, CT, st, mv).then_inc(s_mv, 1)
                dve.wait_ge(s_sd, c + 1)
                nc.vector.reciprocal(rs[:], sd[:]).then_inc(s_rs, 1)
                dve.wait_ge(s_rs, c + 1)
                need(dve, s_out[p], 64 * (u + a // 2))
                normalize(nc, y[p], z, CT, mv, rs).then_inc(s_y, 1)
                dve.wait_ge(s_y, c + 1)


def source_state(nc, ctx):
    def sb(name, shape, dt=F32):
        return ctx.enter_context(nc.sbuf_tensor(f"src_{name}", shape, dt))

    return {"h": sb("h", [D, E]), "sum": sb("sum", [D, 2])}


def layout(I):
    import numpy as np
    c = lambda v: np.ascontiguousarray(v)
    col = lambda v: c(v.reshape(NT, TP).T)
    src, dst = np.asarray(I["src"]), np.asarray(I["dst"])
    w = {k: np.asarray(v) for k, v in I.items()}
    end = np.full(1, -1, dst.dtype)
    f = np.float32
    U = 32
    A = np.zeros((D, D), f)
    B = np.zeros((D, D), f)
    A[0:U, 0:U] = w["L2_gnn_w_lin1_s"]
    for i in range(3):
        A[U + i:D:3, U * (i + 1):U * (i + 2)] = w["L2_gnn_w_lin1_v"]
        B[0:U, U * (i + 1):U * (i + 2)] = w["L2_gnn_w_lin1_s"]
    fc = w["L2_gnn_fc_w2"].reshape(64, 4, U)
    zero = np.zeros((64, U), f)
    fa = np.concatenate([fc[:, 0], fc[:, 2], fc[:, 2], fc[:, 2]], 1)
    fb = np.concatenate([zero, fc[:, 1], fc[:, 1], fc[:, 1]], 1)
    fcc = np.concatenate([zero, fc[:, 3], fc[:, 3], fc[:, 3]], 1)
    oA, oB, oC = (np.zeros((D, D), f) for _ in range(3))
    oA[0:U, 0:U] = w["L2_gnn_w_lin2_s"][0:U]
    for i in range(3):
        r = slice(U * (i + 1), U * (i + 2))
        oA[r, U + i:D:3] = w["L2_gnn_w_lin2_v"][U:2 * U]
        oB[r, U + i:D:3] = w["L2_gnn_w_lin2_v"][0:U]
        oC[r, 0:U] = w["L2_gnn_w_lin2_s"][U:2 * U]
    ptab = np.zeros((N, 2), f)
    ptab[:, 0] = E
    ptab[0:NH, 1] = w["L3_gnn_hyperedge_weight"]
    names = ("L0_gnn_bq", "L0_gnn_bk", "L0_gnn_bv", "L0_gnn_bo", "L1_gnn_msg_b", "L3_gnn_b1", "L3_gnn_gamma", "L3_gnn_beta", "L3_gnn_b2")
    rows = ("L0_gnn_bo", "L1_gnn_upd_b", "L1_gnn_ln_g", "L1_gnn_ln_b", "L3_gnn_b2")
    return dict(
        x=c(w["x"]), src_col=col(src), dst_col=col(dst), dstn_col=col(np.concatenate([dst[1:], end])),
        src_row=c(src[None]), dst_pad=c(np.concatenate([end, dst, end])[None]), type_row=c(w["edge_type_16"][None]),
        ea4T=c(w["edge_attr_4"].T), ea8T=c(w["edge_attr_8"].T), ptab0=ptab,
        tri=np.triu(np.ones((128, 128), f), 1), ident=np.eye(128, dtype=f), identb=np.eye(128, dtype=mybir.dt.np(BF16)),
        sel=np.kron(np.eye(8), np.eye(16, 1)).astype(f),
        heads=(np.kron(np.eye(8), np.ones((16, 16))) * 0.25).astype(f), expand=np.kron(np.eye(8), np.ones((1, 16))).astype(f),
        cols=c(np.stack([w[n] for n in names], 1)), rowv=c(np.stack([w[n] for n in rows])),
        Wq=c(w["L0_gnn_Wq"]), Wk=c(w["L0_gnn_Wk"]), Wv=c(w["L0_gnn_Wv"]), Wo=c(w["L0_gnn_Wo"]),
        Wmx=c(w["L1_gnn_msg_W"][:, 0:D].T), Wme=c(w["L1_gnn_msg_W"][:, D:].T), embT=c(w["L1_gnn_edge_emb_W"].T), Wu=c(w["L1_gnn_upd_W"].T),
        L1A=A, L1B=B, fc1=c(w["L2_gnn_fc_w1"]), fcA=c(fa), fcB=c(fb), fcC=c(fcc), oA=oA, oB=oB, oC=oC,
        W1=c(w["L3_gnn_W1"].T), W2=c(w["L3_gnn_W2"].T),
    )


TABLES = dict(ptab=[N, 2], S4=[E, 4], srow=[1, E + 2], T1=[2 * E, D], T2=[2 * E, D], T3=[2 * E, D],
              TE=[E + 1, D], TH=[E, D], TE2=[E + 1, D], TS=[E, D],
              dsame=[1, E], dpen=[1, E], ssame=[1, E], dinv=[1, E])


def program(nc, g, out):
    with ExitStack() as ctx:
        T = {n: nc.dram_tensor(f"table_{n}", tuple(s), F32).ap() for n, s in TABLES.items()}
        T["ptab1"] = T["ptab"].rearrange("a (b c) -> (a b) c", c=1)
        T["out"] = out
        K = constants(nc, ctx)
        index_phase(nc, g, K, T)
        with ExitStack() as inner:
            dn = Dense(nc, inner, g, T)
            dense_alone(nc, dn, 0, LAG_W)
            attention_phase(nc, g, K, T, dn, LAG_W)
            message_phase(nc, g, K, T, dn, LAG_W + NC)
            equivariant_phase(nc, g, K, T, dn, LAG_W + 2 * NC)
            dense_alone(nc, dn, LAG_W + 3 * NC, DS + LAG_W + 1)
        slots_phase(nc, g, K, T)
        hyperedge_phase(nc, g, K, T, "hA", T["T3"], K["idxS"], "W1", T["TE"])
        with ExitStack() as inner:
            H = source_state(nc, inner)
            node_phase(nc, g, K, T, H)
            batchnorm_phase(nc, g, K, T, H)
            hyperedge_phase(nc, g, K, T, "hB", T["TH"], K["send"], None, T["TE2"])
            result_phase(nc, g, K, T)


def kernel(**inputs):
    import concourse.bacc as bacc
    from concourse.bass_utils import run_bass_kernel_spmd

    nc = bacc.Bacc("TRN2", target_bir_lowering=False, num_devices=1)
    arrays = layout(inputs)
    g = {n: nc.dram_tensor(n, v.shape, mybir.dt.from_np(v.dtype), kind="ExternalInput").ap() for n, v in arrays.items()}
    out = nc.dram_tensor("result", (N, D), F32, kind="ExternalOutput").ap()
    program(nc, g, out)
    return run_bass_kernel_spmd(nc, [arrays], core_ids=[0]).results[0]["result"]
```
